# Optimizing a Trainium2 kernel written in Bass

```python
import numpy as np
import jax
import jax.numpy as jnp

def _softmax(x, axis=-1):
    return jax.nn.softmax(x, axis=axis)

def _gelu(x):
    return jax.nn.gelu(x, approximate=True)

def _silu(x):
    return jax.nn.silu(x)

def _sigmoid(x):
    return jax.nn.sigmoid(x)

def _layernorm(x, axis=-1, eps=1e-05):
    m = jnp.mean(x, axis=axis, keepdims=True)
    v = jnp.var(x, axis=axis, keepdims=True)
    return (x - m) / jnp.sqrt(v + eps)

def _scatter_add(tgt, idx, src, axis=0):
    return tgt.at[idx].add(src)

def _segment_sum(src, seg, n):
    return jax.ops.segment_sum(src, seg, n)
kernel_name = 'mk_gnn_ffn_d4_gnn_r32_c93df9'

def setup_inputs(seed: int=0):
    np.random.seed(seed)
    _w = jnp.asarray

    def _rec_inputs():
        import jax
        import jax.numpy as jnp
        _gk = jax.random.key(seed)
        x = -0.0002117 + 1 * jax.random.normal(jax.random.fold_in(_gk, 1), (3125, 256), jnp.float32)
        src = jax.random.randint(jax.random.fold_in(_gk, 2), (50000,), 0, 3125, jnp.int32)
        dst = jax.random.randint(jax.random.fold_in(_gk, 3), (50000,), 0, 3125, jnp.int32)
        _o = jnp.argsort(dst, stable=True)
        src = src[_o]
        dst = dst[_o]
        edge_weight = jax.random.uniform(jax.random.fold_in(_gk, 13), (50000,), jnp.float32, 0.0, 1)
        return (x, src, dst, edge_weight)
    x, src, dst, edge_weight = _rec_inputs()

    def _L0_gnn_setup():
        import jax, jax.numpy as jnp
        import numpy as np
        N_NODES = 3125
        N_EDGES = 100000
        D = 256
        N_LAYERS = 3

        def gcn_layer(x, src, dst, deg_inv_sqrt, W, b):
            h = x @ W
            norm = deg_inv_sqrt[src] * deg_inv_sqrt[dst]
            msg = h[src] * norm[:, None]
            out = jax.ops.segment_sum(msg, dst, num_segments=N_NODES)
            return out + b
        key = jax.random.key(seed)
        ks = jax.random.split(key, 2 + 2 * N_LAYERS)
        x = jax.random.normal(ks[0], (N_NODES, D), dtype=jnp.float32)
        edge_index = jax.random.randint(ks[1], (2, N_EDGES), 0, N_NODES, dtype=jnp.int64)
        inp = {'x': x, 'edge_index': edge_index}
        for i in range(N_LAYERS):
            limit = np.sqrt(6.0 / (D + D)).astype(np.float32)
            inp[f'W{i + 1}'] = jax.random.uniform(ks[2 + 2 * i], (D, D), dtype=jnp.float32, minval=-limit, maxval=limit)
            inp[f'b{i + 1}'] = jnp.zeros((D,), dtype=jnp.float32)
        return inp
    _L0_gnn_all = _L0_gnn_setup()
    _L0_gnn_in = {k: v for k, v in _L0_gnn_all.items() if k in ('W1', 'b1', 'W2', 'b2', 'W3', 'b3')}
    del _L0_gnn_all

    def _L0_ffn_setup():
        import jax, jax.numpy as jnp
        import numpy as np
        B, S, H, F, E, K = (8, 128, 256, 512, 16, 2)
        EPS = 1e-05
        key = jax.random.key(seed)
        ks = jax.random.split(key, 9)
        sc = 0.02
        return {'x': jax.random.normal(ks[0], (B, S, H), dtype=jnp.float32), 'gate_w': jax.random.normal(ks[1], (H, E), dtype=jnp.float32) * sc, 'gate_b': jnp.zeros((E,), dtype=jnp.float32), 'w1': jax.random.normal(ks[2], (E, H, F), dtype=jnp.float32) * sc, 'b1': jnp.zeros((E, F), dtype=jnp.float32), 'w2': jax.random.normal(ks[3], (E, F, H), dtype=jnp.float32) * sc, 'b2': jnp.zeros((E, H), dtype=jnp.float32), 'gamma': jnp.ones((H,), dtype=jnp.float32), 'beta': jnp.zeros((H,), dtype=jnp.float32)}
    _L0_ffn_all = _L0_ffn_setup()
    _L0_ffn_in = {k: v for k, v in _L0_ffn_all.items() if k in ('gate_w', 'gate_b', 'w1', 'b1', 'w2', 'b2', 'gamma', 'beta')}
    del _L0_ffn_all

    def _L1_gnn_setup():
        import math
        import jax, jax.numpy as jnp
        import numpy as np
        N = 625
        E = 10000
        D_IN = 256
        D_OUT = 256
        H = 8
        DK = D_OUT // H
        key = jax.random.key(seed)
        ks = jax.random.split(key, 16)
        h = jax.random.normal(ks[0], (N, D_IN), dtype=jnp.float32)
        src = jax.random.randint(ks[1], (E,), 0, N, dtype=jnp.int32)
        dst = jax.random.randint(ks[2], (E,), 0, N, dtype=jnp.int32)
        s = 1.0 / math.sqrt(D_IN)
        Wk = jax.random.uniform(ks[3], (D_OUT, D_IN), jnp.float32, -s, s)
        bk = jnp.zeros((D_OUT,), jnp.float32)
        Wq = jax.random.uniform(ks[4], (D_OUT, D_IN), jnp.float32, -s, s)
        bq = jnp.zeros((D_OUT,), jnp.float32)
        Wv = jax.random.uniform(ks[5], (D_OUT, D_IN), jnp.float32, -s, s)
        bv = jnp.zeros((D_OUT,), jnp.float32)
        so = 1.0 / math.sqrt(D_OUT)
        Wa = jax.random.uniform(ks[6], (D_OUT, D_OUT), jnp.float32, -so, so)
        ba = jnp.zeros((D_OUT,), jnp.float32)
        bound = math.sqrt(6.0 / (DK + DK))
        rel_att = jax.random.uniform(ks[7], (H, DK, DK), jnp.float32, -bound, bound)
        rel_msg = jax.random.uniform(ks[8], (H, DK, DK), jnp.float32, -bound, bound)
        rel_pri = jnp.ones((H,), jnp.float32)
        skip = jnp.ones((), jnp.float32)
        return {'h': h, 'src': src, 'dst': dst, 'Wk': Wk, 'bk': bk, 'Wq': Wq, 'bq': bq, 'Wv': Wv, 'bv': bv, 'Wa': Wa, 'ba': ba, 'rel_att': rel_att, 'rel_msg': rel_msg, 'rel_pri': rel_pri, 'skip': skip}
    _L1_gnn_all = _L1_gnn_setup()
    _L1_gnn_in = {k: v for k, v in _L1_gnn_all.items() if k in ('Wk', 'bk', 'Wq', 'bq', 'Wv', 'bv', 'Wa', 'ba', 'rel_att', 'rel_msg', 'rel_pri', 'skip')}
    del _L1_gnn_all

    def _L1_ffn_setup():
        import jax, jax.numpy as jnp
        import numpy as np
        C = 256
        HID = 1024
        E = 8
        TEMP = 1.0
        key = jax.random.key(seed)
        ks = jax.random.split(key, 7)
        x = jax.random.normal(ks[0], (8, 512, C), dtype=jnp.float32)
        W1 = jax.random.normal(ks[1], (C, HID), dtype=jnp.float32) * 0.02
        b1 = jnp.zeros((HID,), dtype=jnp.float32)
        Wg = jax.random.normal(ks[2], (HID, E), dtype=jnp.float32) * 0.02
        bg = jnp.zeros((E,), dtype=jnp.float32)
        Wd = jax.random.normal(ks[3], (E, HID, C), dtype=jnp.float32) * 0.02
        bd = jnp.zeros((E, C), dtype=jnp.float32)
        return {'x': x, 'W1': W1, 'b1': b1, 'Wg': Wg, 'bg': bg, 'Wd': Wd, 'bd': bd}
    _L1_ffn_all = _L1_ffn_setup()
    _L1_ffn_in = {k: v for k, v in _L1_ffn_all.items() if k in ('W1', 'b1', 'Wg', 'bg', 'Wd', 'bd')}
    del _L1_ffn_all

    def _L2_gnn_setup():
        import jax, jax.numpy as jnp
        import numpy as np
        N_NODES = 3125
        N_EDGES = 100000
        IN_F = 256
        OUT_F = 256
        key = jax.random.key(seed)
        k1, k2, k3, k4, k5, k6 = jax.random.split(key, 6)
        H = jax.random.normal(k1, (N_NODES, IN_F), dtype=jnp.float32)
        row = jax.random.randint(k2, (N_EDGES,), 0, N_NODES)
        col = jax.random.randint(k3, (N_EDGES,), 0, N_NODES)
        edge_index = jnp.stack([row, col], axis=0)
        edge_vals = jax.random.uniform(k4, (N_EDGES,), dtype=jnp.float32)
        stdv = 1.0 / np.sqrt(OUT_F)
        W = jax.random.uniform(k5, (IN_F, OUT_F), dtype=jnp.float32, minval=-stdv, maxval=stdv)
        b = jax.random.uniform(k6, (OUT_F,), dtype=jnp.float32, minval=-stdv, maxval=stdv)
        return {'H': H, 'edge_index': edge_index, 'edge_vals': edge_vals, 'W': W, 'b': b}
    _L2_gnn_all = _L2_gnn_setup()
    _L2_gnn_in = {k: v for k, v in _L2_gnn_all.items() if k in ('W', 'b')}
    del _L2_gnn_all

    def _L2_ffn_setup():
        import math
        import jax, jax.numpy as jnp
        import numpy as np
        CAPACITY_FACTOR = 1.25
        TOP_K = 2
        LN_EPS = 1e-05

        def _layer_norm(x, gamma, beta):
            mu = jnp.mean(x, axis=-1, keepdims=True)
            var = jnp.var(x, axis=-1, keepdims=True)
            return (x - mu) * jax.lax.rsqrt(var + LN_EPS) * gamma + beta
        key = jax.random.key(seed)
        ks = jax.random.split(key, 4)
        B, S, D, F, E = (8, 128, 256, 512, 8)
        x = jax.random.normal(ks[0], (B, S, D), dtype=jnp.float32)
        Wr = jax.random.normal(ks[1], (D, E), dtype=jnp.float32) / np.sqrt(D)
        br = jnp.zeros((E,), jnp.float32)
        W1 = jax.random.normal(ks[2], (E, D, F), dtype=jnp.float32) / np.sqrt(D)
        b1 = jnp.zeros((E, F), jnp.float32)
        W2 = jax.random.normal(ks[3], (E, F, D), dtype=jnp.float32) / np.sqrt(F)
        b2 = jnp.zeros((E, D), jnp.float32)
        gamma = jnp.ones((D,), jnp.float32)
        beta = jnp.zeros((D,), jnp.float32)
        return {'x': x, 'Wr': Wr, 'br': br, 'W1': W1, 'b1': b1, 'W2': W2, 'b2': b2, 'gamma': gamma, 'beta': beta}
    _L2_ffn_all = _L2_ffn_setup()
    _L2_ffn_in = {k: v for k, v in _L2_ffn_all.items() if k in ('Wr', 'br', 'W1', 'b1', 'W2', 'b2', 'gamma', 'beta')}
    del _L2_ffn_all

    def _L3_gnn_setup():
        import jax, jax.numpy as jnp
        import numpy as np
        N_NODES = 50000
        N_EDGES = 25000
        D = 256
        N_LAYERS = 3
        BN_EPS = 1e-05
        key = jax.random.key(seed)
        ks = jax.random.split(key, 7)
        x = jax.random.normal(ks[0], (N_NODES, D), dtype=jnp.float32)
        Wl = jax.random.normal(ks[1], (N_LAYERS, D, D), dtype=jnp.float32)
        bl = jax.random.normal(ks[2], (N_LAYERS, D), dtype=jnp.float32)
        Wr = jax.random.normal(ks[3], (N_LAYERS, D, D), dtype=jnp.float32)
        gamma = jax.random.uniform(ks[4], (N_LAYERS, D), dtype=jnp.float32)
        beta = jax.random.normal(ks[5], (N_LAYERS, D), dtype=jnp.float32)
        edge_index = jax.random.randint(ks[6], (2, N_EDGES), 0, N_NODES, dtype=jnp.int64)
        return {'x': x, 'Wl': Wl, 'bl': bl, 'Wr': Wr, 'gamma': gamma, 'beta': beta, 'edge_index': edge_index}
    _L3_gnn_all = _L3_gnn_setup()
    _L3_gnn_in = {k: v for k, v in _L3_gnn_all.items() if k in ('Wl', 'bl', 'Wr', 'gamma', 'beta')}
    del _L3_gnn_all

    def _L3_ffn_setup():
        import jax, jax.numpy as jnp
        import numpy as np
        BN_EPS = 0.001

        def _bn(h, g, b, m, v):
            return g * (h - m) * jax.lax.rsqrt(v + BN_EPS) + b
        key = jax.random.key(seed)
        ks = jax.random.split(key, 8)
        B, F, Df = (256, 64, 256)
        E, H, D = (8, 256, 256)
        s1 = 1.0 / np.sqrt(Df)
        s2 = 1.0 / np.sqrt(H)
        return {'x': jax.random.normal(ks[0], (B, F, Df), jnp.float32), 'Wr': jax.random.normal(ks[1], (Df, E), jnp.float32) * s1, 'br': jnp.zeros((E,), jnp.float32), 'W1': jax.random.normal(ks[2], (E, Df, H), jnp.float32) * s1, 'b1': jnp.zeros((E, H), jnp.float32), 'g1': jnp.ones((E, H), jnp.float32), 'be1': jnp.zeros((E, H), jnp.float32), 'm1': jnp.zeros((E, H), jnp.float32), 'v1': jnp.ones((E, H), jnp.float32), 'W2': jax.random.normal(ks[3], (E, H, H), jnp.float32) * s2, 'b2': jnp.zeros((E, H), jnp.float32), 'g2': jnp.ones((E, H), jnp.float32), 'be2': jnp.zeros((E, H), jnp.float32), 'm2': jnp.zeros((E, H), jnp.float32), 'v2': jnp.ones((E, H), jnp.float32), 'Wo': jax.random.normal(ks[4], (E, H, D), jnp.float32) * s2, 'bo': jnp.zeros((E, D), jnp.float32)}
    _L3_ffn_all = _L3_ffn_setup()
    _L3_ffn_in = {k: v for k, v in _L3_ffn_all.items() if k in ('Wr', 'br', 'W1', 'b1', 'g1', 'be1', 'm1', 'v1', 'W2', 'b2', 'g2', 'be2', 'm2', 'v2', 'Wo', 'bo')}
    del _L3_ffn_all
    return {'x': x, 'src': src, 'dst': dst, 'edge_weight': edge_weight, 'L0_gnn_W1': _L0_gnn_in['W1'], 'L0_gnn_b1': _L0_gnn_in['b1'], 'L0_gnn_W2': _L0_gnn_in['W2'], 'L0_gnn_b2': _L0_gnn_in['b2'], 'L0_gnn_W3': _L0_gnn_in['W3'], 'L0_gnn_b3': _L0_gnn_in['b3'], 'L0_ffn_gate_w': _L0_ffn_in['gate_w'], 'L0_ffn_gate_b': _L0_ffn_in['gate_b'], 'L0_ffn_w1': _L0_ffn_in['w1'], 'L0_ffn_b1': _L0_ffn_in['b1'], 'L0_ffn_w2': _L0_ffn_in['w2'], 'L0_ffn_b2': _L0_ffn_in['b2'], 'L0_ffn_gamma': _L0_ffn_in['gamma'], 'L0_ffn_beta': _L0_ffn_in['beta'], 'L1_gnn_Wk': _L1_gnn_in['Wk'], 'L1_gnn_bk': _L1_gnn_in['bk'], 'L1_gnn_Wq': _L1_gnn_in['Wq'], 'L1_gnn_bq': _L1_gnn_in['bq'], 'L1_gnn_Wv': _L1_gnn_in['Wv'], 'L1_gnn_bv': _L1_gnn_in['bv'], 'L1_gnn_Wa': _L1_gnn_in['Wa'], 'L1_gnn_ba': _L1_gnn_in['ba'], 'L1_gnn_rel_att': _L1_gnn_in['rel_att'], 'L1_gnn_rel_msg': _L1_gnn_in['rel_msg'], 'L1_gnn_rel_pri': _L1_gnn_in['rel_pri'], 'L1_gnn_skip': _L1_gnn_in['skip'], 'L1_ffn_W1': _L1_ffn_in['W1'], 'L1_ffn_b1': _L1_ffn_in['b1'], 'L1_ffn_Wg': _L1_ffn_in['Wg'], 'L1_ffn_bg': _L1_ffn_in['bg'], 'L1_ffn_Wd': _L1_ffn_in['Wd'], 'L1_ffn_bd': _L1_ffn_in['bd'], 'L2_gnn_W': _L2_gnn_in['W'], 'L2_gnn_b': _L2_gnn_in['b'], 'L2_ffn_Wr': _L2_ffn_in['Wr'], 'L2_ffn_br': _L2_ffn_in['br'], 'L2_ffn_W1': _L2_ffn_in['W1'], 'L2_ffn_b1': _L2_ffn_in['b1'], 'L2_ffn_W2': _L2_ffn_in['W2'], 'L2_ffn_b2': _L2_ffn_in['b2'], 'L2_ffn_gamma': _L2_ffn_in['gamma'], 'L2_ffn_beta': _L2_ffn_in['beta'], 'L3_gnn_Wl': _L3_gnn_in['Wl'], 'L3_gnn_bl': _L3_gnn_in['bl'], 'L3_gnn_Wr': _L3_gnn_in['Wr'], 'L3_gnn_gamma': _L3_gnn_in['gamma'], 'L3_gnn_beta': _L3_gnn_in['beta'], 'L3_ffn_Wr': _L3_ffn_in['Wr'], 'L3_ffn_br': _L3_ffn_in['br'], 'L3_ffn_W1': _L3_ffn_in['W1'], 'L3_ffn_b1': _L3_ffn_in['b1'], 'L3_ffn_g1': _L3_ffn_in['g1'], 'L3_ffn_be1': _L3_ffn_in['be1'], 'L3_ffn_m1': _L3_ffn_in['m1'], 'L3_ffn_v1': _L3_ffn_in['v1'], 'L3_ffn_W2': _L3_ffn_in['W2'], 'L3_ffn_b2': _L3_ffn_in['b2'], 'L3_ffn_g2': _L3_ffn_in['g2'], 'L3_ffn_be2': _L3_ffn_in['be2'], 'L3_ffn_m2': _L3_ffn_in['m2'], 'L3_ffn_v2': _L3_ffn_in['v2'], 'L3_ffn_Wo': _L3_ffn_in['Wo'], 'L3_ffn_bo': _L3_ffn_in['bo']}

def reference(x, src, dst, edge_weight, L0_gnn_W1, L0_gnn_b1, L0_gnn_W2, L0_gnn_b2, L0_gnn_W3, L0_gnn_b3, L0_ffn_gate_w, L0_ffn_gate_b, L0_ffn_w1, L0_ffn_b1, L0_ffn_w2, L0_ffn_b2, L0_ffn_gamma, L0_ffn_beta, L1_gnn_Wk, L1_gnn_bk, L1_gnn_Wq, L1_gnn_bq, L1_gnn_Wv, L1_gnn_bv, L1_gnn_Wa, L1_gnn_ba, L1_gnn_rel_att, L1_gnn_rel_msg, L1_gnn_rel_pri, L1_gnn_skip, L1_ffn_W1, L1_ffn_b1, L1_ffn_Wg, L1_ffn_bg, L1_ffn_Wd, L1_ffn_bd, L2_gnn_W, L2_gnn_b, L2_ffn_Wr, L2_ffn_br, L2_ffn_W1, L2_ffn_b1, L2_ffn_W2, L2_ffn_b2, L2_ffn_gamma, L2_ffn_beta, L3_gnn_Wl, L3_gnn_bl, L3_gnn_Wr, L3_gnn_gamma, L3_gnn_beta, L3_ffn_Wr, L3_ffn_br, L3_ffn_W1, L3_ffn_b1, L3_ffn_g1, L3_ffn_be1, L3_ffn_m1, L3_ffn_v1, L3_ffn_W2, L3_ffn_b2, L3_ffn_g2, L3_ffn_be2, L3_ffn_m2, L3_ffn_v2, L3_ffn_Wo, L3_ffn_bo):
    import jax
    import jax.numpy as jnp

    def _L0_gnn_ref(x, edge_index, W1, b1, W2, b2, W3, b3):
        import jax, jax.numpy as jnp
        import numpy as np
        N_NODES = 3125
        N_EDGES = 100000
        D = 256
        N_LAYERS = 3

        def gcn_layer(x, src, dst, deg_inv_sqrt, W, b):
            h = x @ W
            norm = deg_inv_sqrt[src] * deg_inv_sqrt[dst]
            msg = h[src] * norm[:, None]
            out = jax.ops.segment_sum(msg, dst, num_segments=N_NODES)
            return out + b
        loops = jnp.arange(N_NODES, dtype=edge_index.dtype)
        src = jnp.concatenate([edge_index[0], loops])
        dst = jnp.concatenate([edge_index[1], loops])
        deg = jax.ops.segment_sum(jnp.ones_like(dst, dtype=x.dtype), dst, num_segments=N_NODES)
        deg_inv_sqrt = jnp.where(deg > 0, jax.lax.rsqrt(jnp.maximum(deg, 1e-12)), 0.0)
        for W, b in ((W1, b1), (W2, b2), (W3, b3)):
            x = gcn_layer(x, src, dst, deg_inv_sqrt, W, b)
        return x

    def _L0_ffn_ref(x, gate_w, gate_b, w1, b1, w2, b2, gamma, beta):
        import jax, jax.numpy as jnp
        import numpy as np
        B, S, H, F, E, K = (8, 128, 256, 512, 16, 2)
        EPS = 1e-05
        gate_logits = x @ gate_w + gate_b
        topk_vals, topk_idx = jax.lax.top_k(gate_logits, K)
        topk_w = jax.nn.softmax(topk_vals, axis=-1)
        h = jax.nn.relu(jnp.einsum('bsh,ehf->bsef', x, w1) + b1)
        expert_out = jnp.einsum('bsef,efh->bseh', h, w2) + b2
        sel = jnp.take_along_axis(expert_out, topk_idx[:, :, :, None], axis=2)
        moe = jnp.sum(topk_w[..., None] * sel, axis=2)
        y = x + moe
        mu = jnp.mean(y, axis=-1, keepdims=True)
        var = jnp.var(y, axis=-1, keepdims=True)
        return (y - mu) / jnp.sqrt(var + EPS) * gamma + beta

    def _L1_gnn_ref(h, src, dst, Wk, bk, Wq, bq, Wv, bv, Wa, ba, rel_att, rel_msg, rel_pri, skip):
        import math
        import jax, jax.numpy as jnp
        import numpy as np
        N = 625
        E = 10000
        D_IN = 256
        D_OUT = 256
        H = 8
        DK = D_OUT // H
        n = h.shape[0]
        sqrt_dk = math.sqrt(DK)
        k = (h @ Wk.T + bk).reshape(n, H, DK)
        q = (h @ Wq.T + bq).reshape(n, H, DK)
        v = (h @ Wv.T + bv).reshape(n, H, DK)
        k = jnp.einsum('nhd,hde->nhe', k, rel_att)
        v = jnp.einsum('nhd,hde->nhe', v, rel_msg)
        score = jnp.einsum('ehd,ehd->eh', q[dst], k[src]) * rel_pri / sqrt_dk
        m = jax.ops.segment_max(score, dst, num_segments=n)
        ex = jnp.exp(score - m[dst])
        z = jax.ops.segment_sum(ex, dst, num_segments=n)
        attn = ex / z[dst]
        agg = jax.ops.segment_sum(v[src] * attn[:, :, None], dst, num_segments=n)
        t = agg.reshape(n, D_OUT)
        trans = t @ Wa.T + ba
        alpha = jax.nn.sigmoid(skip)
        return trans * alpha + h * (1.0 - alpha)

    def _L1_ffn_ref(x, W1, b1, Wg, bg, Wd, bd):
        import jax, jax.numpy as jnp
        import numpy as np
        C = 256
        HID = 1024
        E = 8
        TEMP = 1.0
        orig_shape = x.shape
        xf = x.reshape(-1, orig_shape[-1])
        H = jax.nn.gelu(xf @ W1 + b1, approximate=False)
        probs = jax.nn.softmax((H @ Wg + bg) / TEMP, axis=-1)
        assign = jnp.argmax(probs, axis=-1)
        out = jnp.zeros_like(xf)
        for e in range(Wd.shape[0]):
            y = H @ Wd[e] + bd[e]
            sel = (assign == e)[:, None]
            out = out + jnp.where(sel, probs[:, e:e + 1] * y, 0.0)
        return out.reshape(orig_shape)

    def _L2_gnn_ref(H, edge_index, edge_vals, W, b):
        import jax, jax.numpy as jnp
        import numpy as np
        N_NODES = 3125
        N_EDGES = 100000
        IN_F = 256
        OUT_F = 256
        HW = H @ W
        row, col = (edge_index[0], edge_index[1])
        msgs = edge_vals[:, None] * HW[col]
        AHW = jax.ops.segment_sum(msgs, row, num_segments=N_NODES)
        return AHW + b

    def _L2_ffn_ref(x, Wr, br, W1, b1, W2, b2, gamma, beta):
        import math
        import jax, jax.numpy as jnp
        import numpy as np
        CAPACITY_FACTOR = 1.25
        TOP_K = 2
        LN_EPS = 1e-05

        def _layer_norm(x, gamma, beta):
            mu = jnp.mean(x, axis=-1, keepdims=True)
            var = jnp.var(x, axis=-1, keepdims=True)
            return (x - mu) * jax.lax.rsqrt(var + LN_EPS) * gamma + beta
        B, S, D = x.shape
        E = Wr.shape[1]
        N = B * S
        K = TOP_K
        logits = jnp.mean(x, axis=1) @ Wr + br
        routing_weights = jax.nn.softmax(logits, axis=-1)
        capacity = float(math.ceil(N * CAPACITY_FACTOR / E))
        expected_loads = routing_weights.sum(axis=0) * (N / B)
        scale = jnp.where(expected_loads > capacity, capacity / expected_loads, 1.0)
        routing_weights = jax.nn.softmax(routing_weights * scale, axis=-1)
        rw_tok = jnp.broadcast_to(routing_weights[:, None, :], (B, S, E)).reshape(N, E)
        top_w, top_i = jax.lax.top_k(rw_tok, K)
        top_w = jax.nn.softmax(top_w, axis=-1)
        xf = x.reshape(N, D)
        h = jax.nn.gelu(jnp.einsum('nd,edf->enf', xf, W1) + b1[:, None, :], approximate=False)
        y = jnp.einsum('enf,efd->end', h, W2) + b2[:, None, :]
        w_dense = jnp.zeros((N, E), x.dtype).at[jnp.arange(N)[:, None], top_i].add(top_w)
        out = jnp.einsum('ne,end->nd', w_dense, y).reshape(B, S, D)
        out = _layer_norm(out + x, gamma, beta)
        return out

    def _L3_gnn_ref(x, Wl, bl, Wr, gamma, beta, edge_index):
        import jax, jax.numpy as jnp
        import numpy as np
        N_NODES = 50000
        N_EDGES = 25000
        D = 256
        N_LAYERS = 3
        BN_EPS = 1e-05
        '3-layer GNN: SAGEConv(mean) -> BatchNorm1d(train) -> ReLU per layer.'
        src = edge_index[0]
        dst = edge_index[1]
        n = x.shape[0]
        deg = jax.ops.segment_sum(jnp.ones((src.shape[0],), dtype=x.dtype), dst, num_segments=n)
        deg = jnp.maximum(deg, 1.0)[:, None]
        n_layers = Wl.shape[0]
        for i in range(n_layers):
            agg = jax.ops.segment_sum(x[src], dst, num_segments=n) / deg
            h = agg @ Wl[i] + bl[i] + x @ Wr[i]
            mu = jnp.mean(h, axis=0)
            var = jnp.mean(jnp.square(h - mu), axis=0)
            h = (h - mu) * jax.lax.rsqrt(var + BN_EPS) * gamma[i] + beta[i]
            x = jax.nn.relu(h)
        return x

    def _L3_ffn_ref(x, Wr, br, W1, b1, g1, be1, m1, v1, W2, b2, g2, be2, m2, v2, Wo, bo):
        import jax, jax.numpy as jnp
        import numpy as np
        BN_EPS = 0.001

        def _bn(h, g, b, m, v):
            return g * (h - m) * jax.lax.rsqrt(v + BN_EPS) + b
        feat = jnp.mean(x, axis=0)
        w = jax.nn.softmax(feat @ Wr + br, axis=-1)
        h = jnp.einsum('bfd,edh->bfeh', x, W1) + b1
        h = jax.nn.relu(_bn(h, g1, be1, m1, v1))
        h = jnp.einsum('bfeh,ehk->bfek', h, W2) + b2
        h = jax.nn.relu(_bn(h, g2, be2, m2, v2))
        y = jnp.einsum('bfeh,ehd->bfed', h, Wo) + bo
        return jnp.einsum('bfed,fe->bfd', y, w)
    edge_index = jnp.stack([src, dst])
    x = x + _L0_gnn_ref(_layernorm(x, axis=-1), edge_index, L0_gnn_W1, L0_gnn_b1, L0_gnn_W2, L0_gnn_b2, L0_gnn_W3, L0_gnn_b3)
    x = x + _L0_ffn_ref(_layernorm(x, axis=-1)[None], L0_ffn_gate_w, L0_ffn_gate_b, L0_ffn_w1, L0_ffn_b1, L0_ffn_w2, L0_ffn_b2, L0_ffn_gamma, L0_ffn_beta)[0]
    x = x + _L1_gnn_ref(_layernorm(x, axis=-1), src, dst, L1_gnn_Wk, L1_gnn_bk, L1_gnn_Wq, L1_gnn_bq, L1_gnn_Wv, L1_gnn_bv, L1_gnn_Wa, L1_gnn_ba, L1_gnn_rel_att, L1_gnn_rel_msg, L1_gnn_rel_pri, L1_gnn_skip)
    x = x + _L1_ffn_ref(_layernorm(x, axis=-1)[None], L1_ffn_W1, L1_ffn_b1, L1_ffn_Wg, L1_ffn_bg, L1_ffn_Wd, L1_ffn_bd)[0]
    x = x + _L2_gnn_ref(_layernorm(x, axis=-1), edge_index, edge_weight, L2_gnn_W, L2_gnn_b)
    x = x + _L2_ffn_ref(_layernorm(x, axis=-1)[None], L2_ffn_Wr, L2_ffn_br, L2_ffn_W1, L2_ffn_b1, L2_ffn_W2, L2_ffn_b2, L2_ffn_gamma, L2_ffn_beta)[0]
    x = x + _L3_gnn_ref(_layernorm(x, axis=-1), L3_gnn_Wl, L3_gnn_bl, L3_gnn_Wr, L3_gnn_gamma, L3_gnn_beta, edge_index)
    x = x + _L3_ffn_ref(_layernorm(x, axis=-1)[None], L3_ffn_Wr, L3_ffn_br, L3_ffn_W1, L3_ffn_b1, L3_ffn_g1, L3_ffn_be1, L3_ffn_m1, L3_ffn_v1, L3_ffn_W2, L3_ffn_b2, L3_ffn_g2, L3_ffn_be2, L3_ffn_m2, L3_ffn_v2, L3_ffn_Wo, L3_ffn_bo)[0]
    return x

_drawn_inputs = setup_inputs


def setup_inputs(seed=0):
    import zlib

    import numpy as np

    out = dict(_drawn_inputs(seed))
    spreads = {'L0_gnn_b1': (0.0, 0.1),
     'L0_gnn_b2': (0.0, 0.1),
     'L0_gnn_b3': (0.0, 0.1),
     'L0_ffn_gate_b': (0.0, 0.1),
     'L0_ffn_b1': (0.0, 0.662),
     'L0_ffn_b2': (0.0, 0.1),
     'L0_ffn_gamma': (1.0, 0.2),
     'L0_ffn_beta': (0.0, 0.1),
     'L1_gnn_bk': (0.0, 2.0),
     'L1_gnn_bq': (0.0, 0.8),
     'L1_gnn_bv': (0.0, 0.1),
     'L1_gnn_ba': (0.0, 0.1),
     'L1_gnn_rel_pri': (1.0, 0.6),
     'L1_ffn_b1': (0.0, 0.8),
     'L1_ffn_bg': (0.0, 0.764),
     'L1_ffn_bd': (0.0, 0.8),
     'L2_ffn_br': (0.0, 2.0),
     'L2_ffn_b1': (0.0, 0.702),
     'L2_ffn_b2': (0.0, 0.444),
     'L2_ffn_gamma': (1.0, 0.598),
     'L2_ffn_beta': (0.0, 0.308),
     'L3_ffn_br': (0.0, 0.8),
     'L3_ffn_b1': (0.0, 0.8),
     'L3_ffn_g1': (1.0, 0.6),
     'L3_ffn_be1': (0.0, 0.8),
     'L3_ffn_m1': (0.0, 0.8),
     'L3_ffn_v1': (1.0, 0.6),
     'L3_ffn_b2': (0.0, 0.8),
     'L3_ffn_g2': (1.0, 0.6),
     'L3_ffn_be2': (0.0, 0.8),
     'L3_ffn_m2': (0.0, 0.8),
     'L3_ffn_v2': (1.0, 0.6),
     'L3_ffn_bo': (0.0, 0.631)}
    factors = {'L1_gnn_Wk': 6.132,
     'L1_gnn_Wq': 6.191,
     'L1_gnn_rel_att': 6.162,
     'L1_ffn_W1': 6.341,
     'L1_ffn_Wg': 6.295,
     'L1_ffn_Wd': 7.37,
     'L2_gnn_b': 4.375,
     'L3_gnn_bl': 64.0}
    for name, (base, spread) in spreads.items():
        noise = np.random.default_rng([zlib.crc32(name.encode()), seed]).standard_normal(out[name].shape)
        drawn = base * np.exp(spread * noise) if base else spread * noise
        out[name] = jnp.asarray(drawn.astype(out[name].dtype))
    for name, factor in factors.items():
        out[name] = (out[name] * factor).astype(out[name].dtype)
    return out
```

```python
import concourse.bass as bass
from concourse import mybir
from contextlib import ExitStack

FP32 = mybir.dt.float32
BF16 = mybir.dt.bfloat16
I32 = mybir.dt.int32
U32 = mybir.dt.uint32
ALU = mybir.AluOpType
ACT = mybir.ActivationFunctionType
AX = mybir.AxisListType.X

N, D, E = 3125, 256, 50000
P = 128
G = -(-N // P)
NP = G * P
LAST = N - (G - 1) * P
KD = D // P
EP = 125
EC = E // EP
HALF = 8
TILES = -(-(E // P + G) // (2 * HALF)) * 2 * HALF
HEADS, DK = 8, 32
AW = D + HEADS
CREDIT = 64
CH = 5
TOK = CH * P
HT = TOK // 2
BIG = 2.0 ** 100


class Signal:

    def __init__(self, ctx, nc, name, credit=CREDIT):
        self.sem = ctx.enter_context(nc.semaphore(name))
        self.base = credit

    def at(self, n):
        return n + self.base

    def passed(self, n):
        self.base += n


class Chain:

    def __init__(self, eng, signal, start=0):
        self.eng, self.steps, self.n = eng, signal, start

    def link(self, ins):
        self.n = self.n + 1
        ins.then_inc(self.steps.sem, 1)
        self.eng.wait_ge(self.steps.sem, self.steps.at(self.n))


def per_tile(eng, lead, follow):
    lead(0, 0)
    with eng.Fori(0, (G - 1) // 2) as i:
        for s in range(2):
            g = i * 2 + s
            lead(g + 1, 1 - s)
            follow(g, s)
    follow(G - 1, 0)


class Core:

    def __init__(self, ctx, nc, dram):
        self.ctx, self.nc, self.dram = ctx, nc, dram
        sb = self.sb
        self.stage = 0
        self.X = sb("X", [P, G * D], FP32)
        self.T = sb("T", [P, G * D], FP32)
        self.ACC = sb("ACC", [P, G * AW], FP32)
        self.B2 = sb("B2", [P, KD * NP], FP32)
        self.iota = sb("iota", [P, 512], FP32)
        self.iota_i = sb("iota_i", [P, 512], I32)
        self.ident = sb("ident", [P, P], FP32)
        self.earlier = sb("earlier", [P, P], FP32)
        self.ones = sb("ones", [P, P], FP32)
        self.ones_last = sb("ones_last", [P, P], FP32)
        self.zeros = sb("zeros", [P, 512], FP32)
        self.rec = {k: sb(f"rec_{k}", [P, TILES * 4], FP32) for k in ("dst", "src")}
        self.group = {k: sb(f"group_{k}", [1, TILES], I32) for k in ("dst", "src")}
        self.indeg = sb("indeg", [P, G], FP32)
        self.dinv = sb("dinv", [P, G], FP32)
        self.rdeg = sb("rdeg", [P, G], FP32)
        self.stat_pair = sb("stat_pair", [P, 2 * G], FP32)
        self.mean = sb("mean", [P, G], FP32)
        self.rstd = sb("rstd", [P, G], FP32)
        self.bank = [ctx.enter_context(nc.psum_tensor(f"bank{i}", [P, 512], FP32)) for i in range(8)]
        names = """act_go vec_go loaded stored const_ready vec act pool ring_staged pool_go gather_free onehot_ready summed
            rows_ready turned turned_out product product_out stats_ready table_written hidden hidden_out outcome
            outcome_used weights_used slot_ready hot_ready hot_used mask_ready turned2 turned2_out score_ready
            exps_ready gates_ready wa wb wc wd""".split()
        self.s = {n: Signal(ctx, nc, n) for n in names}
        self.arrived = [Signal(ctx, nc, f"arrived{j}", 0) for j in range(2 * HALF)]
        self.written = [Signal(ctx, nc, f"written{b}") for b in range(2)]
        self.all_counts = [*self.s.values(), *self.written]

    def sb(self, name, shape, dt):
        return self.ctx.enter_context(self.nc.sbuf_tensor(name, shape, dt))

    def scratch(self, ctx):
        self.stage += 1
        stage = self.stage
        return lambda name, shape, dt: ctx.enter_context(self.nc.sbuf_tensor(f"{name}_{stage}", shape, dt))

    def rows(self, buf, g, width=D, step=None):
        return buf[:, bass.ds(g * (step or width), width)]


def setup(c, x):
    nc, s = c.nc, c.s
    with nc.Block() as block:
        @block.sync
        def _(sp):
            for sig in c.all_counts:
                sp.sem_inc(sig.sem, CREDIT)
            sp.wait_ge(s["const_ready"].sem, s["const_ready"].at(7))
            full = x[0:(G - 1) * P, :].rearrange("(g p) d -> p g d", p=P)
            sp.dma_start(c.X[:, 0:(G - 1) * D].rearrange("p (g d) -> p g d", d=D), full).then_inc(s["loaded"].sem, 16)
            sp.dma_start(c.X[0:LAST, (G - 1) * D:G * D], x[(G - 1) * P:N, :]).then_inc(s["loaded"].sem, 16)
            sp.wait_ge(s["loaded"].sem, s["loaded"].at(32))

        @block.gpsimd
        def _(pool):
            pool.wait_ge(s["const_ready"].sem, CREDIT)
            ready = s["const_ready"].sem
            nc.gpsimd.memset(c.ident[:, :], 0.0).then_inc(ready, 1)
            nc.gpsimd.memset(c.earlier[:, :], 1.0).then_inc(ready, 1)
            nc.gpsimd.memset(c.ones[:, :], 1.0).then_inc(ready, 1)
            nc.gpsimd.memset(c.ones_last[:, :], 1.0).then_inc(ready, 1)
            nc.gpsimd.memset(c.zeros[:, :], 0.0).then_inc(ready, 1)
            nc.gpsimd.iota(c.iota_i[:, :], [[1, 512]], base=0, channel_multiplier=0).then_inc(ready, 1)
            nc.gpsimd.memset(c.X[:, (G - 1) * D:G * D], 0.0).then_inc(ready, 1)
            pool.wait_ge(ready, s["const_ready"].at(7))
            nc.gpsimd.affine_select(out=c.ident[:, :], in_=c.ident[:, :], compare_op=ALU.not_equal, fill=1.0,
                                    base=0, pattern=[[-1, P]], channel_multiplier=1).then_inc(ready, 1)
            nc.gpsimd.affine_select(out=c.earlier[:, :], in_=c.earlier[:, :], compare_op=ALU.is_ge, fill=0.0,
                                    base=-1, pattern=[[1, P]], channel_multiplier=-1).then_inc(ready, 1)
            nc.gpsimd.affine_select(out=c.ones_last[:, :], in_=c.ones_last[:, :], compare_op=ALU.is_ge, fill=0.0,
                                    base=LAST - 1, pattern=[[0, P]], channel_multiplier=-1).then_inc(ready, 1)

        @block.vector
        def _(v):
            v.wait_ge(s["const_ready"].sem, s["const_ready"].at(10))
            nc.vector.tensor_copy(c.iota[:, :], c.iota_i[:, :]).then_inc(s["vec"].sem, 1)
    s["const_ready"].passed(10)
    s["loaded"].passed(32)
    s["vec"].passed(1)


def bucket(c, key, keys, others, weight, degrees):
    nc, s = c.nc, c.s
    rec_dram = c.dram(f"rec_dram_{key}", [P * TILES, 4], FP32)
    with ExitStack() as ctx:
        sb = c.scratch(ctx)
        key_i, other_i = sb("key_i", [EP, EC], I32), sb("other_i", [EP, EC], I32)
        wt = sb("wt", [EP, EC], FP32)
        int_a = sb("int_a", [EP, EC], I32)
        hi, lo = sb("hi", [EP, EC], FP32), sb("lo", [EP, EC], FP32)
        in_bucket = sb("in_bucket", [EP, G * EC], BF16)
        prefix = sb("prefix", [EP, G * EC], FP32)
        rank, first, tmp = sb("rank", [EP, EC], FP32), sb("first", [EP, EC], FP32), sb("tmp", [EP, EC], FP32)
        row_total = sb("row_total", [EP, G], FP32)
        row_offset = sb("row_offset", [EP, G], FP32)
        tiles, tiles_i = sb("tiles", [P, G], FP32), sb("tiles_i", [P, G], I32)
        end, start = sb("end", [P, G], FP32), sb("start", [P, G], FP32)
        slot = sb("slot", [EP, EC], I32)
        out_rec = c.B2[0:EP, 0:EC * 4]
        empty = c.T[:, 0:TILES * 4]
        group_f = sb("group_f", [1, TILES], FP32)
        slot_ring = sb("slot_ring", [EP, 2 * HALF], I32)
        rec_ring = sb("rec_ring", [EP, 2 * HALF * 4], FP32)
        hot_lo = sb("hot_lo", [EP, 4 * P], BF16)
        zb = sb("zb", [EP, P], BF16)
        out4 = out_rec[:, :].rearrange("p (t c) -> p t c", c=4)
        offs, totals, deg = c.bank[0][0:EP, 0:G], c.bank[1][:, 0:G], c.bank[2][:, 0:G]
        rounds = EC // (2 * HALF)

        with nc.Block() as block:
            @block.sync
            def _(sp):
                for dst, src in ((key_i, keys), (other_i, others), (wt, weight)):
                    sp.dma_start(dst[:, :], src.rearrange("(p t) -> p t", p=EP)).then_inc(s["loaded"].sem, 16)
                sp.wait_ge(s["pool"].sem, s["pool"].at(2))
                sp.dma_start(rec_dram.rearrange("(p t) c -> p (t c)", p=P), empty[:, :]).then_inc(s["stored"].sem, 16)
                sp.wait_ge(s["pool"].sem, s["pool"].at(3))
                sp.dma_start(c.rec[key][:, :], rec_dram.rearrange("(p t) c -> p (t c)", p=P)).then_inc(s["loaded"].sem, 16)
                sp.wait_ge(s["loaded"].sem, s["loaded"].at(64))

            @block.gpsimd
            def _(pool):
                nc.gpsimd.memset(empty[:, :], 0.0).then_inc(s["pool"].sem, 1)
                pool.wait_ge(s["pool"].sem, s["pool"].at(1))
                nc.gpsimd.memset(empty[:, :].rearrange("p (t c) -> p t c", c=4)[:, :, 1], -1.0).then_inc(s["pool"].sem, 1)
                pool.wait_ge(s["stored"].sem, s["stored"].at(16))
                pool.wait_ge(s["slot_ready"].sem, s["slot_ready"].at(1))

                def scatter(i, h, first=False):
                    if not first:
                        for j in range(HALF):
                            sig = c.arrived[h * HALF + j]
                            pool.wait_ge(sig.sem, sig.at(i * 16))
                        pool.sem_inc(s["pool_go"].sem, 1)
                    t = i * (2 * HALF) + h * HALF
                    nc.gpsimd.tensor_copy(slot_ring[:, h * HALF:(h + 1) * HALF], slot[:, bass.ds(t, HALF)])\
                        .then_inc(s["ring_staged"].sem, 1)
                    nc.gpsimd.tensor_copy(rec_ring[:, h * HALF * 4:(h + 1) * HALF * 4], out_rec[:, bass.ds(t * 4, HALF * 4)])\
                        .then_inc(s["ring_staged"].sem, 1)
                    pool.wait_ge(s["ring_staged"].sem, s["ring_staged"].at(i * 4 + (h + 1) * 2))
                    pool.sem_inc(s["pool_go"].sem, 1)
                    for j in range(h * HALF, (h + 1) * HALF):
                        nc.gpsimd.indirect_dma_start(
                            rec_dram[:, :], bass.IndirectOffsetOnAxis(ap=slot_ring[:, j:j + 1], axis=0),
                            rec_ring[:, j * 4:(j + 1) * 4], None).then_inc(c.arrived[j].sem, 16)

                for h in range(2):
                    scatter(0, h, True)
                with pool.Fori(1, rounds) as i:
                    for h in range(2):
                        scatter(i, h)
                for j in range(2 * HALF):
                    pool.wait_ge(c.arrived[j].sem, c.arrived[j].at(rounds * 16))
                pool.sem_inc(s["pool"].sem, 1)

            @block.tensor
            def _(pe):
                pe.wait_ge(s["rows_ready"].sem, s["rows_ready"].at(1))
                nc.tensor.matmul(offs, c.earlier[0:EP, 0:EP], row_total[:, :], start=True, stop=True)
                nc.tensor.matmul(totals, c.ones[0:EP, :], row_total[:, :], start=True, stop=True).then_inc(s["product"].sem, 1)
                if degrees:
                    oh = in_bucket[:, :].rearrange("p (g t) -> p g t", t=EC)
                    nc.tensor.matmul(deg, zb[:, :], zb[:, 0:G], start=True, stop=False)
                    with pe.Fori(0, EC // 4) as i:
                        for j in range(4):
                            pe.wait_ge(s["onehot_ready"].sem, s["onehot_ready"].at(i * 4 + j + 1))
                            nc.tensor.matmul(deg, hot_lo[:, j * P:(j + 1) * P], oh[:, :, bass.ds(i * 4 + j, 1)],
                                             start=False, stop=False).then_inc(s["summed"].sem, 1)
                    nc.tensor.matmul(deg, zb[:, :], zb[:, 0:G], start=False, stop=True).then_inc(s["product"].sem, 1)

            @block.vector
            def _(v):
                ch = Chain(v, s["vec"])
                v.wait_ge(s["loaded"].sem, s["loaded"].at(48))
                ch.link(nc.vector.tensor_scalar(int_a[:, :], key_i[:, :], 7, None, ALU.logical_shift_right))
                ch.link(nc.vector.tensor_copy(hi[:, :], int_a[:, :]))
                ch.link(nc.vector.tensor_scalar(int_a[:, :], key_i[:, :], P - 1, None, ALU.bitwise_and))
                ch.link(nc.vector.tensor_copy(lo[:, :], int_a[:, :]))
                ch.link(nc.vector.memset(zb[:, :], 0.0))
                ch.link(nc.vector.memset(out_rec[:, :], 0.0))
                ch.link(nc.vector.tensor_copy(out4[:, :, 0].bitcast(I32), other_i[:, :]))
                ch.link(nc.vector.tensor_copy(out4[:, :, 1], lo[:, :]))
                ch.link(nc.vector.tensor_copy(out4[:, :, 2], wt[:, :]))
                ch.link(nc.vector.memset(rank[:, :], 0.0))
                ch.link(nc.vector.memset(first[:, :], 0.0))
                n0 = ch.n
                with v.Fori(0, G) as b:
                    one = Chain(v, s["vec"], b * 2 + n0)
                    ob, pb = c.rows(in_bucket, b, EC), c.rows(prefix, b, EC)
                    one.link(nc.vector.tensor_scalar(ob, hi[:, :], c.iota[0:EP, bass.ds(b, 1)], None, ALU.is_equal))
                    one.link(nc.vector.tensor_tensor_scan(pb, ob, c.zeros[0:EP, 0:EC], 0.0, ALU.add, ALU.add))
                ch.n = n0 + 2 * G
                pr = prefix[:, :].rearrange("p (g t) -> p g t", t=EC)
                ch.link(nc.vector.tensor_copy(row_total[:, :], pr[:, :, EC - 1]))
                v.sem_inc(s["rows_ready"].sem, 1)
                v.wait_ge(s["product"].sem, s["product"].at(1))
                ch.link(nc.vector.tensor_scalar(row_offset[:, :], offs, -1.0, None, ALU.add))
                ch.link(nc.vector.tensor_scalar(tiles_i[:, :], totals, float(P - 1), None, ALU.add))
                ch.link(nc.vector.tensor_scalar(tiles_i[:, :], tiles_i[:, :], 7, None, ALU.logical_shift_right))
                ch.link(nc.vector.tensor_copy(tiles[:, :], tiles_i[:, :]))
                ch.link(nc.vector.tensor_tensor_scan(end[:, :], tiles[:, :], c.zeros[:, 0:G], 0.0, ALU.add, ALU.add))
                ch.link(nc.vector.tensor_tensor(start[:, :], end[:, :], tiles[:, :], ALU.subtract))
                n1 = ch.n
                with v.Fori(0, G) as b:
                    one = Chain(v, s["vec"], b * 3 + n1)
                    ob, pb, col = c.rows(in_bucket, b, EC), c.rows(prefix, b, EC), bass.ds(b, 1)
                    one.link(nc.vector.scalar_tensor_tensor(tmp[:, :], pb, row_offset[:, col], ob, ALU.add, ALU.mult))
                    one.link(nc.vector.tensor_tensor(rank[:, :], rank[:, :], tmp[:, :], ALU.add))
                    one.link(nc.vector.scalar_tensor_tensor(first[:, :], ob, start[0:EP, col], first[:, :], ALU.mult, ALU.add))
                ch.n = n1 + 3 * G
                ch.link(nc.vector.tensor_copy(int_a[:, :], rank[:, :]))
                ch.link(nc.vector.tensor_scalar(slot[:, :], int_a[:, :], P - 1, None, ALU.bitwise_and))
                ch.link(nc.vector.tensor_scalar(int_a[:, :], int_a[:, :], 7, None, ALU.logical_shift_right))
                ch.link(nc.vector.tensor_copy(tmp[:, :], int_a[:, :]))
                ch.link(nc.vector.tensor_tensor(first[:, :], first[:, :], tmp[:, :], ALU.add))
                ch.link(nc.vector.tensor_copy(tmp[:, :], slot[:, :]))
                ch.link(nc.vector.scalar_tensor_tensor(first[:, :], tmp[:, :], float(TILES), first[:, :], ALU.mult, ALU.add))
                ch.link(nc.vector.tensor_copy(slot[:, :], first[:, :]))
                v.sem_inc(s["slot_ready"].sem, 1)
                ch.link(nc.vector.memset(group_f[:, :], 0.0))
                n2 = ch.n
                with v.Fori(0, G) as b:
                    one = Chain(v, s["vec"], b + n2)
                    one.link(nc.vector.scalar_tensor_tensor(group_f[:, :], c.iota[0:1, 0:TILES], end[0:1, bass.ds(b, 1)],
                                                            group_f[:, :], ALU.is_ge, ALU.add))
                ch.n = n2 + G
                ch.link(nc.vector.tensor_scalar(c.group[key][:, :], group_f[:, :], float(G - 1), None, ALU.min))
                if degrees:
                    with v.Fori(0, EC // 4) as i:
                        for j in range(4):
                            v.wait_ge(s["summed"].sem, s["summed"].at(i * 4 + j - 3))
                            nc.vector.tensor_scalar(hot_lo[:, j * P:(j + 1) * P], c.iota[0:EP, 0:P],
                                                    lo[:, bass.ds(i * 4 + j, 1)], None, ALU.is_equal)\
                                .then_inc(s["onehot_ready"].sem, 1)
                    v.wait_ge(s["product"].sem, s["product"].at(2))
                    ch.link(nc.vector.tensor_copy(c.indeg[:, :], deg))
                    ch.link(nc.vector.tensor_scalar(c.rdeg[:, :], c.indeg[:, :], 1.0, None, ALU.max))
                    ch.link(nc.vector.reciprocal(c.rdeg[:, :], c.rdeg[:, :]))
                    ch.link(nc.vector.tensor_scalar(c.dinv[:, :], c.indeg[:, :], 1.0, None, ALU.add))
                    v.sem_inc(s["stats_ready"].sem, 1)
                    v.wait_ge(s["act"].sem, s["act"].at(1))
                    ch.link(nc.vector.reciprocal(c.dinv[:, :], c.dinv[:, :]))
                c.vec_steps = ch.n

            @block.scalar
            def _(act):
                if degrees:
                    act.wait_ge(s["stats_ready"].sem, s["stats_ready"].at(1))
                    nc.scalar.activation(c.dinv[:, :], c.dinv[:, :], ACT.Sqrt).then_inc(s["act"].sem, 1)
    s["loaded"].passed(64)
    s["stored"].passed(16)
    s["pool"].passed(3)
    s["pool_go"].passed(4 * rounds - 2)
    s["ring_staged"].passed(4 * rounds)
    for sig in c.arrived:
        sig.passed(16 * rounds)
    s["rows_ready"].passed(1)
    s["slot_ready"].passed(1)
    s["vec"].passed(c.vec_steps)
    s["product"].passed(1)
    if degrees:
        s["product"].passed(1)
        s["onehot_ready"].passed(EC)
        s["summed"].passed(EC)
        s["stats_ready"].passed(1)
        s["act"].passed(1)


def row_stats(c, v, stats, agg, source, start, prepare=None):
    nc, s = c.nc, c.s
    steps = 4 if prepare else 3
    pair = c.stat_pair[:, :]
    with v.Fori(0, G // CH) as i:
        base = i * steps + start

        def together(n, last):
            last.then_inc(s["vec"].sem, 1)
            v.wait_ge(s["vec"].sem, s["vec"].at(base + n))
            v.sem_inc(s["vec_go"].sem, 1)
        if prepare:
            for t in range(CH):
                last = prepare(i * CH + t)
            together(1, last)
        for t in range(CH):
            last = nc.vector.bn_stats(stats[:, t * 6:(t + 1) * 6], source(i * CH + t))
        together(steps - 2, last)
        for t in range(CH):
            last = nc.vector.bn_aggr(agg[:, t * 2:(t + 1) * 2], stats[:, t * 6:(t + 1) * 6])
        together(steps - 1, last)
        together(steps, nc.vector.tensor_copy(pair[:, bass.ds(i * (2 * CH), 2 * CH)], agg[:, :]))
    return steps * (G // CH)


def layernorm(c, turn=False, eps=1e-5):
    nc, s = c.nc, c.s
    with ExitStack() as ctx:
        sb = c.scratch(ctx)
        stats, agg = sb("ln_stats", [P, 6 * CH], FP32), sb("ln_agg", [P, 2 * CH], FP32)
        ring = sb("ln_ring", [P, 2 * D], FP32)
        before = 3 * (G // CH) + 3
        with nc.Block() as block:
            @block.vector
            def _(v):
                ch = Chain(v, s["vec"], row_stats(c, v, stats, agg, lambda g: c.rows(c.X, g), 0))
                pair = c.stat_pair[:, :].rearrange("p (g n) -> p g n", n=2)
                ch.link(nc.vector.tensor_copy(c.mean[:, :], pair[:, :, 0]))
                ch.link(nc.vector.tensor_scalar(c.rstd[:, :], pair[:, :, 1], eps, None, ALU.add))
                v.sem_inc(s["stats_ready"].sem, 1)
                v.wait_ge(s["act"].sem, s["act"].at(1))
                ch.link(nc.vector.reciprocal(c.rstd[:, :], c.rstd[:, :]))
                if not turn:
                    with v.Fori(0, G) as g:
                        nc.vector.tensor_scalar(c.rows(c.T, g), c.rows(c.X, g), c.mean[:, bass.ds(g, 1)],
                                                c.rstd[:, bass.ds(g, 1)], ALU.subtract, ALU.mult).then_inc(s["vec"].sem, 1)
                else:
                    def normed(g, b):
                        v.wait_ge(s["turned"].sem, s["turned"].at(g - 1))
                        v.wait_ge(s["rows_ready"].sem, s["rows_ready"].at(g - 1))
                        nc.vector.tensor_scalar(ring[:, b * D:(b + 1) * D], c.rows(c.X, g), c.mean[:, bass.ds(g, 1)],
                                                c.rstd[:, bass.ds(g, 1)], ALU.subtract, ALU.mult).then_inc(s["vec"].sem, 1)

                    def out(g, b):
                        v.wait_ge(s["turned"].sem, s["turned"].at(g + 1))
                        dst = c.B2[:, :].rearrange("p (k n) -> p k n", k=KD)[:, :, bass.ds(g * P, P)]
                        nc.vector.tensor_copy(dst, c.bank[b][:, 0:D].rearrange("p (k n) -> p k n", k=KD))\
                            .then_inc(s["turned_out"].sem, 1)
                    per_tile(v, normed, out)

            @block.scalar
            def _(act):
                act.wait_ge(s["stats_ready"].sem, s["stats_ready"].at(1))
                nc.scalar.activation(c.rstd[:, :], c.rstd[:, :], ACT.Sqrt).then_inc(s["act"].sem, 1)
                if turn:
                    def copy(g, b):
                        act.wait_ge(s["vec"].sem, s["vec"].at(before + 1 + g))
                        nc.scalar.activation(c.rows(c.T, g), ring[:, b * D:(b + 1) * D], ACT.Copy)\
                            .then_inc(s["rows_ready"].sem, 1)
                    per_tile(act, copy, lambda g, b: None)

            @block.tensor
            def _(pe):
                if turn:
                    def turned(g, b):
                        pe.wait_ge(s["vec"].sem, s["vec"].at(before + 1 + g))
                        pe.wait_ge(s["turned_out"].sem, s["turned_out"].at(g - 1))
                        for k in range(KD):
                            last = nc.tensor.transpose(c.bank[b][:, k * P:(k + 1) * P],
                                                       ring[:, b * D + k * P:b * D + (k + 1) * P], c.ident[:, :])
                        last.then_inc(s["turned"].sem, 1)
                    per_tile(pe, turned, lambda g, b: None)
    s["vec"].passed(before + G)
    s["stats_ready"].passed(1)
    s["act"].passed(1)
    if turn:
        s["turned"].passed(G)
        s["turned_out"].passed(G)
        s["rows_ready"].passed(G)


def project(c, ins, outs, post_steps=0, loads=()):
    nc, s = c.nc, c.s
    nin, nout = len(ins), len(outs)
    vec_outs = [o for o in outs if o[2][0] == "vec"]
    act_outs = [(n, o) for n, o in enumerate(outs) if o[2][0] != "vec"]
    stores = [n for n, o in act_outs if o[2][0] in ("dram", "both")]
    with ExitStack() as ctx:
        sb = c.scratch(ctx)
        ring = sb("pj_ring", [P, 2 * nin * D], FP32)
        turned = sb("pj_turned", [P, 2 * nin * D], FP32)
        staged = sb("pj_staged", [P, 2 * nout * D], FP32)

        def slot(buf, b, n, count):
            return buf[:, (b * count + n) * D:(b * count + n + 1) * D]

        def target(n, g, b):
            post = outs[n][2]
            return post[1](g) if post[0] in ("sbuf", "both") else slot(staged, b, n, nout)

        def product(n, b):
            return c.bank[4 + 2 * b + n // 2][:, (n % 2) * D:(n % 2 + 1) * D]

        with nc.Block() as block:
            @block.sync
            def _(sp):
                for dst, src in loads:
                    sp.dma_start(dst, src).then_inc(s["loaded"].sem, 16)
                if loads:
                    sp.wait_ge(s["loaded"].sem, s["loaded"].at(16 * len(loads)))
                    sp.sem_inc(s["const_ready"].sem, 1)
                if stores:
                    def store(g, b):
                        sp.wait_ge(s["product_out"].sem, s["product_out"].at(g + 1))
                        for n in stores:
                            table = outs[n][2][-1]
                            sp.dma_start(table[bass.ds(g * P, P), :], target(n, g, b)).then_inc(c.written[b].sem, 16)
                    per_tile(sp, store, lambda g, b: None)
                    for b in range(2):
                        sp.wait_ge(c.written[b].sem, c.written[b].at(16 * len(stores) * ((G + 1 - b) // 2)))

            @block.vector
            def _(v):
                if loads:
                    v.wait_ge(s["const_ready"].sem, s["const_ready"].at(1))
                def lead(g, b):
                    v.wait_ge(s["turned"].sem, s["turned"].at(g - 1))
                    for n, make in enumerate(ins):
                        make(g, slot(ring, b, n, nin)).then_inc(s["rows_ready"].sem, 1)

                def follow(g, b):
                    if vec_outs:
                        v.wait_ge(s["product"].sem, s["product"].at(g + 1))
                        ch = Chain(v, s["vec"], g * post_steps)
                        for n, o in enumerate(outs):
                            if o[2][0] == "vec":
                                o[2][1](ch, g, product(n, b))
                        v.sem_inc(s["outcome_used"].sem, 1)
                per_tile(v, lead, follow)

            @block.tensor
            def _(pe):
                if loads:
                    pe.wait_ge(s["const_ready"].sem, s["const_ready"].at(1))

                def turn(g, b):
                    pe.wait_ge(s["rows_ready"].sem, s["rows_ready"].at(nin * (g + 1)))
                    pe.wait_ge(s["turned_out"].sem, s["turned_out"].at(g - 1))
                    for n in range(nin):
                        for k in range(KD):
                            last = nc.tensor.transpose(c.bank[2 * b + n][:, k * P:(k + 1) * P],
                                                       slot(ring, b, n, nin)[:, k * P:(k + 1) * P], c.ident[:, :])
                    last.then_inc(s["turned"].sem, 1)

                def multiply(g, b):
                    pe.wait_ge(s["turned_out"].sem, s["turned_out"].at(g + 1))
                    if act_outs:
                        pe.wait_ge(s["product_out"].sem, s["product_out"].at(g - 1))
                    if vec_outs:
                        pe.wait_ge(s["outcome_used"].sem, s["outcome_used"].at(g - 1))
                    for m, (weights, bias, _) in enumerate(outs):
                        todo = [(slot(turned, b, n, nin)[:, k * P:(k + 1) * P], w[:, k * D:(k + 1) * D])
                                for n, w in enumerate(weights) if w is not None for k in range(KD)]
                        if bias is not None:
                            todo.append((c.ones[0:1, :], bias))
                        for q, (a, w) in enumerate(todo):
                            last = nc.tensor.matmul(product(m, b), a, w, start=(q == 0), stop=(q == len(todo) - 1))
                    last.then_inc(s["product"].sem, 1)
                per_tile(pe, turn, multiply)

            @block.scalar
            def _(act):
                def evacuate(g, b):
                    act.wait_ge(s["turned"].sem, s["turned"].at(g + 1))
                    act.wait_ge(s["product"].sem, s["product"].at(g - 1))
                    for n in range(nin):
                        last = nc.scalar.activation(slot(turned, b, n, nin), c.bank[2 * b + n][:, 0:D], ACT.Copy)
                    last.then_inc(s["turned_out"].sem, 1)

                def finish(g, b):
                    if not act_outs:
                        return
                    act.wait_ge(s["product"].sem, s["product"].at(g + 1))
                    if stores:
                        act.wait_ge(c.written[b].sem, c.written[b].at((g - b) * (8 * len(stores))))
                    for n, o in act_outs:
                        last = nc.scalar.activation(target(n, g, b), product(n, b), ACT.Copy)
                    last.then_inc(s["product_out"].sem, 1)
                per_tile(act, evacuate, finish)
    if loads:
        s["loaded"].passed(16 * len(loads))
        s["const_ready"].passed(1)
    s["rows_ready"].passed(nin * G)
    for n in ("turned", "turned_out", "product"):
        s[n].passed(G)
    if act_outs:
        s["product_out"].passed(G)
    if stores:
        for b in range(2):
            c.written[b].passed(16 * len(stores) * ((G + 1 - b) // 2))
    if vec_outs:
        s["outcome_used"].passed(G)
        s["vec"].passed(post_steps * G)


def record(c, key):
    r = c.rec[key][:, :].rearrange("p (t c) -> p t c", c=4)
    return r[:, :, 0].bitcast(I32), r[:, :, 1], r[:, :, 2]


def halves(eng, body):
    for h in range(2):
        body(h, h, True)
    with eng.Fori(1, TILES // (2 * HALF)) as i:
        for h in range(2):
            body(i * 2 + h, h, False)


def stage_index(c, act, key, idx_ring, k, h, freed):
    if freed is not None:
        act.wait_ge(freed.sem, freed.at(k * HALF - HALF))
        act.sem_inc(c.s["act_go"].sem, 1)
    c.nc.scalar.activation(idx_ring[:, h * HALF:(h + 1) * HALF], record(c, key)[0][:, bass.ds(k * HALF, HALF)], ACT.Copy)\
        .then_inc(c.s["ring_staged"].sem, 1)


def gather_rows(c, pool, table, idx_ring, rows):
    nc, s = c.nc, c.s

    def body(k, h, first):
        pool.wait_ge(s["ring_staged"].sem, s["ring_staged"].at(k + 1))
        pool.sem_inc(s["pool_go"].sem, 1)
        for j in range(h * HALF, (h + 1) * HALF):
            nc.gpsimd.indirect_dma_start(rows[:, j * D:(j + 1) * D], None, table[:, :],
                                         bass.IndirectOffsetOnAxis(ap=idx_ring[:, j:j + 1], axis=0))\
                .then_inc(c.arrived[j].sem, 16)
    halves(pool, body)


def gather_passed(c, waits=TILES // HALF - 2):
    c.s["ring_staged"].passed(TILES // HALF)
    c.s["pool_go"].passed(TILES // HALF)
    c.s["act_go"].passed(waits)
    for sig in c.arrived:
        sig.passed(16 * TILES // (2 * HALF))


def aggregate(c, table, key, weighted=False, clear=True):
    nc, s = c.nc, c.s
    _, low, weight = record(c, key)
    rounds = TILES // (2 * HALF)
    with ExitStack() as ctx:
        sb = c.scratch(ctx)
        idx_ring = sb("ag_idx", [P, 2 * HALF], I32)
        rows = sb("ag_rows", [P, 2 * HALF * D], FP32)
        hot = sb("ag_hot", [P, 2 * HALF * P], FP32)
        with nc.Block() as block:
            @block.gpsimd
            def _(pool):
                gather_rows(c, pool, table, idx_ring, rows)

            @block.scalar
            def _(act):
                halves(act, lambda k, h, first: stage_index(c, act, key, idx_ring, k, h, None if first else s["product"]))

            @block.tensor
            def _(pe):
                def body(k, h, first):
                    for j in range(HALF):
                        q = h * HALF + j
                        pe.wait_ge(s["onehot_ready"].sem, s["onehot_ready"].at(k * HALF + j + 1))
                        pe.wait_ge(c.arrived[q].sem, c.arrived[q].at((k - h) * 8 + 16))
                        pe.wait_ge(s["summed"].sem, s["summed"].at(k * HALF + j - HALF + 1))
                        nc.tensor.matmul(c.bank[j][:, 0:D], hot[:, q * P:(q + 1) * P], rows[:, q * D:(q + 1) * D],
                                         start=True, stop=True).then_inc(s["product"].sem, 1)
                halves(pe, body)

            @block.vector
            def _(v):
                if clear:
                    nc.vector.memset(c.ACC[:, :], 0.0).then_inc(s["vec"].sem, 1)
                    v.wait_ge(s["vec"].sem, s["vec"].at(1))

                def hots(k, h):
                    v.wait_ge(s["product"].sem, s["product"].at((k - 1) * HALF))
                    for j in range(HALF):
                        q = h * HALF + j
                        t = bass.ds(k * HALF + j, 1)
                        if weighted:
                            ins = nc.vector.tensor_scalar(hot[:, q * P:(q + 1) * P], c.iota[:, 0:P], low[:, t],
                                                          weight[:, t], ALU.is_equal, ALU.mult)
                        else:
                            ins = nc.vector.tensor_scalar(hot[:, q * P:(q + 1) * P], c.iota[:, 0:P], low[:, t],
                                                          None, ALU.is_equal)
                        ins.then_inc(s["onehot_ready"].sem, 1)

                def sums(k, h):
                    for j in range(HALF):
                        t = k * HALF + j
                        g = v.value_load(c.group[key][0:1, bass.ds(t, 1)], min_val=0, max_val=G - 1)
                        v.wait_ge(s["summed"].sem, s["summed"].at(t))
                        v.wait_ge(s["product"].sem, s["product"].at(t + 1))
                        acc = c.rows(c.ACC, g, D, AW)
                        nc.vector.tensor_tensor(acc, acc, c.bank[j][:, 0:D], ALU.add).then_inc(s["summed"].sem, 1)
                hots(0, 0)
                with v.Fori(0, rounds - 1) as i:
                    for h in range(2):
                        hots(i * 2 + h + 1, 1 - h)
                        sums(i * 2 + h, h)
                k = TILES // HALF - 2
                hots(k + 1, 1)
                sums(k, 0)
                sums(k + 1, 1)
    gather_passed(c)
    for n in ("product", "summed", "onehot_ready"):
        s[n].passed(TILES)
    if clear:
        s["vec"].passed(1)


def spread(row):
    return row.partition_broadcast(P)


def weight_view(w):
    return w.rearrange("(k p) f -> p k f", p=P)


def as_k(t):
    return t.rearrange("p (k f) -> p k f", k=KD)


def gcn(c, a):
    nc, s = c.nc, c.s
    layernorm(c)
    table = c.dram("gcn_table", [NP, D], FP32)
    with ExitStack() as ctx:
        w = ctx.enter_context(nc.sbuf_tensor("gcn_w", [P, KD * D], FP32))
        bias = ctx.enter_context(nc.sbuf_tensor("gcn_b", [P, D], FP32))
        for layer in range(3):
            def scaled(g, out):
                return nc.vector.tensor_scalar(out, c.rows(c.T, g), c.dinv[:, bass.ds(g, 1)], None, ALU.mult)
            project(c, [scaled], [([w], None, ("both", lambda g: c.rows(c.ACC, g, D, AW), table))],
                    loads=[(as_k(w[:, :]), weight_view(a[f"L0_gnn_W{layer + 1}"])),
                           (bias[:, :], spread(a[f"L0_gnn_b{layer + 1}"]))])
            aggregate(c, table, "dst", clear=False)
            last = layer == 2
            with nc.Block() as block:
                @block.vector
                def _(v):
                    with v.Fori(0, G) as g:
                        ch = Chain(v, s["vec"], g)
                        acc, t = c.rows(c.ACC, g, D, AW), c.rows(c.T, g)
                        ch.link(nc.vector.scalar_tensor_tensor(t, acc, c.dinv[:, bass.ds(g, 1)], bias[:, :], ALU.mult, ALU.add))
                    if last:
                        nc.vector.tensor_tensor(c.X[:, :], c.X[:, :], c.T[:, :], ALU.add).then_inc(s["vec"].sem, 1)
            s["vec"].passed(G + last)


def gate_logits(c, w_gate, bias_row, width, logits):
    nc, s = c.nc, c.s
    xt = c.B2[:, :].rearrange("p (k n) -> p k n", k=KD)
    with ExitStack() as ctx:
        sb = c.scratch(ctx)
        ring = sb("gl_ring", [P, 2 * D], FP32)
        w = sb("gl_w", [P, KD * width], FP32)
        row = sb("gl_row", [1, width], FP32)
        with nc.Block() as block:
            @block.sync
            def _(sp):
                sp.dma_start(w[:, :].rearrange("p (k f) -> p k f", k=KD), weight_view(w_gate)).then_inc(s["loaded"].sem, 16)
                sp.dma_start(row[:, :], bias_row).then_inc(s["loaded"].sem, 16)

            @block.vector
            def _(v):
                def stage(g, b):
                    v.wait_ge(s["product"].sem, s["product"].at(g - 1))
                    nc.vector.tensor_copy(ring[:, b * D:(b + 1) * D].rearrange("p (k n) -> p k n", k=KD),
                                          xt[:, :, bass.ds(g * P, P)]).then_inc(s["rows_ready"].sem, 1)

                def out(g, b):
                    v.wait_ge(s["product"].sem, s["product"].at(g + 1))
                    nc.vector.tensor_copy(logits[:, bass.ds(g * width, width)], c.bank[b][:, 0:width])\
                        .then_inc(s["product_out"].sem, 1)
                per_tile(v, stage, out)

            @block.tensor
            def _(pe):
                pe.wait_ge(s["loaded"].sem, s["loaded"].at(32))

                def multiply(g, b):
                    pe.wait_ge(s["rows_ready"].sem, s["rows_ready"].at(g + 1))
                    pe.wait_ge(s["product_out"].sem, s["product_out"].at(g - 1))
                    o = c.bank[b][:, 0:width]
                    for k in range(KD):
                        nc.tensor.matmul(o, ring[:, b * D + k * P:b * D + (k + 1) * P], w[:, k * width:(k + 1) * width],
                                         start=(k == 0), stop=False)
                    nc.tensor.matmul(o, c.ones[0:1, :], row[:, :], start=False, stop=True).then_inc(s["product"].sem, 1)
                per_tile(pe, multiply, lambda g, b: None)
    s["loaded"].passed(32)
    for n in ("rows_ready", "product", "product_out"):
        s[n].passed(G)


class Expert:

    def __init__(self, w1, w2, b2, mid=None):
        self.w1, self.w2, self.b2, self.mid = w1, w2, b2, mid


def experts(c, count, width, expert, act1, column1, gate, mid_act=None, column2=None):
    nc, s = c.nc, c.s
    nf = width // P
    units = 2 * (G // CH)
    xt = c.B2[:, 0:KD * NP].rearrange("p (k n) -> p k n", k=KD)
    mid = mid_act is not None
    n_loads = 4 if mid else 3
    with ExitStack() as ctx:
        sb = c.scratch(ctx)
        w1 = sb("ex_w1", [P, 2 * KD * width], FP32)
        w2 = sb("ex_w2", [P, 2 * nf * D], FP32)
        b2 = sb("ex_b2", [P, 2 * D], FP32)
        wm = sb("ex_wm", [P, 2 * nf * width], FP32) if mid else None
        hid = sb("ex_hid", [P, 2 * nf * TOK], FP32)
        hid2 = sb("ex_hid2", [P, 2 * nf * TOK], FP32) if mid else hid
        tmp = sb("ex_tmp", [P, 4 * D], FP32)
        stages = 2 if mid else 1
        tables = [x for col in (column1, column2) if col for x in col if not isinstance(x, float)]
        local = [sb(f"ex_column{n}", [P, 2 * nf], FP32) for n in range(len(tables))]
        per_unit = stages * nf * 2

        def h(buf, slot, f, n0, n):
            o = (slot * nf + f) * TOK + n0
            return buf[:, o:o + n]

        def outcome_bank(n):
            return c.bank[4 + n % 2][:, 0:D]

        def rounds(eng, body):
            if count > 2:
                with eng.Fori(0, count // 2 - 1) as i:
                    body(i, False)
            body(count // 2 - 1, True)

        with nc.Block() as block:
            @block.sync
            def _(sp):
                def load(e, slot, used):
                    if used is not None:
                        sp.wait_ge(s["weights_used"].sem, s["weights_used"].at(used))
                    sig = s["wa"] if slot == 0 else s["wb"]
                    pairs = [(w1[:, slot * KD * width:(slot + 1) * KD * width].rearrange("p (k f) -> p k f", k=KD), expert.w1(sp, e)),
                             (w2[:, slot * nf * D:(slot + 1) * nf * D].rearrange("p (k f) -> p k f", k=nf), expert.w2(sp, e)),
                             (b2[:, slot * D:(slot + 1) * D], expert.b2(sp, e))]
                    if mid:
                        pairs.append((wm[:, slot * nf * width:(slot + 1) * nf * width].rearrange("p (k f) -> p k f", k=nf),
                                      expert.mid(sp, e)))
                    for dst, src in pairs:
                        sp.dma_start(dst, src).then_inc(sig.sem, 16)
                load(0, 0, None)
                load(1, 1, None)
                if count > 2:
                    with sp.Fori(1, count // 2) as i:
                        load(i * 2, 0, i * 2 - 1)
                        load(i * 2 + 1, 1, i * 2)

            def weights_here(eng, i, slot, ahead=0):
                sig = s["wa"] if slot == 0 else s["wb"]
                eng.wait_ge(sig.sem, sig.at((i + ahead) * (16 * n_loads) + 16 * n_loads))

            @block.tensor
            def _(pe):
                def first_layer(i, u):
                    ahead, u = u // units, u % units
                    slot, ck, q = u // (units // 2), u % (units // 2), u % 2
                    if ck == 0:
                        weights_here(pe, i, slot, ahead)
                    n0 = (i + ahead) * (units * per_unit) + u * per_unit
                    for f in range(nf):
                        for half in range(2):
                            n = f * 2 + half
                            bank = n % 4
                            pe.wait_ge(s["hidden_out"].sem, s["hidden_out"].at(n0 + n - 3))
                            for k in range(KD):
                                last = nc.tensor.matmul(
                                    c.bank[bank][:, 0:HT], w1[:, (slot * KD + k) * width + f * P:(slot * KD + k) * width + (f + 1) * P],
                                    xt[:, k, ck * TOK + half * HT:ck * TOK + (half + 1) * HT], start=(k == 0), stop=(k == KD - 1))
                            last.then_inc(s["hidden"].sem, 1)

                def mid_layer(i, u):
                    slot, q = u // (units // 2), u % 2
                    n0 = i * (units * per_unit) + u * per_unit + nf * 2
                    pe.wait_ge(s["hidden_out"].sem, s["hidden_out"].at(n0))
                    for f in range(nf):
                        for half in range(2):
                            n = f * 2 + half
                            for k in range(nf):
                                last = nc.tensor.matmul(
                                    c.bank[n % 4][:, 0:HT], wm[:, (slot * nf + k) * width + f * P:(slot * nf + k) * width + (f + 1) * P],
                                    h(hid, q, k, half * HT, HT), start=(k == 0), stop=(k == nf - 1))
                            last.then_inc(s["hidden"].sem, 1)

                def last_layer(i, u, is_last):
                    slot, q = u // (units // 2), u % 2
                    pe.wait_ge(s["hidden_out"].sem, s["hidden_out"].at(i * (units * per_unit) + (u + 1) * per_unit))
                    for t in range(CH):
                        n = u * CH + t
                        pe.wait_ge(s["outcome_used"].sem, s["outcome_used"].at(i * (units * CH) + n - 1))
                        for k in range(nf):
                            last = nc.tensor.matmul(outcome_bank(n), h(hid2, q, k, t * P, P), w2[:, (slot * nf + k) * D:(slot * nf + k + 1) * D],
                                                    start=(k == 0), stop=(k == nf - 1))
                        last.then_inc(s["outcome"].sem, 1)

                if mid:
                    def body(i, is_last):
                        for u in range(units):
                            first_layer(i, u)
                            mid_layer(i, u)
                            last_layer(i, u, is_last)
                    rounds(pe, body)
                else:
                    first_layer(0, 0)

                    def body(i, is_last):
                        for u in range(units):
                            if not (is_last and u == units - 1):
                                first_layer(i, u + 1)
                            last_layer(i, u, is_last)
                    rounds(pe, body)

            @block.scalar
            def _(act):
                def body(i, is_last):
                    for u in range(units):
                        e_slot, q = u // (units // 2), u % 2
                        e = i * 2 + e_slot
                        act.wait_ge(s["outcome"].sem, s["outcome"].at(i * (units * CH) + (u - 1) * CH))
                        if u % (units // 2) == 0:
                            act.sem_inc(s["act_go"].sem, 1)
                            for n, table in enumerate(tables):
                                nc.scalar.activation(local[n][:, e_slot * nf:(e_slot + 1) * nf],
                                                     table[:, bass.ds(e * nf, nf)], ACT.Copy).then_inc(s["act"].sem, 1)
                            act.wait_ge(s["act"].sem, s["act"].at((i * 2 + e_slot + 1) * len(tables)))
                        for stage in range(stages):
                            fn, column = ((act1, column1), (mid_act, column2))[stage]
                            for f in range(nf):
                                scale, bias = [x if isinstance(x, float) else
                                               local[tables.index(x)][:, e_slot * nf + f:e_slot * nf + f + 1] for x in column]
                                for half in range(2):
                                    n = stage * nf * 2 + f * 2 + half
                                    act.wait_ge(s["hidden"].sem, s["hidden"].at(i * (units * per_unit) + u * per_unit + n + 1))
                                    nc.scalar.activation(h(hid if stage == 0 else hid2, q, f, half * HT, HT),
                                                         c.bank[(f * 2 + half) % 4][:, 0:HT], fn, bias=bias, scale=scale)\
                                        .then_inc(s["hidden_out"].sem, 1)
                rounds(act, body)

            @block.vector
            def _(v):
                nc.vector.memset(c.ACC[:, :], 0.0).then_inc(s["vec"].sem, 1)
                v.wait_ge(s["vec"].sem, s["vec"].at(1))

                def body(i, is_last):
                    for u in range(units):
                        slot, ck = u // (units // 2), u % (units // 2)
                        if ck == 0:
                            weights_here(v, i, slot)
                        for t in range(CH):
                            n = u * CH + t
                            tile = ck * CH + t
                            part = tmp[:, (n % 2) * D:(n % 2 + 1) * D]
                            v.wait_ge(s["outcome"].sem, s["outcome"].at(i * (units * CH) + n + 1))
                            nc.vector.tensor_tensor(part, outcome_bank(n), b2[:, slot * D:(slot + 1) * D], ALU.add)\
                                .then_inc(s["outcome_used"].sem, 1)
                            v.wait_ge(s["outcome_used"].sem, s["outcome_used"].at(i * (units * CH) + n + 1))
                            acc = c.ACC[:, tile * AW:tile * AW + D]
                            nc.vector.scalar_tensor_tensor(acc, part, gate(tile, i * 2 + slot), acc, ALU.mult, ALU.add)\
                                .then_inc(s["vec"].sem, 1)
                            v.wait_ge(s["vec"].sem, s["vec"].at(i * (units * CH) + n + 2))
                        if ck == units // 2 - 1:
                            v.sem_inc(s["weights_used"].sem, 1)
                rounds(v, body)
    pairs = count // 2
    for n in ("wa", "wb"):
        s[n].passed(pairs * 16 * n_loads)
    s["weights_used"].passed(count)
    s["act"].passed(count * len(tables))
    s["hidden"].passed(pairs * units * per_unit)
    s["hidden_out"].passed(pairs * units * per_unit)
    s["outcome"].passed(pairs * units * CH)
    s["outcome_used"].passed(pairs * units * CH)
    s["vec"].passed(pairs * units * CH + 1)


def top_two(c, logits, width, gates):
    nc, s = c.nc, c.s
    with ExitStack() as ctx:
        sb = c.scratch(ctx)
        best, where = sb("tt_best", [P, G * 8], FP32), sb("tt_where", [P, G * 8], U32)
        where_f = sb("tt_where_f", [P, G * 8], FP32)
        w = sb("tt_w", [P, 4 * G], FP32)
        hot = sb("tt_hot", [P, G * width], FP32)
        b3 = best[:, :].rearrange("p (g e) -> p g e", e=8)
        w3 = where_f[:, :].rearrange("p (g e) -> p g e", e=8)
        g3 = gates.rearrange("p (g e) -> p g e", e=width)
        h3 = hot[:, :].rearrange("p (g e) -> p g e", e=width)
        number = c.iota[:, 0:width].unsqueeze(1).broadcast_to([P, G, width])

        def wide(col):
            return col.unsqueeze(2).broadcast_to([P, G, width])
        e2, share1, share2 = w[:, 0:G], w[:, G:2 * G], w[:, 2 * G:3 * G]
        with nc.Block() as block:
            @block.vector
            def _(v):
                ch = Chain(v, s["vec"])
                for g in range(G):
                    row = logits[:, g * width:(g + 1) * width]
                    ch.link(nc.vector.max(best[:, g * 8:(g + 1) * 8], row))
                    ch.link(nc.vector.max_index(where[:, g * 8:(g + 1) * 8], best[:, g * 8:(g + 1) * 8], row))
                ch.link(nc.vector.tensor_copy(where_f[:, :], where[:, :]))
                ch.link(nc.vector.tensor_tensor(e2, b3[:, :, 1], b3[:, :, 0], ALU.subtract))
                v.sem_inc(s["stats_ready"].sem, 1)
                v.wait_ge(s["act"].sem, s["act"].at(1))
                ch.link(nc.vector.tensor_scalar(share1, e2, 1.0, None, ALU.add))
                ch.link(nc.vector.reciprocal(share1, share1))
                ch.link(nc.vector.tensor_tensor(share2, share1, e2, ALU.mult))
                ch.link(nc.vector.tensor_tensor(g3, number, wide(w3[:, :, 0]), ALU.is_equal))
                ch.link(nc.vector.tensor_tensor(g3, g3, wide(share1), ALU.mult))
                ch.link(nc.vector.tensor_tensor(h3, number, wide(w3[:, :, 1]), ALU.is_equal))
                ch.link(nc.vector.tensor_tensor(h3, h3, wide(share2), ALU.mult))
                ch.link(nc.vector.tensor_tensor(g3, g3, h3, ALU.add))
                c.vec_steps = ch.n

            @block.scalar
            def _(act):
                act.wait_ge(s["stats_ready"].sem, s["stats_ready"].at(1))
                nc.scalar.activation(e2, e2, ACT.Exp).then_inc(s["act"].sem, 1)
    s["vec"].passed(c.vec_steps)
    s["stats_ready"].passed(1)
    s["act"].passed(1)


def columns(v):
    return v.rearrange("e (f p) -> p (e f)", p=P)


def moe_relu(c, a):
    nc, s = c.nc, c.s
    layernorm(c, turn=True)
    ne, width = 16, 512
    nf = width // P
    with ExitStack() as ctx:
        sb = c.scratch(ctx)
        logits, gates = sb("logits", [P, G * ne], FP32), sb("gates", [P, G * ne], FP32)
        b1 = sb("b1", [P, ne * nf], FP32)
        gamma, beta = sb("gamma", [P, D], FP32), sb("beta", [P, D], FP32)
        load(c, [(b1[:, :], columns(a["L0_ffn_b1"])), (gamma[:, :], spread(a["L0_ffn_gamma"])),
                 (beta[:, :], spread(a["L0_ffn_beta"]))])
        gate_logits(c, a["L0_ffn_gate_w"], a["L0_ffn_gate_b"].unsqueeze(0), ne, logits)
        top_two(c, logits[:, :], ne, gates[:, :])
        w1, w2, b2 = a["L0_ffn_w1"], a["L0_ffn_w2"], a["L0_ffn_b2"]
        experts(c, ne, width,
                Expert(lambda sp, e: at_expert(w1, e), lambda sp, e: at_expert(w2, e), lambda sp, e: row_spread(b2, e)),
                ACT.Relu, (1.0, b1),
                lambda tile, e: gates[:, bass.ds(e + tile * ne, 1)])
        add_normed(c, gamma, beta)


def load(c, pairs):
    s = c.s
    with c.nc.Block() as block:
        @block.sync
        def _(sp):
            for dst, src in pairs:
                sp.dma_start(dst, src, allow_slow_non_contiguous=True).then_inc(s["loaded"].sem, 16)
            sp.wait_ge(s["loaded"].sem, s["loaded"].at(16 * len(pairs)))
    s["loaded"].passed(16 * len(pairs))


def at_expert(w, e):
    return w[bass.ds(e, 1), :, :].rearrange("e (k p) f -> p (e k) f", p=P)


def row_spread(b, e):
    return b[bass.ds(e, 1), :].squeeze(0).partition_broadcast(P)


def add_normed(c, gamma, beta, eps=1e-5):
    nc, s = c.nc, c.s
    with ExitStack() as ctx:
        sb = c.scratch(ctx)
        stats, agg = sb("an_stats", [P, 6 * CH], FP32), sb("an_agg", [P, 2 * CH], FP32)
        before = 4 * (G // CH) + 3
        with nc.Block() as block:
            @block.vector
            def _(v):
                def add(g):
                    return nc.vector.tensor_tensor(c.rows(c.T, g), c.rows(c.T, g), c.rows(c.ACC, g, D, AW), ALU.add)
                ch = Chain(v, s["vec"], row_stats(c, v, stats, agg, lambda g: c.rows(c.T, g), 0, add))
                pair = c.stat_pair[:, :].rearrange("p (g n) -> p g n", n=2)
                ch.link(nc.vector.tensor_copy(c.mean[:, :], pair[:, :, 0]))
                ch.link(nc.vector.tensor_scalar(c.rstd[:, :], pair[:, :, 1], eps, None, ALU.add))
                v.sem_inc(s["stats_ready"].sem, 1)
                v.wait_ge(s["act"].sem, s["act"].at(1))
                ch.link(nc.vector.reciprocal(c.rstd[:, :], c.rstd[:, :]))
                with v.Fori(0, G) as g:
                    last = nc.vector.tensor_scalar(c.rows(c.T, g), c.rows(c.T, g), c.mean[:, bass.ds(g, 1)],
                                                   c.rstd[:, bass.ds(g, 1)], ALU.subtract, ALU.mult)
                    last.then_inc(s["vec"].sem, 1)
                v.wait_ge(s["vec"].sem, s["vec"].at(before + G))
                ch = Chain(v, s["vec"], before + G)
                t3 = c.T[:, :].rearrange("p (g d) -> p g d", d=D)

                def wide(x):
                    return x[:, :].unsqueeze(1).broadcast_to([P, G, D])
                ch.link(nc.vector.tensor_tensor(t3, t3, wide(gamma), ALU.mult))
                ch.link(nc.vector.tensor_tensor(t3, t3, wide(beta), ALU.add))
                ch.link(nc.vector.tensor_tensor(c.X[:, :], c.X[:, :], c.T[:, :], ALU.add))

            @block.scalar
            def _(act):
                act.wait_ge(s["stats_ready"].sem, s["stats_ready"].at(1))
                nc.scalar.activation(c.rstd[:, :], c.rstd[:, :], ACT.Sqrt).then_inc(s["act"].sem, 1)
    s["vec"].passed(before + G + 3)
    s["stats_ready"].passed(1)
    s["act"].passed(1)


def add_rows(c, buf, step, bias=None):
    nc, s = c.nc, c.s
    x3 = c.X[:, :].rearrange("p (g d) -> p g d", d=D)
    with nc.Block() as block:
        @block.vector
        def _(v):
            ch = Chain(v, s["vec"])
            ch.link(nc.vector.tensor_tensor(x3, x3, buf[:, :].rearrange("p (g d) -> p g d", d=step)[:, :, 0:D], ALU.add))
            if bias is not None:
                ch.link(nc.vector.tensor_tensor(x3, x3, bias[:, :].unsqueeze(1).broadcast_to([P, G, D]), ALU.add))
    s["vec"].passed(2 if bias is not None else 1)


def pairs_of_halves(eng, body):
    n = TILES // (2 * HALF)
    with eng.Fori(0, n - 1) as i:
        for h in range(2):
            body(i * 2 + h, h, False)
    body(2 * n - 2, 0, False)
    body(2 * n - 1, 1, True)


def edge_scores(c, k_table, scores):
    nc, s = c.nc, c.s
    _, low, _ = record(c, "dst")
    with ExitStack() as ctx:
        sb = c.scratch(ctx)
        idx_ring = sb("es_idx", [P, 2 * HALF], I32)
        rows = sb("es_rows", [P, 2 * HALF * D], FP32)
        hot = sb("es_hot", [P, 2 * HALF * P], FP32)
        hot_t = sb("es_hot_t", [P, 4 * P], FP32)
        prod = sb("es_prod", [P, HALF * D], FP32)
        with nc.Block() as block:
            @block.gpsimd
            def _(pool):
                gather_rows(c, pool, k_table, idx_ring, rows)

            @block.tensor
            def _(pe):
                def turn(t, q, j):
                    pe.wait_ge(s["onehot_ready"].sem, s["onehot_ready"].at(t + 1))
                    pe.wait_ge(s["turned_out"].sem, s["turned_out"].at(t - 3))
                    nc.tensor.transpose(c.bank[j % 4][:, 0:P], hot[:, q * P:(q + 1) * P], c.ident[:, :])\
                        .then_inc(s["turned"].sem, 1)

                def body(k, h, last):
                    for j in range(HALF):
                        t = k * HALF + j
                        if not (last and j == HALF - 1):
                            turn(t + 1, (h * HALF + j + 1) % (2 * HALF), j + 1)
                        g = pe.value_load(c.group["dst"][0:1, bass.ds(t, 1)], min_val=0, max_val=G - 1)
                        pe.wait_ge(s["turned_out"].sem, s["turned_out"].at(t + 1))
                        pe.wait_ge(s["summed"].sem, s["summed"].at(t - 3))
                        nc.tensor.matmul(c.bank[4 + j % 4][:, 0:D], hot_t[:, (j % 4) * P:(j % 4 + 1) * P], c.rows(c.B2, g),
                                         start=True, stop=True).then_inc(s["product"].sem, 1)
                turn(0, 0, 0)
                pairs_of_halves(pe, body)

            @block.scalar
            def _(act):
                def body(k, h, last):
                    for j in range(HALF):
                        t = k * HALF + j
                        act.wait_ge(s["turned"].sem, s["turned"].at(t + 1))
                        act.wait_ge(s["product"].sem, s["product"].at(t - 3))
                        nc.scalar.activation(hot_t[:, (j % 4) * P:(j % 4 + 1) * P], c.bank[j % 4][:, 0:P], ACT.Copy)\
                            .then_inc(s["turned_out"].sem, 1)
                        if j == HALF // 2 and not last:
                            stage_index(c, act, "dst", idx_ring, k + 1, 1 - h, s["summed"])
                stage_index(c, act, "dst", idx_ring, 0, 0, None)
                pairs_of_halves(act, body)

            @block.vector
            def _(v):
                def hots(k, h):
                    v.wait_ge(s["turned"].sem, s["turned"].at((k - 1) * HALF))
                    for j in range(HALF):
                        q = h * HALF + j
                        nc.vector.tensor_scalar(hot[:, q * P:(q + 1) * P], c.iota[:, 0:P], low[:, bass.ds(k * HALF + j, 1)],
                                                None, ALU.is_equal).then_inc(s["onehot_ready"].sem, 1)

                def body(k, h, last):
                    if not last:
                        hots(k + 1, 1 - h)
                    for j in range(HALF):
                        q = h * HALF + j
                        v.wait_ge(s["product"].sem, s["product"].at(k * HALF + j + 1))
                        v.wait_ge(c.arrived[q].sem, c.arrived[q].at((k - h) * 8 + 16))
                        v.wait_ge(s["vec"].sem, s["vec"].at(k))
                        nc.vector.tensor_tensor(prod[:, j * D:(j + 1) * D], c.bank[4 + j % 4][:, 0:D],
                                                rows[:, q * D:(q + 1) * D], ALU.mult).then_inc(s["summed"].sem, 1)
                    v.wait_ge(s["summed"].sem, s["summed"].at((k + 1) * HALF))
                    nc.vector.tensor_reduce(scores[:, bass.ds(k * (HALF * HEADS), HALF * HEADS)],
                                            prod[:, :].rearrange("p (h e) -> p h e", e=DK), AX.X, ALU.add)\
                        .then_inc(s["vec"].sem, 1)
                hots(0, 0)
                pairs_of_halves(v, body)
    gather_passed(c, TILES // HALF - 1)
    for n in ("product", "summed", "onehot_ready", "turned", "turned_out"):
        s[n].passed(TILES)
    s["vec"].passed(TILES // HALF)


def score_maxima(c, scores, maxima):
    nc, s = c.nc, c.s
    _, low, _ = record(c, "dst")
    W = 3 * HEADS
    with ExitStack() as ctx:
        sb = c.scratch(ctx)
        parts = sb("sm_parts", [P, TILES * W], BF16)
        rest = sb("sm_rest", [P, TILES * HEADS], FP32)
        ring = sb("sm_ring", [P, 2 * HALF * W], BF16)
        turned = sb("sm_turned", [W, 2 * P], BF16)
        miss = sb("sm_miss", [P, 2 * HALF * P], BF16)
        pick = sb("sm_pick", [W, HEADS * P], BF16)
        big = sb("sm_big", [P, 4 * P], BF16)
        ident_b = sb("sm_ident", [P, P], BF16)
        tile_max = sb("sm_tile_max", [P, 2 * HEADS], FP32)
        part = parts[:, :].rearrange("p (t k e) -> p t k e", k=3, e=HEADS)
        s3 = scores.rearrange("p (t e) -> p t e", e=HEADS)
        r3 = rest[:, :].rearrange("p (t e) -> p t e", e=HEADS)
        with nc.Block() as block:
            @block.gpsimd
            def _(pool):
                nc.gpsimd.memset(pick[:, :], 0.0).then_inc(s["pool"].sem, 1)
                for n in range(3):
                    pool.wait_ge(s["pool"].sem, s["pool"].at(n + 1))
                    v3 = pick[:, :].rearrange("r (h n) -> r h n", n=P)
                    nc.gpsimd.affine_select(out=v3, in_=v3, compare_op=ALU.not_equal, fill=1.0, base=-n * HEADS,
                                            pattern=[[-1, HEADS], [0, P]], channel_multiplier=1).then_inc(s["pool"].sem, 1)
                pool.wait_ge(s["mask_ready"].sem, s["mask_ready"].at(1))

                def body(k, h, last):
                    pool.wait_ge(s["turned"].sem, s["turned"].at((k - 1) * HALF))
                    pool.sem_inc(s["pool_go"].sem, 1)
                    nc.gpsimd.tensor_copy(ring[:, h * HALF * W:(h + 1) * HALF * W], parts[:, bass.ds(k * (HALF * W), HALF * W)])\
                        .then_inc(s["ring_staged"].sem, 1)
                pairs_of_halves(pool, body)

            @block.tensor
            def _(pe):
                pe.wait_ge(s["pool"].sem, s["pool"].at(4))
                pe.wait_ge(s["mask_ready"].sem, s["mask_ready"].at(1))

                def turn(t, q, j, k):
                    pe.wait_ge(s["ring_staged"].sem, s["ring_staged"].at(k + 1))
                    pe.wait_ge(s["turned_out"].sem, s["turned_out"].at(t - 1))
                    nc.tensor.transpose(c.bank[6 + j % 2][:, 0:P // 2].bitcast(BF16)[0:W, 0:P],
                                        ring[:, q * W:(q + 1) * W], ident_b[:, :]).then_inc(s["turned"].sem, 1)

                def body(k, h, last):
                    for j in range(HALF):
                        t, q = k * HALF + j, h * HALF + j
                        if not (last and j == HALF - 1):
                            turn(t + 1, (q + 1) % (2 * HALF), j + 1, k + (j + 1) // HALF)
                        pe.wait_ge(s["onehot_ready"].sem, s["onehot_ready"].at(t + 1))
                        pe.wait_ge(s["summed"].sem, s["summed"].at(t - 1))
                        pe.wait_ge(s["turned_out"].sem, s["turned_out"].at(t + 1))
                        for n in range(2):
                            o = c.bank[2 * (j % 2) + n]
                            nc.tensor.matmul(o[:, :], miss[:, q * P:(q + 1) * P], big[:, :], start=True, stop=False)
                            for e in range(4):
                                head = 4 * n + e
                                last_mm = nc.tensor.matmul(o[:, e * P:(e + 1) * P], pick[:, head * P:(head + 1) * P],
                                                           turned[:, (j % 2) * P:(j % 2 + 1) * P], start=False, stop=(e == 3))
                        last_mm.then_inc(s["product"].sem, 1)
                turn(0, 0, 0, 0)
                pairs_of_halves(pe, body)

            @block.scalar
            def _(act):
                def body(k, h, last):
                    for j in range(HALF):
                        t = k * HALF + j
                        act.wait_ge(s["turned"].sem, s["turned"].at(t + 1))
                        act.wait_ge(s["product"].sem, s["product"].at(t - 1))
                        nc.scalar.activation(turned[:, (j % 2) * P:(j % 2 + 1) * P],
                                             c.bank[6 + j % 2][:, 0:P // 2].bitcast(BF16)[0:W, 0:P], ACT.Copy)\
                            .then_inc(s["turned_out"].sem, 1)
                pairs_of_halves(act, body)

            @block.vector
            def _(v):
                ch = Chain(v, s["vec"])
                ch.link(nc.vector.tensor_copy(part[:, :, 0, :], s3))
                ch.link(nc.vector.tensor_tensor(r3, s3, part[:, :, 0, :], ALU.subtract))
                ch.link(nc.vector.tensor_copy(part[:, :, 1, :], r3))
                ch.link(nc.vector.tensor_tensor(r3, r3, part[:, :, 1, :], ALU.subtract))
                ch.link(nc.vector.tensor_copy(part[:, :, 2, :], r3))
                ch.link(nc.vector.tensor_copy(ident_b[:, :], c.ident[:, :]))
                for n in range(4):
                    ch.link(nc.vector.tensor_scalar(big[:, n * P:(n + 1) * P], c.ident[:, :], BIG, None, ALU.mult))
                ch.link(nc.vector.memset(maxima[:, :], -BIG))
                v.sem_inc(s["mask_ready"].sem, 1)
                before = ch.n

                def misses(k, h):
                    v.wait_ge(s["product"].sem, s["product"].at((k - 1) * HALF))
                    for j in range(HALF):
                        q = h * HALF + j
                        nc.vector.tensor_scalar(miss[:, q * P:(q + 1) * P], c.iota[:, 0:P], low[:, bass.ds(k * HALF + j, 1)],
                                                -1.0, ALU.is_equal, ALU.add).then_inc(s["onehot_ready"].sem, 1)

                def body(k, h, last):
                    if not last:
                        misses(k + 1, 1 - h)
                    for j in range(HALF):
                        t = k * HALF + j
                        g = v.value_load(c.group["dst"][0:1, bass.ds(t, 1)], min_val=0, max_val=G - 1)
                        v.wait_ge(s["product"].sem, s["product"].at(t + 1))
                        o = (j % 2) * HEADS
                        for n in range(2):
                            red = nc.vector.tensor_reduce(tile_max[:, o + 4 * n:o + 4 * n + 4],
                                                          c.bank[2 * (j % 2) + n][:, :].rearrange("p (h e) -> p h e", e=P),
                                                          AX.X, ALU.max)
                        red.then_inc(s["summed"].sem, 1)
                        v.wait_ge(s["summed"].sem, s["summed"].at(t + 1))
                        v.wait_ge(s["vec"].sem, s["vec"].at(t + before))
                        m = c.rows(maxima, g, HEADS)
                        nc.vector.tensor_tensor(m, m, tile_max[:, o:o + HEADS], ALU.max).then_inc(s["vec"].sem, 1)
                misses(0, 0)
                pairs_of_halves(v, body)
                c.vec_steps = before
    s["vec"].passed(c.vec_steps + TILES)
    s["pool"].passed(4)
    s["pool_go"].passed(TILES // HALF)
    s["ring_staged"].passed(TILES // HALF)
    s["mask_ready"].passed(1)
    for n in ("product", "summed", "onehot_ready", "turned", "turned_out"):
        s[n].passed(TILES)


def attend(c, v_table, scores, maxima):
    nc, s = c.nc, c.s
    _, low, _ = record(c, "dst")
    with ExitStack() as ctx:
        sb = c.scratch(ctx)
        idx_ring = sb("at_idx", [P, 2 * HALF], I32)
        rows = sb("at_rows", [P, 2 * HALF * D], FP32)
        hot = sb("at_hot", [P, 2 * HALF * P], FP32)
        hot_t = sb("at_hot_t", [P, HALF * P], FP32)
        diff = sb("at_diff", [P, 2 * HALF * HEADS], FP32)
        weighed = sb("at_weighed", [P, HALF * AW], FP32)
        w3 = weighed[:, :].rearrange("p (t a) -> p t a", a=AW)
        with nc.Block() as block:
            @block.gpsimd
            def _(pool):
                gather_rows(c, pool, v_table, idx_ring, rows)

            @block.tensor
            def _(pe):
                def peaks(k, h):
                    for m in range(2):
                        pe.wait_ge(s["onehot_ready"].sem, s["onehot_ready"].at(k * HALF + 4 * m + 4))
                        pe.wait_ge(s["turned_out"].sem, s["turned_out"].at(k * 2 + m - 1))
                        for j in range(4 * m, 4 * m + 4):
                            q = h * HALF + j
                            turn = nc.tensor.transpose(c.bank[m][:, (j % 4) * P:(j % 4 + 1) * P], hot[:, q * P:(q + 1) * P],
                                                       c.ident[:, :])
                        turn.then_inc(s["turned"].sem, 1)
                    pe.wait_ge(s["vec"].sem, s["vec"].at(k))
                    for j in range(HALF):
                        g = pe.value_load(c.group["dst"][0:1, bass.ds(k * HALF + j, 1)], min_val=0, max_val=G - 1)
                        if j % 4 == 0:
                            pe.wait_ge(s["turned_out"].sem, s["turned_out"].at(k * 2 + j // 4 + 1))
                        peak = nc.tensor.matmul(c.bank[2 + h][:, j * HEADS:(j + 1) * HEADS], hot_t[:, j * P:(j + 1) * P],
                                                c.rows(maxima, g, HEADS), start=True, stop=True)
                    peak.then_inc(s["hot_used"].sem, 1)

                def body(k, h, last):
                    if not last:
                        peaks(k + 1, 1 - h)
                    for j in range(HALF):
                        q = h * HALF + j
                        pe.wait_ge(s["score_ready"].sem, s["score_ready"].at(k * HALF + j + 1))
                        pe.wait_ge(s["summed"].sem, s["summed"].at(k * HALF + j - 3))
                        nc.tensor.matmul(c.bank[4 + j % 4][:, 0:AW], hot[:, q * P:(q + 1) * P], weighed[:, j * AW:(j + 1) * AW],
                                         start=True, stop=True).then_inc(s["product"].sem, 1)
                peaks(0, 0)
                pairs_of_halves(pe, body)

            @block.scalar
            def _(act):
                def turns(k, h):
                    for m in range(2):
                        act.wait_ge(s["turned"].sem, s["turned"].at(k * 2 + m + 1))
                        act.wait_ge(s["hot_used"].sem, s["hot_used"].at(k))
                        nc.scalar.activation(hot_t[:, 4 * m * P:4 * (m + 1) * P], c.bank[m][:, :], ACT.Copy)\
                            .then_inc(s["turned_out"].sem, 1)

                def body(k, h, last):
                    act.wait_ge(s["vec"].sem, s["vec"].at(k + 1 + 1))
                    act.wait_ge(s["product"].sem, s["product"].at(k * HALF))
                    nc.scalar.activation(w3[:, :, D:AW],
                                         diff[:, h * HALF * HEADS:(h + 1) * HALF * HEADS].rearrange("p (t e) -> p t e", e=HEADS),
                                         ACT.Exp).then_inc(s["exps_ready"].sem, 1)
                    if not last:
                        stage_index(c, act, "dst", idx_ring, k + 1, 1 - h, s["score_ready"])
                        turns(k + 1, 1 - h)
                stage_index(c, act, "dst", idx_ring, 0, 0, None)
                turns(0, 0)
                pairs_of_halves(act, body)

            @block.vector
            def _(v):
                nc.vector.memset(c.ACC[:, :], 0.0).then_inc(s["vec"].sem, 1)
                v.wait_ge(s["vec"].sem, s["vec"].at(1))

                def hots(k, h):
                    v.wait_ge(s["product"].sem, s["product"].at((k - 1) * HALF))
                    for j in range(HALF):
                        q = h * HALF + j
                        nc.vector.tensor_scalar(hot[:, q * P:(q + 1) * P], c.iota[:, 0:P], low[:, bass.ds(k * HALF + j, 1)],
                                                None, ALU.is_equal).then_inc(s["onehot_ready"].sem, 1)

                def body(k, h, last):
                    if not last:
                        hots(k + 1, 1 - h)
                    v.wait_ge(s["hot_used"].sem, s["hot_used"].at(k + 1))
                    v.wait_ge(s["exps_ready"].sem, s["exps_ready"].at(k - 1))
                    nc.vector.tensor_tensor(diff[:, h * HALF * HEADS:(h + 1) * HALF * HEADS],
                                            scores[:, bass.ds(k * (HALF * HEADS), HALF * HEADS)],
                                            c.bank[2 + h][:, 0:HALF * HEADS], ALU.subtract).then_inc(s["vec"].sem, 1)
                    v.wait_ge(s["exps_ready"].sem, s["exps_ready"].at(k + 1))
                    for j in range(HALF):
                        q = h * HALF + j
                        v.wait_ge(c.arrived[q].sem, c.arrived[q].at((k - h) * 8 + 16))
                        nc.vector.tensor_tensor(
                            w3[:, j, 0:D].rearrange("p (h e) -> p h e", e=DK),
                            rows[:, q * D:(q + 1) * D].rearrange("p (h e) -> p h e", e=DK),
                            w3[:, j, D:AW].unsqueeze(2).broadcast_to([P, HEADS, DK]), ALU.mult).then_inc(s["score_ready"].sem, 1)
                    for j in range(HALF):
                        t = k * HALF + j
                        g = v.value_load(c.group["dst"][0:1, bass.ds(t, 1)], min_val=0, max_val=G - 1)
                        v.wait_ge(s["product"].sem, s["product"].at(t + 1))
                        v.wait_ge(s["summed"].sem, s["summed"].at(t))
                        acc = c.rows(c.ACC, g, AW)
                        nc.vector.tensor_tensor(acc, acc, c.bank[4 + j % 4][:, 0:AW], ALU.add).then_inc(s["summed"].sem, 1)
                hots(0, 0)
                pairs_of_halves(v, body)
    gather_passed(c, TILES // HALF - 1)
    for n in ("product", "summed", "onehot_ready", "score_ready"):
        s[n].passed(TILES)
    for n in ("turned", "turned_out"):
        s[n].passed(TILES // 4)
    s["hot_used"].passed(TILES // HALF)
    s["exps_ready"].passed(TILES // HALF)
    s["vec"].passed(TILES // HALF + 1)


def fold(c, w, bias, rel, out_w, out_row, pri=None):
    nc, s = c.nc, c.s
    with ExitStack() as ctx:
        sb = c.scratch(ctx)
        wt, r, b = sb("fo_w", [P, KD * D], FP32), sb("fo_r", [P, KD * D], FP32), sb("fo_b", [P, KD], FP32)
        n_loads = 2 + HEADS
        with nc.Block() as block:
            @block.sync
            def _(sp):
                sp.dma_start(as_k(wt[:, :]), weight_view(w)).then_inc(s["loaded"].sem, 16)
                sp.dma_start(b[:, :], bias.rearrange("(k p) -> p k", p=P), allow_slow_non_contiguous=True)\
                    .then_inc(s["loaded"].sem, 16)
                sp.wait_ge(s["vec"].sem, s["vec"].at(1))
                for h in range(HEADS):
                    p0, k = DK * (h % 4), h // 4
                    sp.dma_start(r[p0:p0 + DK, k * D + h * DK:k * D + (h + 1) * DK], rel[h, :, :]).then_inc(s["loaded"].sem, 16)
                sp.wait_ge(s["loaded"].sem, s["loaded"].at(16 * n_loads))

            @block.tensor
            def _(pe):
                pe.wait_ge(s["loaded"].sem, s["loaded"].at(16 * n_loads))
                for m in range(KD):
                    for k in range(KD):
                        nc.tensor.matmul(c.bank[m][:, 0:D], wt[:, k * D + m * P:k * D + (m + 1) * P], r[:, k * D:(k + 1) * D],
                                         start=(k == 0), stop=(k == KD - 1))
                for k in range(KD):
                    last = nc.tensor.matmul(c.bank[2][0:1, 0:D], b[:, k:k + 1], r[:, k * D:(k + 1) * D],
                                            start=(k == 0), stop=(k == KD - 1))
                last.then_inc(s["product"].sem, 1)

            @block.vector
            def _(v):
                nc.vector.memset(r[:, :], 0.0).then_inc(s["vec"].sem, 1)
                v.wait_ge(s["product"].sem, s["product"].at(1))
                for m, (dst, src) in enumerate([(out_w[:, 0:D], c.bank[0][:, 0:D]), (out_w[:, D:2 * D], c.bank[1][:, 0:D]),
                                                (out_row[:, :], c.bank[2][0:1, 0:D])]):
                    if pri is None:
                        nc.vector.tensor_copy(dst, src).then_inc(s["vec"].sem, 1)
                    else:
                        n = P if m < 2 else 1
                        nc.vector.tensor_tensor(dst.rearrange("p (h e) -> p h e", e=DK), src.rearrange("p (h e) -> p h e", e=DK),
                                                pri[0:n, :].unsqueeze(2).broadcast_to([n, HEADS, DK]), ALU.mult)\
                            .then_inc(s["vec"].sem, 1)
    s["loaded"].passed(16 * n_loads)
    s["product"].passed(1)
    s["vec"].passed(4)


def attention(c, a):
    nc, s = c.nc, c.s
    layernorm(c)
    k_table, v_table = c.dram("k_table", [NP, D], FP32), c.dram("v_table", [NP, D], FP32)
    with ExitStack() as ctx:
        sb = c.scratch(ctx)
        wk, wv = sb("wk", [P, KD * D], FP32), sb("wv", [P, KD * D], FP32)
        wq, wa = sb("wq", [P, KD * D], FP32), sb("wa", [P, KD * D], FP32)
        rk, rv, rq, ra = (sb(f"row_{n}", [1, D], FP32) for n in "kvqa")
        pri, alpha = sb("pri", [P, HEADS], FP32), sb("alpha", [P, 2], FP32)
        maxima = sb("maxima", [P, G * HEADS], FP32)
        zr = sb("zr", [P, G * HEADS], FP32)
        scores = sb("scores", [P, TILES * HEADS], FP32)
        load(c, [(as_k(wq[:, :]), weight_view(a["L1_gnn_Wq"])), (as_k(wa[:, :]), weight_view(a["L1_gnn_Wa"])),
                 (rq[:, :], a["L1_gnn_bq"].unsqueeze(0)), (ra[:, :], a["L1_gnn_ba"].unsqueeze(0)),
                 (pri[:, :], spread(a["L1_gnn_rel_pri"])), (alpha[:, 0:1], a["L1_gnn_skip"].squeeze(0).partition_broadcast(P))])
        with nc.Block() as block:
            @block.scalar
            def _(act):
                nc.scalar.activation(alpha[:, 0:1], alpha[:, 0:1], ACT.Sigmoid).then_inc(s["act"].sem, 1)

            @block.vector
            def _(v):
                nc.vector.tensor_scalar(pri[:, :], pri[:, :], DK ** -0.5, None, ALU.mult).then_inc(s["vec"].sem, 1)
                v.wait_ge(s["act"].sem, s["act"].at(1))
                nc.vector.tensor_scalar(alpha[:, 1:2], alpha[:, 0:1], -1.0, 1.0, ALU.mult, ALU.add).then_inc(s["vec"].sem, 1)
        s["act"].passed(1)
        s["vec"].passed(2)
        fold(c, a["L1_gnn_Wk"], a["L1_gnn_bk"], a["L1_gnn_rel_att"], wk, rk, pri)
        fold(c, a["L1_gnn_Wv"], a["L1_gnn_bv"], a["L1_gnn_rel_msg"], wv, rv)

        def plain(g, out):
            return nc.vector.tensor_copy(out, c.rows(c.T, g))
        project(c, [plain], [([wk], rk[:, :], ("dram", k_table)), ([wv], rv[:, :], ("dram", v_table)),
                             ([wq], rq[:, :], ("sbuf", lambda g: c.rows(c.B2, g)))])
        edge_scores(c, k_table, scores[:, :])
        score_maxima(c, scores[:, :], maxima)
        attend(c, v_table, scores[:, :], maxima)
        acc3 = c.ACC[:, :].rearrange("p (g a) -> p g a", a=AW)
        with nc.Block() as block:
            @block.vector
            def _(v):
                ch = Chain(v, s["vec"])
                z = zr[:, :].rearrange("p (g h) -> p g h", h=HEADS)
                ch.link(nc.vector.tensor_scalar(z, acc3[:, :, D:AW], 1e-30, None, ALU.max))
                ch.link(nc.vector.reciprocal(zr[:, :], zr[:, :]))
        s["vec"].passed(2)

        def shares(g, out):
            return nc.vector.tensor_tensor(out.rearrange("p (h e) -> p h e", e=DK),
                                           c.rows(c.ACC, g, D, AW).rearrange("p (h e) -> p h e", e=DK),
                                           c.rows(zr, g, HEADS).unsqueeze(2).broadcast_to([P, HEADS, DK]), ALU.mult)

        def mix(ch, g, product):
            x = c.rows(c.X, g)
            ch.link(nc.vector.scalar_tensor_tensor(x, product, alpha[:, 0:1], x, ALU.mult, ALU.add))
            ch.link(nc.vector.scalar_tensor_tensor(x, c.rows(c.T, g), alpha[:, 1:2], x, ALU.mult, ALU.add))
        project(c, [shares], [([wa], ra[:, :], ("vec", mix))], post_steps=2)


def softmax_rows(v, nc, ch, s, act_count, x, rows, width, small):
    top = small[:, 0:rows]
    x3 = x.rearrange("p (g e) -> p g e", e=width)

    def wide(col):
        return col.unsqueeze(2).broadcast_to([P, rows, width])
    ch.link(nc.vector.tensor_reduce(top, x3, AX.X, ALU.max))
    ch.link(nc.vector.tensor_tensor(x3, x3, wide(top), ALU.subtract))
    v.sem_inc(s["stats_ready"].sem, 1)
    v.wait_ge(s["exps_ready"].sem, s["exps_ready"].at(act_count))
    ch.link(nc.vector.tensor_reduce(top, x3, AX.X, ALU.add))
    ch.link(nc.vector.reciprocal(top, top))
    ch.link(nc.vector.tensor_tensor(x3, x3, wide(top), ALU.mult))


def moe_top_one(c, a):
    nc, s = c.nc, c.s
    layernorm(c, turn=True)
    width, ne = 1024, 8
    nf = width // P
    chunks = G // CH
    xt = c.B2[:, 0:KD * NP].rearrange("p (k n) -> p k n", k=KD)
    with ExitStack() as ctx:
        sb = c.scratch(ctx)
        w1, b1 = sb("w1", [P, KD * width], FP32), sb("b1", [P, nf], FP32)
        wg, bg = sb("wg", [P, nf * ne], FP32), sb("bg", [1, ne], FP32)
        wd = sb("wd", [P, 2 * nf * D], FP32)
        bd = sb("bd", [P, ne * D], FP32)
        hid = sb("hid", [P, nf * TOK], FP32)
        probs, small = sb("probs", [P, CH * ne], FP32), sb("small", [P, 8], FP32)
        best, where = sb("best", [P, CH * 8], FP32), sb("where", [P, CH * 8], U32)
        where_f, gates = sb("where_f", [P, CH * 8], FP32), sb("gates", [P, CH * ne], FP32)
        tmp = sb("tmp", [P, 2 * D], FP32)
        acc3 = c.ACC[:, :].rearrange("p (g a) -> p g a", a=AW)
        load(c, [(w1[:, :].rearrange("p (k f) -> p k f", k=KD), weight_view(a["L1_ffn_W1"])),
                 (b1[:, :], a["L1_ffn_b1"].rearrange("(f p) -> p f", p=P)),
                 (wg[:, :].rearrange("p (k f) -> p k f", k=nf), weight_view(a["L1_ffn_Wg"])),
                 (bg[:, :], a["L1_ffn_bg"].unsqueeze(0)),
                 (bd[:, :], a["L1_ffn_bd"].rearrange("e d -> (e d)").partition_broadcast(P))])
        wdown = a["L1_ffn_Wd"]

        with nc.Block() as block:
            @block.sync
            def _(sp):
                def body(i, first):
                    for e in range(ne):
                        if not (first and e < 2):
                            sp.wait_ge(s["weights_used"].sem, s["weights_used"].at(i * ne + e - 1))
                        sig = s["wa"] if e % 2 == 0 else s["wb"]
                        sp.dma_start(wd[:, (e % 2) * nf * D:(e % 2 + 1) * nf * D].rearrange("p (k f) -> p k f", k=nf),
                                     wdown[e, :, :].rearrange("(k p) f -> p k f", p=P)).then_inc(sig.sem, 16)
                body(0, True)
                with sp.Fori(1, chunks) as i:
                    body(i, False)

            @block.tensor
            def _(pe):
                with pe.Fori(0, chunks) as i:
                    for f in range(nf):
                        for half in range(2):
                            n = f * 2 + half
                            pe.wait_ge(s["hidden_out"].sem, s["hidden_out"].at(i * (2 * nf) + n - 3))
                            for k in range(KD):
                                last = nc.tensor.matmul(
                                    c.bank[n % 4][:, 0:HT], w1[:, k * width + f * P:k * width + (f + 1) * P],
                                    xt[:, k, bass.ds(i * TOK + half * HT, HT)], start=(k == 0), stop=(k == KD - 1))
                            last.then_inc(s["hidden"].sem, 1)
                    pe.wait_ge(s["hidden_out"].sem, s["hidden_out"].at((i + 1) * (2 * nf)))
                    for t in range(CH):
                        o = c.bank[6][:, t * ne:(t + 1) * ne]
                        for k in range(nf):
                            nc.tensor.matmul(o, hid[:, k * TOK + t * P:k * TOK + (t + 1) * P], wg[:, k * ne:(k + 1) * ne],
                                             start=(k == 0), stop=False)
                        last = nc.tensor.matmul(o, c.ones[0:1, :], bg[:, :], start=False, stop=True)
                    last.then_inc(s["product"].sem, 1)
                    for e in range(ne):
                        sig = s["wa"] if e % 2 == 0 else s["wb"]
                        pe.wait_ge(sig.sem, sig.at(i * (16 * ne // 2) + 16 * (e // 2 + 1)))
                        for t in range(CH):
                            n = e * CH + t
                            pe.wait_ge(s["outcome_used"].sem, s["outcome_used"].at(i * (ne * CH) + n - 1))
                            for k in range(nf):
                                last = nc.tensor.matmul(c.bank[4 + n % 2][:, 0:D], hid[:, k * TOK + t * P:k * TOK + (t + 1) * P],
                                                        wd[:, ((e % 2) * nf + k) * D:((e % 2) * nf + k + 1) * D],
                                                        start=(k == 0), stop=(k == nf - 1))
                            last.then_inc(s["outcome"].sem, 1)
                        pe.wait_ge(s["outcome"].sem, s["outcome"].at(i * (ne * CH) + (e + 1) * CH))
                        pe.sem_inc(s["weights_used"].sem, 1)

            @block.scalar
            def _(act):
                with act.Fori(0, chunks) as i:
                    act.wait_ge(s["outcome"].sem, s["outcome"].at(i * (ne * CH)))
                    for f in range(nf):
                        for half in range(2):
                            n = f * 2 + half
                            act.wait_ge(s["hidden"].sem, s["hidden"].at(i * (2 * nf) + n + 1))
                            nc.scalar.activation(hid[:, f * TOK + half * HT:f * TOK + (half + 1) * HT],
                                                 c.bank[n % 4][:, 0:HT], ACT.Gelu, bias=b1[:, f:f + 1])\
                                .then_inc(s["hidden_out"].sem, 1)
                    act.wait_ge(s["stats_ready"].sem, s["stats_ready"].at(i + 1))
                    nc.scalar.activation(probs[:, :], probs[:, :], ACT.Exp).then_inc(s["exps_ready"].sem, 1)

            @block.vector
            def _(v):
                nc.vector.memset(c.ACC[:, :], 0.0).then_inc(s["act_go"].sem, 1)
                v.wait_ge(s["act_go"].sem, s["act_go"].at(1))
                PER = 6 + 2 * CH + 3 + ne * CH
                with v.Fori(0, chunks) as i:
                    ch = Chain(v, s["vec"], i * PER)
                    v.wait_ge(s["product"].sem, s["product"].at(i + 1))
                    ch.link(nc.vector.tensor_copy(probs[:, :], c.bank[6][:, 0:CH * ne]))
                    softmax_rows(v, nc, ch, s, i + 1, probs[:, :], CH, ne, small)
                    for t in range(CH):
                        row = probs[:, t * ne:(t + 1) * ne]
                        v.sem_inc(s["vec_go"].sem, 1)
                        ch.link(nc.vector.max(best[:, t * 8:(t + 1) * 8], row))
                        v.sem_inc(s["vec_go"].sem, 1)
                        ch.link(nc.vector.max_index(where[:, t * 8:(t + 1) * 8], best[:, t * 8:(t + 1) * 8], row))
                    ch.link(nc.vector.tensor_copy(where_f[:, :], where[:, :]))
                    g3 = gates[:, :].rearrange("p (g e) -> p g e", e=ne)
                    w3 = where_f[:, :].rearrange("p (g e) -> p g e", e=8)
                    ch.link(nc.vector.tensor_tensor(g3, c.iota[:, 0:ne].unsqueeze(1).broadcast_to([P, CH, ne]),
                                                    w3[:, :, 0].unsqueeze(2).broadcast_to([P, CH, ne]), ALU.is_equal))
                    ch.link(nc.vector.tensor_tensor(gates[:, :], gates[:, :], probs[:, :], ALU.mult))
                    for e in range(ne):
                        for t in range(CH):
                            n = e * CH + t
                            part = tmp[:, (n % 2) * D:(n % 2 + 1) * D]
                            v.wait_ge(s["outcome"].sem, s["outcome"].at(i * (ne * CH) + n + 1))
                            nc.vector.tensor_tensor(part, c.bank[4 + n % 2][:, 0:D], bd[:, e * D:(e + 1) * D], ALU.add)\
                                .then_inc(s["outcome_used"].sem, 1)
                            v.wait_ge(s["outcome_used"].sem, s["outcome_used"].at(i * (ne * CH) + n + 1))
                            acc = c.ACC[:, bass.ds(i * (CH * AW) + t * AW, D)]
                            ch.link(nc.vector.scalar_tensor_tensor(acc, part, gates[:, t * ne + e:t * ne + e + 1], acc,
                                                                   ALU.mult, ALU.add))
                c.vec_steps = PER * chunks
        s["vec"].passed(c.vec_steps)
        s["act_go"].passed(1)
        for n in ("wa", "wb"):
            s[n].passed(chunks * 16 * ne // 2)
        s["weights_used"].passed(chunks * ne)
        s["hidden"].passed(chunks * 2 * nf)
        s["hidden_out"].passed(chunks * 2 * nf)
        s["outcome"].passed(chunks * ne * CH)
        s["outcome_used"].passed(chunks * ne * CH)
        for n in ("product", "stats_ready", "exps_ready"):
            s[n].passed(chunks)
    add_rows(c, c.ACC, AW)


def weighted_graph(c, a):
    layernorm(c)
    table = c.dram("w_table", [NP, D], FP32)
    with ExitStack() as ctx:
        sb = c.scratch(ctx)
        w, bias = sb("w", [P, KD * D], FP32), sb("bias", [P, D], FP32)

        def plain(g, out):
            return c.nc.vector.tensor_copy(out, c.rows(c.T, g))
        project(c, [plain], [([w], None, ("dram", table))],
                loads=[(as_k(w[:, :]), weight_view(a["L2_gnn_W"])), (bias[:, :], spread(a["L2_gnn_b"]))])
        aggregate(c, table, "src", weighted=True)
        add_rows(c, c.ACC, AW, bias)


def token_sums(c, pe, buf, step, out, ready=None):
    nc = c.nc
    nc.tensor.matmul(out, c.zeros[:, 0:P], c.zeros[:, 0:D], start=True, stop=False)
    with pe.Fori(0, G - 1) as g:
        if ready is not None:
            ready(g)
        nc.tensor.matmul(out, c.ones[:, :], c.rows(buf, g, D, step), start=False, stop=False)
    if ready is not None:
        ready(G - 1)
    return nc.tensor.matmul(out, c.ones_last[:, :], buf[:, (G - 1) * step:(G - 1) * step + D], start=False, stop=True)


def moe_graph_gate(c, a):
    nc, s = c.nc, c.s
    layernorm(c, turn=True)
    ne, width = 8, 512
    nf = width // P
    capacity = float(-(-int(N * 1.25 * 1000) // (ne * 1000)))
    with ExitStack() as ctx:
        sb = c.scratch(ctx)
        mean, mean_t = sb("mean_row", [P, D], FP32), sb("mean_t", [P, D], FP32)
        wr, br = sb("wr", [P, KD * ne], FP32), sb("br", [1, ne], FP32)
        r, t8, small = sb("r", [P, ne], FP32), sb("t8", [P, ne], FP32), sb("small", [P, 8], FP32)
        best, where, share = sb("best", [P, 8], FP32), sb("where", [P, 8], U32), sb("share", [P, 2], FP32)
        number = sb("number", [1, 8], I32)
        b1 = sb("b1", [P, 2 * nf], FP32)
        gamma, beta = sb("gamma", [P, D], FP32), sb("beta", [P, D], FP32)
        load(c, [(wr[:, :].rearrange("p (k f) -> p k f", k=KD), weight_view(a["L2_ffn_Wr"])),
                 (br[:, :], a["L2_ffn_br"].unsqueeze(0)),
                 (gamma[:, :], spread(a["L2_ffn_gamma"])), (beta[:, :], spread(a["L2_ffn_beta"]))])
        with nc.Block() as block:
            @block.tensor
            def _(pe):
                token_sums(c, pe, c.T, D, c.bank[0][:, 0:D]).then_inc(s["product"].sem, 1)
                pe.wait_ge(s["rows_ready"].sem, s["rows_ready"].at(1))
                for k in range(KD):
                    last = nc.tensor.transpose(c.bank[1][:, k * P:(k + 1) * P], mean[:, k * P:(k + 1) * P], c.ident[:, :])
                last.then_inc(s["product"].sem, 1)
                pe.wait_ge(s["rows_ready"].sem, s["rows_ready"].at(2))
                for k in range(KD):
                    nc.tensor.matmul(c.bank[2][:, 0:ne], mean_t[:, k * P:(k + 1) * P], wr[:, k * ne:(k + 1) * ne],
                                     start=(k == 0), stop=False)
                nc.tensor.matmul(c.bank[2][:, 0:ne], c.ones[0:1, :], br[:, :], start=False, stop=True)\
                    .then_inc(s["product"].sem, 1)

            @block.scalar
            def _(act):
                for n, x in enumerate((r, r, share[:, 0:1])):
                    act.wait_ge(s["stats_ready"].sem, s["stats_ready"].at(n + 1))
                    nc.scalar.activation(x[:, :], x[:, :], ACT.Exp).then_inc(s["exps_ready"].sem, 1)

            @block.vector
            def _(v):
                ch = Chain(v, s["vec"])
                v.wait_ge(s["product"].sem, s["product"].at(1))
                nc.vector.tensor_scalar(mean[:, :], c.bank[0][:, 0:D], 1.0 / N, None, ALU.mult).then_inc(s["rows_ready"].sem, 1)
                v.wait_ge(s["product"].sem, s["product"].at(2))
                nc.vector.tensor_copy(mean_t[:, :], c.bank[1][:, 0:D]).then_inc(s["rows_ready"].sem, 1)
                v.wait_ge(s["product"].sem, s["product"].at(3))
                ch.link(nc.vector.tensor_copy(r[:, :], c.bank[2][:, 0:ne]))
                softmax_rows(v, nc, ch, s, 1, r[:, :], 1, ne, small)
                ch.link(nc.vector.tensor_scalar(t8[:, :], r[:, :], float(N), None, ALU.mult))
                ch.link(nc.vector.tensor_scalar(best[:, :], t8[:, :], capacity, None, ALU.is_gt))
                ch.link(nc.vector.tensor_scalar(t8[:, :], t8[:, :], capacity, None, ALU.max))
                ch.link(nc.vector.reciprocal(t8[:, :], t8[:, :]))
                ch.link(nc.vector.tensor_scalar(t8[:, :], t8[:, :], capacity, None, ALU.mult))
                ch.link(nc.vector.tensor_tensor(t8[:, :], t8[:, :], best[:, :], ALU.mult))
                ch.link(nc.vector.tensor_scalar(best[:, :], best[:, :], -1.0, 1.0, ALU.mult, ALU.add))
                ch.link(nc.vector.tensor_tensor(t8[:, :], t8[:, :], best[:, :], ALU.add))
                ch.link(nc.vector.tensor_tensor(r[:, :], r[:, :], t8[:, :], ALU.mult))
                softmax_rows(v, nc, ch, s, 2, r[:, :], 1, ne, small)
                ch.link(nc.vector.max(best[:, :], r[:, :]))
                ch.link(nc.vector.max_index(where[:, :], best[:, :], r[:, :]))
                ch.link(nc.vector.tensor_copy(number[:, :], where[0:1, :]))
                ch.link(nc.vector.tensor_tensor(share[:, 0:1], best[:, 1:2], best[:, 0:1], ALU.subtract))
                v.sem_inc(s["stats_ready"].sem, 1)
                v.wait_ge(s["exps_ready"].sem, s["exps_ready"].at(3))
                ch.link(nc.vector.tensor_scalar(t8[:, 0:1], share[:, 0:1], 1.0, None, ALU.add))
                ch.link(nc.vector.reciprocal(t8[:, 0:1], t8[:, 0:1]))
                ch.link(nc.vector.tensor_tensor(share[:, 1:2], share[:, 0:1], t8[:, 0:1], ALU.mult))
                ch.link(nc.vector.tensor_copy(share[:, 0:1], t8[:, 0:1]))
                c.vec_steps = ch.n
        s["vec"].passed(c.vec_steps)
        s["product"].passed(3)
        s["rows_ready"].passed(2)
        s["stats_ready"].passed(3)
        s["exps_ready"].passed(3)

        w1, w2, b2, b1_d = (a[f"L2_ffn_{n}"] for n in ("W1", "W2", "b2", "b1"))
        with nc.Block() as block:
            @block.sync
            def _(sp):
                for n in range(2):
                    e = sp.value_load(number[0:1, n:n + 1], min_val=0, max_val=ne - 1)
                    src = b1_d[bass.ds(e, 1), :].rearrange("e (f p) -> p (e f)", p=P)
                    sp.dma_start(b1[:, n * nf:(n + 1) * nf], src, allow_slow_non_contiguous=True).then_inc(s["loaded"].sem, 16)
                sp.wait_ge(s["loaded"].sem, s["loaded"].at(32))
        s["loaded"].passed(32)

        def chosen(sp, n):
            return sp.value_load(number[0:1, n:n + 1], min_val=0, max_val=ne - 1)
        experts(c, 2, width,
                Expert(lambda sp, n: at_expert(w1, chosen(sp, n)), lambda sp, n: at_expert(w2, chosen(sp, n)),
                       lambda sp, n: row_spread(b2, chosen(sp, n))),
                ACT.Gelu, (1.0, b1), lambda tile, n: share[:, n:n + 1])
        add_normed(c, gamma, beta)


def batchnorm_relu(c, gamma, beta, eps=1e-5):
    nc, s = c.nc, c.s
    with ExitStack() as ctx:
        sb = c.scratch(ctx)
        mean, scale = sb("bn_mean", [P, D], FP32), sb("bn_scale", [P, D], FP32)
        squares = sb("bn_squares", [P, 2 * D], FP32)
        with nc.Block() as block:
            @block.tensor
            def _(pe):
                token_sums(c, pe, c.ACC, AW, c.bank[0][:, 0:D]).then_inc(s["product"].sem, 1)
                o = c.bank[1][:, 0:D]

                def add(g, b):
                    pe.wait_ge(s["turned_out"].sem, s["turned_out"].at(g + 1))
                    nc.tensor.matmul(o, c.ones[:, :], squares[:, b * D:(b + 1) * D], start=False, stop=False)\
                        .then_inc(s["turned"].sem, 1)
                nc.tensor.matmul(o, c.zeros[:, 0:P], c.zeros[:, 0:D], start=True, stop=False)
                with pe.Fori(0, (G - 1) // 2) as i:
                    for b in range(2):
                        add(i * 2 + b, b)
                pe.wait_ge(s["turned_out"].sem, s["turned_out"].at(G))
                nc.tensor.matmul(o, c.ones_last[:, :], squares[:, 0:D], start=False, stop=True).then_inc(s["product"].sem, 1)

            @block.scalar
            def _(act):
                def square(g, b):
                    act.wait_ge(s["rows_ready"].sem, s["rows_ready"].at(g + 1))
                    act.wait_ge(s["turned"].sem, s["turned"].at(g - 1))
                    act.sem_inc(s["act_go"].sem, 1)
                    nc.scalar.activation(squares[:, b * D:(b + 1) * D], c.rows(c.ACC, g, D, AW), ACT.Square)\
                        .then_inc(s["turned_out"].sem, 1)
                per_tile(act, square, lambda g, b: None)
                act.wait_ge(s["stats_ready"].sem, s["stats_ready"].at(1))
                nc.scalar.activation(scale[:, :], scale[:, :], ACT.Sqrt).then_inc(s["act"].sem, 1)

            @block.vector
            def _(v):
                ch = Chain(v, s["vec"])
                v.wait_ge(s["product"].sem, s["product"].at(1))
                ch.link(nc.vector.tensor_scalar(mean[:, :], c.bank[0][:, 0:D], 1.0 / N, None, ALU.mult))
                with v.Fori(0, G) as g:
                    h = c.rows(c.ACC, g, D, AW)
                    nc.vector.tensor_tensor(h, h, mean[:, :], ALU.subtract).then_inc(s["rows_ready"].sem, 1)
                v.wait_ge(s["product"].sem, s["product"].at(2))
                ch.link(nc.vector.tensor_scalar(scale[:, :], c.bank[1][:, 0:D], 1.0 / N, eps, ALU.mult, ALU.add))
                v.sem_inc(s["stats_ready"].sem, 1)
                v.wait_ge(s["act"].sem, s["act"].at(1))
                ch.link(nc.vector.reciprocal(scale[:, :], scale[:, :]))
                ch.link(nc.vector.tensor_tensor(scale[:, :], scale[:, :], gamma, ALU.mult))
                with v.Fori(0, G) as g:
                    ch = Chain(v, s["vec"], g * 3 + 4)
                    h, t = c.rows(c.ACC, g, D, AW), c.rows(c.T, g)
                    ch.link(nc.vector.tensor_tensor(t, h, scale[:, :], ALU.mult))
                    ch.link(nc.vector.tensor_tensor(t, t, beta, ALU.add))
                    ch.link(nc.vector.tensor_scalar(t, t, 0.0, None, ALU.max))
    s["product"].passed(2)
    s["act_go"].passed(G)
    s["act"].passed(1)
    s["stats_ready"].passed(1)
    s["rows_ready"].passed(G)
    s["turned_out"].passed(G)
    s["turned"].passed(G - 1)
    s["vec"].passed(3 * G + 4)


def sage(c, a):
    nc, s = c.nc, c.s
    layernorm(c)
    table = c.dram("sage_table", [NP, D], FP32)
    with ExitStack() as ctx:
        sb = c.scratch(ctx)
        wl, wr, bl = sb("wl", [P, KD * D], FP32), sb("wr", [P, KD * D], FP32), sb("bl", [1, D], FP32)
        gamma, beta = sb("gamma", [P, D], FP32), sb("beta", [P, D], FP32)
        for layer in range(3):
            load(c, [(table.rearrange("(g p) d -> p g d", p=P), c.T[:, :].rearrange("p (g d) -> p g d", d=D)),
                     (as_k(wl[:, :]), weight_view(a["L3_gnn_Wl"][layer, :, :])),
                     (as_k(wr[:, :]), weight_view(a["L3_gnn_Wr"][layer, :, :])),
                     (bl[:, :], a["L3_gnn_bl"][layer:layer + 1, :]),
                     (gamma[:, :], a["L3_gnn_gamma"][layer, :].partition_broadcast(P)),
                     (beta[:, :], a["L3_gnn_beta"][layer, :].partition_broadcast(P))])
            aggregate(c, table, "dst")

            def mean_rows(g, out):
                return nc.vector.tensor_scalar(out, c.rows(c.ACC, g, D, AW), c.rdeg[:, bass.ds(g, 1)], None, ALU.mult)

            def own_rows(g, out):
                return nc.vector.tensor_copy(out, c.rows(c.T, g))
            project(c, [mean_rows, own_rows], [([wl, wr], bl[:, :], ("sbuf", lambda g: c.rows(c.ACC, g, D, AW)))])
            batchnorm_relu(c, gamma[:, :], beta[:, :])
    add_rows(c, c.T, D)


def deep_experts(c, a):
    nc, s = c.nc, c.s
    layernorm(c, turn=True)
    ne, width, eps = 8, 256, 1e-3
    nf = width // P
    with ExitStack() as ctx:
        sb = c.scratch(ctx)
        gates, small = sb("gates", [P, G * ne], FP32), sb("small", [P, G], FP32)
        names = [f"{n}{m}" for m in (1, 2) for n in ("g", "be", "m", "v", "b")]
        t = {n: sb(f"bn_{n}", [P, ne * nf], FP32) for n in names}
        load(c, [(t[n][:, :], columns(a[f"L3_ffn_{n}"])) for n in names])
        gate_logits(c, a["L3_ffn_Wr"], a["L3_ffn_br"].unsqueeze(0), ne, gates)
        with nc.Block() as block:
            @block.scalar
            def _(act):
                for m in (1, 2):
                    act.wait_ge(s["rows_ready"].sem, s["rows_ready"].at(m))
                    nc.scalar.activation(t[f"v{m}"][:, :], t[f"v{m}"][:, :], ACT.Sqrt).then_inc(s["act"].sem, 1)
                act.wait_ge(s["stats_ready"].sem, s["stats_ready"].at(1))
                nc.scalar.activation(gates[:, :], gates[:, :], ACT.Exp).then_inc(s["exps_ready"].sem, 1)

            @block.vector
            def _(v):
                ch = Chain(v, s["vec"])
                for m in (1, 2):
                    g, be, mu, var, b = (t[f"{n}{m}"][:, :] for n in ("g", "be", "m", "v", "b"))
                    ch.link(nc.vector.tensor_scalar(var, var, eps, None, ALU.add))
                    v.sem_inc(s["rows_ready"].sem, 1)
                    v.wait_ge(s["act"].sem, s["act"].at(m))
                    ch.link(nc.vector.reciprocal(var, var))
                    ch.link(nc.vector.tensor_tensor(var, var, g, ALU.mult))
                    ch.link(nc.vector.tensor_tensor(b, b, mu, ALU.subtract))
                    ch.link(nc.vector.tensor_tensor(b, b, var, ALU.mult))
                    ch.link(nc.vector.tensor_tensor(b, b, be, ALU.add))
                softmax_rows(v, nc, ch, s, 1, gates[:, :], G, ne, small)
                c.vec_steps = ch.n
        s["vec"].passed(c.vec_steps)
        s["rows_ready"].passed(2)
        s["act"].passed(2)
        s["stats_ready"].passed(1)
        s["exps_ready"].passed(1)
        w1, w2, wo, bo = (a[f"L3_ffn_{n}"] for n in ("W1", "W2", "Wo", "bo"))
        experts(c, ne, width,
                Expert(lambda sp, e: at_expert(w1, e), lambda sp, e: at_expert(wo, e), lambda sp, e: row_spread(bo, e),
                       lambda sp, e: at_expert(w2, e)),
                ACT.Relu, (t["v1"], t["b1"]), lambda tile, e: gates[:, bass.ds(e + tile * ne, 1)],
                ACT.Relu, (t["v2"], t["b2"]))
    add_rows(c, c.ACC, AW)


def finish(c, out):
    nc, s = c.nc, c.s
    with nc.Block() as block:
        @block.sync
        def _(sp):
            full = out[0:(G - 1) * P, :].rearrange("(g p) d -> p g d", p=P)
            sp.dma_start(full, c.X[:, 0:(G - 1) * D].rearrange("p (g d) -> p g d", d=D)).then_inc(s["stored"].sem, 16)
            sp.dma_start(out[(G - 1) * P:N, :], c.X[0:LAST, (G - 1) * D:G * D]).then_inc(s["stored"].sem, 16)
            sp.wait_ge(s["stored"].sem, s["stored"].at(32))


def build(nc, a, out):
    with ExitStack() as ctx:
        def dram(name, shape, dt):
            return nc.dram_tensor(name, shape, dt, kind="Internal").ap()
        c = Core(ctx, nc, dram)
        setup(c, a["x"])
        bucket(c, "dst", a["dst"], a["src"], a["edge_weight"], degrees=True)
        bucket(c, "src", a["src"], a["dst"], a["edge_weight"], degrees=False)
        gcn(c, a)
        moe_relu(c, a)
        attention(c, a)
        moe_top_one(c, a)
        weighted_graph(c, a)
        moe_graph_gate(c, a)
        sage(c, a)
        deep_experts(c, a)
        finish(c, out)


def kernel(**inputs):
    import numpy as _np
    import concourse.bacc as _bacc
    from concourse import mybir as _mybir
    from concourse.bass_utils import run_bass_kernel_spmd as _run

    nc = _bacc.Bacc("TRN2", target_bir_lowering=False, num_devices=1)
    arrays, args = {}, {}
    for name in inputs:
        a = _np.ascontiguousarray(inputs[name])
        if name == "L1_gnn_skip":
            a = a.reshape(1, 1)
        if name in ("L1_gnn_Wq", "L1_gnn_Wa"):
            a = _np.ascontiguousarray(a.T)
        arrays[f"in_{name}"] = a
        args[name] = nc.dram_tensor(f"in_{name}", a.shape, _mybir.dt.from_np(a.dtype), kind="ExternalInput").ap()
    out = nc.dram_tensor("out_0", (3125, 256), _mybir.dt.float32, kind="ExternalOutput").ap()
    build(nc, args, out)
    r = _run(nc, [arrays], core_ids=[0])
    return r.results[0]["out_0"]
```

```python
import concourse.bass as bass
from concourse import mybir
from contextlib import ExitStack

FP32 = mybir.dt.float32
BF16 = mybir.dt.bfloat16
I32 = mybir.dt.int32
U32 = mybir.dt.uint32
ALU = mybir.AluOpType
ACT = mybir.ActivationFunctionType
AX = mybir.AxisListType.X

N, D, E = 3125, 256, 50000
P = 128
G = -(-N // P)
NP = G * P
LAST = N - (G - 1) * P
KD = D // P
EP = 125
EC = E // EP
HALF = 8
TILES = -(-(E // P + G) // (2 * HALF)) * 2 * HALF
HEADS, DK = 8, 32
AW = D + HEADS
CREDIT = 64
CH = 5
TOK = CH * P
HT = TOK // 2
BIG = 2.0 ** 100
ROUND = 6


class Signal:

    def __init__(self, ctx, nc, name, credit=CREDIT):
        self.sem = ctx.enter_context(nc.semaphore(name))
        self.base = credit

    def at(self, n):
        return n + self.base

    def passed(self, n):
        self.base += n


class Chain:

    def __init__(self, eng, signal, start=0):
        self.eng, self.steps, self.n = eng, signal, start

    def link(self, ins):
        self.n = self.n + 1
        ins.then_inc(self.steps.sem, 1)
        self.eng.wait_ge(self.steps.sem, self.steps.at(self.n))


def per_tile(eng, lead, follow):
    lead(0, 0)
    with eng.Fori(0, (G - 1) // 2) as i:
        for s in range(2):
            g = i * 2 + s
            lead(g + 1, 1 - s)
            follow(g, s)
    follow(G - 1, 0)


class Core:

    def __init__(self, ctx, nc, dram):
        self.ctx, self.nc, self.dram = ctx, nc, dram
        sb = self.sb
        self.stage = 0
        self.X = sb("X", [P, G * D], FP32)
        self.T = sb("T", [P, G * D], FP32)
        self.ACC = sb("ACC", [P, G * AW], FP32)
        self.B2 = sb("B2", [P, KD * NP], FP32)
        self.iota = sb("iota", [P, 512], FP32)
        self.iota_i = sb("iota_i", [P, 512], I32)
        self.ident = sb("ident", [P, P], FP32)
        self.earlier = sb("earlier", [P, P], FP32)
        self.ones = sb("ones", [P, P], FP32)
        self.ones_last = sb("ones_last", [P, P], FP32)
        self.zeros = sb("zeros", [P, 512], FP32)
        self.rec = {k: sb(f"rec_{k}", [P, TILES * 4], FP32) for k in ("dst", "src")}
        self.group = {k: sb(f"group_{k}", [1, TILES], I32) for k in ("dst", "src")}
        self.indeg = sb("indeg", [P, G], FP32)
        self.dinv = sb("dinv", [P, G], FP32)
        self.rdeg = sb("rdeg", [P, G], FP32)
        self.stat_pair = sb("stat_pair", [P, 2 * G], FP32)
        self.mean = sb("mean", [P, G], FP32)
        self.rstd = sb("rstd", [P, G], FP32)
        self.bank = [ctx.enter_context(nc.psum_tensor(f"bank{i}", [P, 512], FP32)) for i in range(8)]
        names = """act_go vec_go loaded stored const_ready vec act pool ring_staged pool_go gather_free onehot_ready summed
            rows_ready turned turned_out product product_out stats_ready table_written hidden hidden_out outcome
            outcome_used weights_used slot_ready hot_ready hot_used mask_ready turned2 turned2_out score_ready
            exps_ready gates_ready slots_staged scattered fetched wa wb wc wd""".split()
        self.s = {n: Signal(ctx, nc, n) for n in names}
        self.arrived = [Signal(ctx, nc, f"arrived{j}", 0) for j in range(2 * HALF)]
        self.written = [Signal(ctx, nc, f"written{b}") for b in range(2)]
        self.all_counts = [*self.s.values(), *self.written]

    def sb(self, name, shape, dt):
        return self.ctx.enter_context(self.nc.sbuf_tensor(name, shape, dt))

    def scratch(self, ctx):
        self.stage += 1
        stage = self.stage
        return lambda name, shape, dt: ctx.enter_context(self.nc.sbuf_tensor(f"{name}_{stage}", shape, dt))

    def rows(self, buf, g, width=D, step=None):
        return buf[:, bass.ds(g * (step or width), width)]


def setup(c, x):
    nc, s = c.nc, c.s
    with nc.Block() as block:
        @block.sync
        def _(sp):
            for sig in c.all_counts:
                sp.sem_inc(sig.sem, CREDIT)
            sp.wait_ge(s["const_ready"].sem, s["const_ready"].at(7))
            full = x[0:(G - 1) * P, :].rearrange("(g p) d -> p g d", p=P)
            sp.dma_start(c.X[:, 0:(G - 1) * D].rearrange("p (g d) -> p g d", d=D), full).then_inc(s["loaded"].sem, 16)
            sp.dma_start(c.X[0:LAST, (G - 1) * D:G * D], x[(G - 1) * P:N, :]).then_inc(s["loaded"].sem, 16)
            sp.wait_ge(s["loaded"].sem, s["loaded"].at(32))

        @block.gpsimd
        def _(pool):
            pool.wait_ge(s["const_ready"].sem, CREDIT)
            ready = s["const_ready"].sem
            nc.gpsimd.memset(c.ident[:, :], 0.0).then_inc(ready, 1)
            nc.gpsimd.memset(c.earlier[:, :], 1.0).then_inc(ready, 1)
            nc.gpsimd.memset(c.ones[:, :], 1.0).then_inc(ready, 1)
            nc.gpsimd.memset(c.ones_last[:, :], 1.0).then_inc(ready, 1)
            nc.gpsimd.memset(c.zeros[:, :], 0.0).then_inc(ready, 1)
            nc.gpsimd.iota(c.iota_i[:, :], [[1, 512]], base=0, channel_multiplier=0).then_inc(ready, 1)
            nc.gpsimd.memset(c.X[:, (G - 1) * D:G * D], 0.0).then_inc(ready, 1)
            pool.wait_ge(ready, s["const_ready"].at(7))
            nc.gpsimd.affine_select(out=c.ident[:, :], in_=c.ident[:, :], compare_op=ALU.not_equal, fill=1.0,
                                    base=0, pattern=[[-1, P]], channel_multiplier=1).then_inc(ready, 1)
            nc.gpsimd.affine_select(out=c.earlier[:, :], in_=c.earlier[:, :], compare_op=ALU.is_ge, fill=0.0,
                                    base=-1, pattern=[[1, P]], channel_multiplier=-1).then_inc(ready, 1)
            nc.gpsimd.affine_select(out=c.ones_last[:, :], in_=c.ones_last[:, :], compare_op=ALU.is_ge, fill=0.0,
                                    base=LAST - 1, pattern=[[0, P]], channel_multiplier=-1).then_inc(ready, 1)

        @block.vector
        def _(v):
            v.wait_ge(s["const_ready"].sem, s["const_ready"].at(10))
            nc.vector.tensor_copy(c.iota[:, :], c.iota_i[:, :]).then_inc(s["vec"].sem, 1)
    s["const_ready"].passed(10)
    s["loaded"].passed(32)
    s["vec"].passed(1)


class Scatter:

    def __init__(self, c, key, sb):
        self.key = key
        self.dram = c.dram(f"rec_dram_{key}", [P * TILES, 4], FP32)
        self.slot = sb("slot", [EP, EC], I32)
        self.records = sb("out_rec", [EP, EC * 4], FP32)
        self.slot_ring = sb("slot_ring", [EP, 2 * HALF], I32)
        self.rec_ring = sb("rec_ring", [EP, 2 * HALF * 4], FP32)

    def run(self, c, pool):
        nc, s = c.nc, c.s

        def scatter(i, h, first=False):
            if not first:
                for j in range(HALF):
                    sig = c.arrived[h * HALF + j]
                    pool.wait_ge(sig.sem, sig.at(i * 16))
                pool.sem_inc(s["pool_go"].sem, 1)
            t = i * (2 * HALF) + h * HALF
            nc.gpsimd.tensor_copy(self.slot_ring[:, h * HALF:(h + 1) * HALF], self.slot[:, bass.ds(t, HALF)])\
                .then_inc(s["slots_staged"].sem, 1)
            nc.gpsimd.tensor_copy(self.rec_ring[:, h * HALF * 4:(h + 1) * HALF * 4],
                                  self.records[:, bass.ds(t * 4, HALF * 4)]).then_inc(s["slots_staged"].sem, 1)
            pool.wait_ge(s["slots_staged"].sem, s["slots_staged"].at(i * 4 + (h + 1) * 2))
            pool.sem_inc(s["pool_go"].sem, 1)
            for j in range(h * HALF, (h + 1) * HALF):
                nc.gpsimd.indirect_dma_start(
                    self.dram[:, :], bass.IndirectOffsetOnAxis(ap=self.slot_ring[:, j:j + 1], axis=0),
                    self.rec_ring[:, j * 4:(j + 1) * 4], None).then_inc(c.arrived[j].sem, 16)

        rounds = EC // (2 * HALF)
        for h in range(2):
            scatter(0, h, True)
        with pool.Fori(1, rounds) as i:
            for h in range(2):
                scatter(i, h)
        for j in range(2 * HALF):
            pool.wait_ge(c.arrived[j].sem, c.arrived[j].at(rounds * 16))
        pool.sem_inc(s["scattered"].sem, 1)

    def fetch(self, c, sp):
        sp.wait_ge(c.s["scattered"].sem, c.s["scattered"].at(1))
        sp.dma_start(c.rec[self.key][:, :], self.dram.rearrange("(p t) c -> p (t c)", p=P)).then_inc(c.s["fetched"].sem, 16)
        sp.wait_ge(c.s["fetched"].sem, c.s["fetched"].at(16))

    def passed(self, c):
        rounds = EC // (2 * HALF)
        c.s["slots_staged"].passed(4 * rounds)
        c.s["pool_go"].passed(4 * rounds - 2)
        c.s["scattered"].passed(1)
        c.s["fetched"].passed(16)
        for sig in c.arrived:
            sig.passed(16 * rounds)


def bucket(c, key, keys, others, weight, degrees, move, now):
    nc, s = c.nc, c.s
    slot, out_rec, rec_dram = move.slot, move.records, move.dram
    with ExitStack() as ctx:
        sb = c.scratch(ctx)
        key_i, other_i = sb("key_i", [EP, EC], I32), sb("other_i", [EP, EC], I32)
        wt = sb("wt", [EP, EC], FP32)
        int_a = sb("int_a", [EP, EC], I32)
        hi, lo = sb("hi", [EP, EC], FP32), sb("lo", [EP, EC], FP32)
        in_bucket = c.B2[0:EP, 0:G * EC // 2].bitcast(BF16)
        prefix = sb("prefix", [EP, G * EC], FP32)
        rank, first, tmp = sb("rank", [EP, EC], FP32), sb("first", [EP, EC], FP32), sb("tmp", [EP, EC], FP32)
        row_total = sb("row_total", [EP, G], FP32)
        row_offset = sb("row_offset", [EP, G], FP32)
        tiles, tiles_i = sb("tiles", [P, G], FP32), sb("tiles_i", [P, G], I32)
        end, start = sb("end", [P, G], FP32), sb("start", [P, G], FP32)
        empty = c.T[:, 0:TILES * 4]
        group_f = sb("group_f", [1, TILES], FP32)
        hot_lo = sb("hot_lo", [EP, 4 * P], BF16)
        zb = sb("zb", [EP, P], BF16)
        out4 = out_rec[:, :].rearrange("p (t c) -> p t c", c=4)
        offs, totals, deg = c.bank[0][0:EP, 0:G], c.bank[1][:, 0:G], c.bank[2][:, 0:G]

        with nc.Block() as block:
            @block.sync
            def _(sp):
                for dst, src in ((key_i, keys), (other_i, others), (wt, weight)):
                    sp.dma_start(dst[:, :], src.rearrange("(p t) -> p t", p=EP)).then_inc(s["loaded"].sem, 16)
                sp.wait_ge(s["pool"].sem, s["pool"].at(2))
                sp.dma_start(rec_dram.rearrange("(p t) c -> p (t c)", p=P), empty[:, :]).then_inc(s["stored"].sem, 16)
                sp.wait_ge(s["stored"].sem, s["stored"].at(16))
                if now:
                    move.fetch(c, sp)

            @block.gpsimd
            def _(pool):
                nc.gpsimd.memset(empty[:, :], 0.0).then_inc(s["pool"].sem, 1)
                pool.wait_ge(s["pool"].sem, s["pool"].at(1))
                nc.gpsimd.memset(empty[:, :].rearrange("p (t c) -> p t c", c=4)[:, :, 1], -1.0).then_inc(s["pool"].sem, 1)
                if now:
                    pool.wait_ge(s["stored"].sem, s["stored"].at(16))
                    pool.wait_ge(s["slot_ready"].sem, s["slot_ready"].at(1))
                    move.run(c, pool)

            @block.tensor
            def _(pe):
                pe.wait_ge(s["rows_ready"].sem, s["rows_ready"].at(1))
                nc.tensor.matmul(offs, c.earlier[0:EP, 0:EP], row_total[:, :], start=True, stop=True)
                nc.tensor.matmul(totals, c.ones[0:EP, :], row_total[:, :], start=True, stop=True).then_inc(s["product"].sem, 1)
                if degrees:
                    oh = in_bucket[:, :].rearrange("p (g t) -> p g t", t=EC)
                    nc.tensor.matmul(deg, zb[:, :], zb[:, 0:G], start=True, stop=False)
                    with pe.Fori(0, EC // 4) as i:
                        for j in range(4):
                            pe.wait_ge(s["onehot_ready"].sem, s["onehot_ready"].at(i * 4 + j + 1))
                            nc.tensor.matmul(deg, hot_lo[:, j * P:(j + 1) * P], oh[:, :, bass.ds(i * 4 + j, 1)],
                                             start=False, stop=False).then_inc(s["summed"].sem, 1)
                    nc.tensor.matmul(deg, zb[:, :], zb[:, 0:G], start=False, stop=True).then_inc(s["product"].sem, 1)

            @block.vector
            def _(v):
                ch = Chain(v, s["vec"])
                v.wait_ge(s["loaded"].sem, s["loaded"].at(48))
                ch.link(nc.vector.tensor_scalar(int_a[:, :], key_i[:, :], 7, None, ALU.logical_shift_right))
                ch.link(nc.vector.tensor_copy(hi[:, :], int_a[:, :]))
                ch.link(nc.vector.tensor_scalar(int_a[:, :], key_i[:, :], P - 1, None, ALU.bitwise_and))
                ch.link(nc.vector.tensor_copy(lo[:, :], int_a[:, :]))
                ch.link(nc.vector.memset(zb[:, :], 0.0))
                ch.link(nc.vector.memset(out_rec[:, :], 0.0))
                ch.link(nc.vector.tensor_copy(out4[:, :, 0].bitcast(I32), other_i[:, :]))
                ch.link(nc.vector.tensor_copy(out4[:, :, 1], lo[:, :]))
                ch.link(nc.vector.tensor_copy(out4[:, :, 2], wt[:, :]))
                ch.link(nc.vector.memset(rank[:, :], 0.0))
                ch.link(nc.vector.memset(first[:, :], 0.0))
                n0 = ch.n
                with v.Fori(0, G) as b:
                    one = Chain(v, s["vec"], b * 2 + n0)
                    ob, pb = c.rows(in_bucket, b, EC), c.rows(prefix, b, EC)
                    one.link(nc.vector.tensor_scalar(ob, hi[:, :], c.iota[0:EP, bass.ds(b, 1)], None, ALU.is_equal))
                    one.link(nc.vector.tensor_tensor_scan(pb, ob, c.zeros[0:EP, 0:EC], 0.0, ALU.add, ALU.add))
                ch.n = n0 + 2 * G
                pr = prefix[:, :].rearrange("p (g t) -> p g t", t=EC)
                ch.link(nc.vector.tensor_copy(row_total[:, :], pr[:, :, EC - 1]))
                v.sem_inc(s["rows_ready"].sem, 1)
                v.wait_ge(s["product"].sem, s["product"].at(1))
                ch.link(nc.vector.tensor_scalar(row_offset[:, :], offs, -1.0, None, ALU.add))
                ch.link(nc.vector.tensor_scalar(tiles_i[:, :], totals, float(P - 1), None, ALU.add))
                ch.link(nc.vector.tensor_scalar(tiles_i[:, :], tiles_i[:, :], 7, None, ALU.logical_shift_right))
                ch.link(nc.vector.tensor_copy(tiles[:, :], tiles_i[:, :]))
                ch.link(nc.vector.tensor_tensor_scan(end[:, :], tiles[:, :], c.zeros[:, 0:G], 0.0, ALU.add, ALU.add))
                ch.link(nc.vector.tensor_tensor(start[:, :], end[:, :], tiles[:, :], ALU.subtract))
                n1 = ch.n
                with v.Fori(0, G) as b:
                    one = Chain(v, s["vec"], b * 3 + n1)
                    ob, pb, col = c.rows(in_bucket, b, EC), c.rows(prefix, b, EC), bass.ds(b, 1)
                    one.link(nc.vector.scalar_tensor_tensor(tmp[:, :], pb, row_offset[:, col], ob, ALU.add, ALU.mult))
                    one.link(nc.vector.tensor_tensor(rank[:, :], rank[:, :], tmp[:, :], ALU.add))
                    one.link(nc.vector.scalar_tensor_tensor(first[:, :], ob, start[0:EP, col], first[:, :], ALU.mult, ALU.add))
                ch.n = n1 + 3 * G
                ch.link(nc.vector.tensor_copy(int_a[:, :], rank[:, :]))
                ch.link(nc.vector.tensor_scalar(slot[:, :], int_a[:, :], P - 1, None, ALU.bitwise_and))
                ch.link(nc.vector.tensor_scalar(int_a[:, :], int_a[:, :], 7, None, ALU.logical_shift_right))
                ch.link(nc.vector.tensor_copy(tmp[:, :], int_a[:, :]))
                ch.link(nc.vector.tensor_tensor(first[:, :], first[:, :], tmp[:, :], ALU.add))
                ch.link(nc.vector.tensor_copy(tmp[:, :], slot[:, :]))
                ch.link(nc.vector.scalar_tensor_tensor(first[:, :], tmp[:, :], float(TILES), first[:, :], ALU.mult, ALU.add))
                ch.link(nc.vector.tensor_copy(slot[:, :], first[:, :]))
                v.sem_inc(s["slot_ready"].sem, 1)
                ch.link(nc.vector.memset(group_f[:, :], 0.0))
                n2 = ch.n
                with v.Fori(0, G) as b:
                    one = Chain(v, s["vec"], b + n2)
                    one.link(nc.vector.scalar_tensor_tensor(group_f[:, :], c.iota[0:1, 0:TILES], end[0:1, bass.ds(b, 1)],
                                                            group_f[:, :], ALU.is_ge, ALU.add))
                ch.n = n2 + G
                ch.link(nc.vector.tensor_scalar(c.group[key][:, :], group_f[:, :], float(G - 1), None, ALU.min))
                if degrees:
                    with v.Fori(0, EC // 4) as i:
                        for j in range(4):
                            v.wait_ge(s["summed"].sem, s["summed"].at(i * 4 + j - 3))
                            nc.vector.tensor_scalar(hot_lo[:, j * P:(j + 1) * P], c.iota[0:EP, 0:P],
                                                    lo[:, bass.ds(i * 4 + j, 1)], None, ALU.is_equal)\
                                .then_inc(s["onehot_ready"].sem, 1)
                    v.wait_ge(s["product"].sem, s["product"].at(2))
                    ch.link(nc.vector.tensor_copy(c.indeg[:, :], deg))
                    ch.link(nc.vector.tensor_scalar(c.rdeg[:, :], c.indeg[:, :], 1.0, None, ALU.max))
                    ch.link(nc.vector.reciprocal(c.rdeg[:, :], c.rdeg[:, :]))
                    ch.link(nc.vector.tensor_scalar(c.dinv[:, :], c.indeg[:, :], 1.0, None, ALU.add))
                    v.sem_inc(s["stats_ready"].sem, 1)
                    v.wait_ge(s["act"].sem, s["act"].at(1))
                    ch.link(nc.vector.reciprocal(c.dinv[:, :], c.dinv[:, :]))
                c.vec_steps = ch.n

            @block.scalar
            def _(act):
                if degrees:
                    act.wait_ge(s["stats_ready"].sem, s["stats_ready"].at(1))
                    nc.scalar.activation(c.dinv[:, :], c.dinv[:, :], ACT.Sqrt).then_inc(s["act"].sem, 1)
    s["loaded"].passed(48)
    s["stored"].passed(16)
    s["pool"].passed(2)
    if now:
        move.passed(c)
    s["rows_ready"].passed(1)
    s["slot_ready"].passed(1)
    s["vec"].passed(c.vec_steps)
    s["product"].passed(1)
    if degrees:
        s["product"].passed(1)
        s["onehot_ready"].passed(EC)
        s["summed"].passed(EC)
        s["stats_ready"].passed(1)
        s["act"].passed(1)


def row_stats(c, v, stats, agg, source, start, prepare=None):
    nc, s = c.nc, c.s
    steps = 4 if prepare else 3
    pair = c.stat_pair[:, :]
    with v.Fori(0, G // CH) as i:
        base = i * steps + start

        def together(n, last):
            last.then_inc(s["vec"].sem, 1)
            v.wait_ge(s["vec"].sem, s["vec"].at(base + n))
            v.sem_inc(s["vec_go"].sem, 1)
        if prepare:
            for t in range(CH):
                last = prepare(i * CH + t)
            together(1, last)
        for t in range(CH):
            last = nc.vector.bn_stats(stats[:, t * 6:(t + 1) * 6], source(i * CH + t))
        together(steps - 2, last)
        for t in range(CH):
            last = nc.vector.bn_aggr(agg[:, t * 2:(t + 1) * 2], stats[:, t * 6:(t + 1) * 6])
        together(steps - 1, last)
        together(steps, nc.vector.tensor_copy(pair[:, bass.ds(i * (2 * CH), 2 * CH)], agg[:, :]))
    return steps * (G // CH)


def layernorm(c, turn=False, eps=1e-5):
    nc, s = c.nc, c.s
    with ExitStack() as ctx:
        sb = c.scratch(ctx)
        stats, agg = sb("ln_stats", [P, 6 * CH], FP32), sb("ln_agg", [P, 2 * CH], FP32)
        ring = sb("ln_ring", [P, 2 * D], FP32)
        before = 3 * (G // CH) + 3
        with nc.Block() as block:
            @block.vector
            def _(v):
                ch = Chain(v, s["vec"], row_stats(c, v, stats, agg, lambda g: c.rows(c.X, g), 0))
                pair = c.stat_pair[:, :].rearrange("p (g n) -> p g n", n=2)
                ch.link(nc.vector.tensor_copy(c.mean[:, :], pair[:, :, 0]))
                ch.link(nc.vector.tensor_scalar(c.rstd[:, :], pair[:, :, 1], eps, None, ALU.add))
                v.sem_inc(s["stats_ready"].sem, 1)
                v.wait_ge(s["act"].sem, s["act"].at(1))
                ch.link(nc.vector.reciprocal(c.rstd[:, :], c.rstd[:, :]))
                if not turn:
                    with v.Fori(0, G) as g:
                        nc.vector.tensor_scalar(c.rows(c.T, g), c.rows(c.X, g), c.mean[:, bass.ds(g, 1)],
                                                c.rstd[:, bass.ds(g, 1)], ALU.subtract, ALU.mult).then_inc(s["vec"].sem, 1)
                else:
                    def normed(g, b):
                        v.wait_ge(s["turned"].sem, s["turned"].at(g - 1))
                        v.wait_ge(s["rows_ready"].sem, s["rows_ready"].at(g - 1))
                        nc.vector.tensor_scalar(ring[:, b * D:(b + 1) * D], c.rows(c.X, g), c.mean[:, bass.ds(g, 1)],
                                                c.rstd[:, bass.ds(g, 1)], ALU.subtract, ALU.mult).then_inc(s["vec"].sem, 1)

                    def out(g, b):
                        v.wait_ge(s["turned"].sem, s["turned"].at(g + 1))
                        dst = c.B2[:, :].rearrange("p (k n) -> p k n", k=KD)[:, :, bass.ds(g * P, P)]
                        nc.vector.tensor_copy(dst, c.bank[b][:, 0:D].rearrange("p (k n) -> p k n", k=KD))\
                            .then_inc(s["turned_out"].sem, 1)
                    per_tile(v, normed, out)

            @block.scalar
            def _(act):
                act.wait_ge(s["stats_ready"].sem, s["stats_ready"].at(1))
                nc.scalar.activation(c.rstd[:, :], c.rstd[:, :], ACT.Sqrt).then_inc(s["act"].sem, 1)
                if turn:
                    def copy(g, b):
                        act.wait_ge(s["vec"].sem, s["vec"].at(before + 1 + g))
                        nc.scalar.activation(c.rows(c.T, g), ring[:, b * D:(b + 1) * D], ACT.Copy)\
                            .then_inc(s["rows_ready"].sem, 1)
                    per_tile(act, copy, lambda g, b: None)

            @block.tensor
            def _(pe):
                if turn:
                    def turned(g, b):
                        pe.wait_ge(s["vec"].sem, s["vec"].at(before + 1 + g))
                        pe.wait_ge(s["turned_out"].sem, s["turned_out"].at(g - 1))
                        for k in range(KD):
                            last = nc.tensor.transpose(c.bank[b][:, k * P:(k + 1) * P],
                                                       ring[:, b * D + k * P:b * D + (k + 1) * P], c.ident[:, :])
                        last.then_inc(s["turned"].sem, 1)
                    per_tile(pe, turned, lambda g, b: None)
    s["vec"].passed(before + G)
    s["stats_ready"].passed(1)
    s["act"].passed(1)
    if turn:
        s["turned"].passed(G)
        s["turned_out"].passed(G)
        s["rows_ready"].passed(G)


def project(c, ins, outs, post_steps=0, loads=()):
    nc, s = c.nc, c.s
    nin, nout = len(ins), len(outs)
    vec_outs = [o for o in outs if o[2][0] == "vec"]
    act_outs = [(n, o) for n, o in enumerate(outs) if o[2][0] != "vec"]
    stores = [n for n, o in act_outs if o[2][0] in ("dram", "both")]
    with ExitStack() as ctx:
        sb = c.scratch(ctx)
        ring = sb("pj_ring", [P, 2 * nin * D], FP32)
        turned = sb("pj_turned", [P, 2 * nin * D], FP32)
        staged = sb("pj_staged", [P, 2 * nout * D], FP32)

        def slot(buf, b, n, count):
            return buf[:, (b * count + n) * D:(b * count + n + 1) * D]

        def target(n, g, b):
            post = outs[n][2]
            return post[1](g) if post[0] in ("sbuf", "both") else slot(staged, b, n, nout)

        def product(n, b):
            return c.bank[4 + 2 * b + n // 2][:, (n % 2) * D:(n % 2 + 1) * D]

        with nc.Block() as block:
            @block.sync
            def _(sp):
                for dst, src in loads:
                    sp.dma_start(dst, src).then_inc(s["loaded"].sem, 16)
                if loads:
                    sp.wait_ge(s["loaded"].sem, s["loaded"].at(16 * len(loads)))
                    sp.sem_inc(s["const_ready"].sem, 1)
                if stores:
                    def store(g, b):
                        sp.wait_ge(s["product_out"].sem, s["product_out"].at(g + 1))
                        for n in stores:
                            table = outs[n][2][-1]
                            sp.dma_start(table[bass.ds(g * P, P), :], target(n, g, b)).then_inc(c.written[b].sem, 16)
                    per_tile(sp, store, lambda g, b: None)
                    for b in range(2):
                        sp.wait_ge(c.written[b].sem, c.written[b].at(16 * len(stores) * ((G + 1 - b) // 2)))

            @block.vector
            def _(v):
                if loads:
                    v.wait_ge(s["const_ready"].sem, s["const_ready"].at(1))
                def lead(g, b):
                    v.wait_ge(s["turned"].sem, s["turned"].at(g - 1))
                    for n, make in enumerate(ins):
                        make(g, slot(ring, b, n, nin)).then_inc(s["rows_ready"].sem, 1)

                def follow(g, b):
                    if vec_outs:
                        v.wait_ge(s["product"].sem, s["product"].at(g + 1))
                        ch = Chain(v, s["vec"], g * post_steps)
                        for n, o in enumerate(outs):
                            if o[2][0] == "vec":
                                o[2][1](ch, g, product(n, b))
                        v.sem_inc(s["outcome_used"].sem, 1)
                per_tile(v, lead, follow)

            @block.tensor
            def _(pe):
                if loads:
                    pe.wait_ge(s["const_ready"].sem, s["const_ready"].at(1))

                def turn(g, b):
                    pe.wait_ge(s["rows_ready"].sem, s["rows_ready"].at(nin * (g + 1)))
                    pe.wait_ge(s["turned_out"].sem, s["turned_out"].at(g - 1))
                    for n in range(nin):
                        for k in range(KD):
                            last = nc.tensor.transpose(c.bank[2 * b + n][:, k * P:(k + 1) * P],
                                                       slot(ring, b, n, nin)[:, k * P:(k + 1) * P], c.ident[:, :])
                    last.then_inc(s["turned"].sem, 1)

                def multiply(g, b):
                    pe.wait_ge(s["turned_out"].sem, s["turned_out"].at(g + 1))
                    if act_outs:
                        pe.wait_ge(s["product_out"].sem, s["product_out"].at(g - 1))
                    if vec_outs:
                        pe.wait_ge(s["outcome_used"].sem, s["outcome_used"].at(g - 1))
                    for m, (weights, bias, _) in enumerate(outs):
                        todo = [(slot(turned, b, n, nin)[:, k * P:(k + 1) * P], w[:, k * D:(k + 1) * D])
                                for n, w in enumerate(weights) if w is not None for k in range(KD)]
                        if bias is not None:
                            todo.append((c.ones[0:1, :], bias))
                        for q, (a, w) in enumerate(todo):
                            last = nc.tensor.matmul(product(m, b), a, w, start=(q == 0), stop=(q == len(todo) - 1))
                    last.then_inc(s["product"].sem, 1)
                per_tile(pe, turn, multiply)

            @block.scalar
            def _(act):
                def evacuate(g, b):
                    act.wait_ge(s["turned"].sem, s["turned"].at(g + 1))
                    act.wait_ge(s["product"].sem, s["product"].at(g - 1))
                    for n in range(nin):
                        last = nc.scalar.activation(slot(turned, b, n, nin), c.bank[2 * b + n][:, 0:D], ACT.Copy)
                    last.then_inc(s["turned_out"].sem, 1)

                def finish(g, b):
                    if not act_outs:
                        return
                    act.wait_ge(s["product"].sem, s["product"].at(g + 1))
                    if stores:
                        act.wait_ge(c.written[b].sem, c.written[b].at((g - b) * (8 * len(stores))))
                    for n, o in act_outs:
                        last = nc.scalar.activation(target(n, g, b), product(n, b), ACT.Copy)
                    last.then_inc(s["product_out"].sem, 1)
                per_tile(act, evacuate, finish)
    if loads:
        s["loaded"].passed(16 * len(loads))
        s["const_ready"].passed(1)
    s["rows_ready"].passed(nin * G)
    for n in ("turned", "turned_out", "product"):
        s[n].passed(G)
    if act_outs:
        s["product_out"].passed(G)
    if stores:
        for b in range(2):
            c.written[b].passed(16 * len(stores) * ((G + 1 - b) // 2))
    if vec_outs:
        s["outcome_used"].passed(G)
        s["vec"].passed(post_steps * G)


def groups_of_half(c, engine, key, k):
    _, values = c.nc.values_load_multi_w_load_instructions(c.group[key][0:1, bass.ds(k * HALF, HALF)], engines=[engine],
                                                           min_val=0, max_val=G - 1)
    return values


def record(c, key):
    r = c.rec[key][:, :].rearrange("p (t c) -> p t c", c=4)
    return r[:, :, 0].bitcast(I32), r[:, :, 1], r[:, :, 2]


def halves(eng, body):
    for h in range(2):
        body(h, h, True)
    with eng.Fori(1, TILES // (2 * HALF)) as i:
        for h in range(2):
            body(i * 2 + h, h, False)


def stage_index(c, act, key, idx_ring, k, h, freed):
    if freed is not None:
        act.wait_ge(freed.sem, freed.at(k * HALF - HALF))
        act.sem_inc(c.s["act_go"].sem, 1)
    c.nc.scalar.activation(idx_ring[:, h * HALF:(h + 1) * HALF], record(c, key)[0][:, bass.ds(k * HALF, HALF)], ACT.Copy)\
        .then_inc(c.s["ring_staged"].sem, 1)


def gather_rows(c, pool, table, idx_ring, rows, stride=D):
    nc, s = c.nc, c.s

    def body(k, h, first):
        pool.wait_ge(s["ring_staged"].sem, s["ring_staged"].at(k + 1))
        pool.sem_inc(s["pool_go"].sem, 1)
        for j in range(h * HALF, (h + 1) * HALF):
            nc.gpsimd.indirect_dma_start(rows[:, j * stride:j * stride + D], None, table[:, :],
                                         bass.IndirectOffsetOnAxis(ap=idx_ring[:, j:j + 1], axis=0))\
                .then_inc(c.arrived[j].sem, 16)
    halves(pool, body)


def gather_passed(c, waits=TILES // HALF - 2):
    c.s["ring_staged"].passed(TILES // HALF)
    c.s["pool_go"].passed(TILES // HALF)
    c.s["act_go"].passed(waits)
    for sig in c.arrived:
        sig.passed(16 * TILES // (2 * HALF))


def aggregate(c, table, key, weighted=False, clear=True):
    nc, s = c.nc, c.s
    _, low, weight = record(c, key)
    rounds = TILES // (2 * HALF)
    with ExitStack() as ctx:
        sb = c.scratch(ctx)
        idx_ring = sb("ag_idx", [P, 2 * HALF], I32)
        rows = sb("ag_rows", [P, 2 * HALF * D], FP32)
        hot = sb("ag_hot", [P, 2 * HALF * P], FP32)
        with nc.Block() as block:
            @block.gpsimd
            def _(pool):
                gather_rows(c, pool, table, idx_ring, rows)

            @block.scalar
            def _(act):
                halves(act, lambda k, h, first: stage_index(c, act, key, idx_ring, k, h, None if first else s["product"]))

            @block.tensor
            def _(pe):
                def body(k, h, first):
                    for j in range(HALF):
                        q = h * HALF + j
                        pe.wait_ge(s["onehot_ready"].sem, s["onehot_ready"].at(k * HALF + j + 1))
                        pe.wait_ge(c.arrived[q].sem, c.arrived[q].at((k - h) * 8 + 16))
                        pe.wait_ge(s["summed"].sem, s["summed"].at(k * HALF + j - HALF + 1))
                        nc.tensor.matmul(c.bank[j][:, 0:D], hot[:, q * P:(q + 1) * P], rows[:, q * D:(q + 1) * D],
                                         start=True, stop=True).then_inc(s["product"].sem, 1)
                halves(pe, body)

            @block.vector
            def _(v):
                if clear:
                    nc.vector.memset(c.ACC[:, :], 0.0).then_inc(s["vec"].sem, 1)
                    v.wait_ge(s["vec"].sem, s["vec"].at(1))

                def hots(k, h):
                    v.wait_ge(s["product"].sem, s["product"].at((k - 1) * HALF))
                    for j in range(HALF):
                        q = h * HALF + j
                        t = bass.ds(k * HALF + j, 1)
                        if weighted:
                            ins = nc.vector.tensor_scalar(hot[:, q * P:(q + 1) * P], c.iota[:, 0:P], low[:, t],
                                                          weight[:, t], ALU.is_equal, ALU.mult)
                        else:
                            ins = nc.vector.tensor_scalar(hot[:, q * P:(q + 1) * P], c.iota[:, 0:P], low[:, t],
                                                          None, ALU.is_equal)
                        ins.then_inc(s["onehot_ready"].sem, 1)

                def sums(k, h):
                    for j, g in enumerate(groups_of_half(c, mybir.EngineType.DVE, key, k)):
                        t = k * HALF + j
                        v.wait_ge(s["summed"].sem, s["summed"].at(t))
                        v.wait_ge(s["product"].sem, s["product"].at(t + 1))
                        acc = c.rows(c.ACC, g, D, AW)
                        nc.vector.tensor_tensor(acc, acc, c.bank[j][:, 0:D], ALU.add).then_inc(s["summed"].sem, 1)
                hots(0, 0)
                with v.Fori(0, rounds - 1) as i:
                    for h in range(2):
                        hots(i * 2 + h + 1, 1 - h)
                        sums(i * 2 + h, h)
                k = TILES // HALF - 2
                hots(k + 1, 1)
                sums(k, 0)
                sums(k + 1, 1)
    gather_passed(c)
    for n in ("product", "summed", "onehot_ready"):
        s[n].passed(TILES)
    if clear:
        s["vec"].passed(1)


def spread(row):
    return row.partition_broadcast(P)


def weight_view(w):
    return w.rearrange("(k p) f -> p k f", p=P)


def as_k(t):
    return t.rearrange("p (k f) -> p k f", k=KD)


def gcn(c, a):
    nc, s = c.nc, c.s
    layernorm(c)
    table = c.dram("gcn_table", [NP, D], FP32)
    with ExitStack() as ctx:
        w = ctx.enter_context(nc.sbuf_tensor("gcn_w", [P, KD * D], FP32))
        bias = ctx.enter_context(nc.sbuf_tensor("gcn_b", [P, D], FP32))
        for layer in range(3):
            def scaled(g, out):
                return nc.vector.tensor_scalar(out, c.rows(c.T, g), c.dinv[:, bass.ds(g, 1)], None, ALU.mult)
            project(c, [scaled], [([w], None, ("both", lambda g: c.rows(c.ACC, g, D, AW), table))],
                    loads=[(as_k(w[:, :]), weight_view(a[f"L0_gnn_W{layer + 1}"])),
                           (bias[:, :], spread(a[f"L0_gnn_b{layer + 1}"]))])
            aggregate(c, table, "dst", clear=False)
            last = layer == 2
            with nc.Block() as block:
                @block.vector
                def _(v):
                    with v.Fori(0, G) as g:
                        ch = Chain(v, s["vec"], g)
                        acc, t = c.rows(c.ACC, g, D, AW), c.rows(c.T, g)
                        ch.link(nc.vector.scalar_tensor_tensor(t, acc, c.dinv[:, bass.ds(g, 1)], bias[:, :], ALU.mult, ALU.add))
                    if last:
                        nc.vector.tensor_tensor(c.X[:, :], c.X[:, :], c.T[:, :], ALU.add).then_inc(s["vec"].sem, 1)
            s["vec"].passed(G + last)


def gate_logits(c, w_gate, bias_row, width, logits):
    nc, s = c.nc, c.s
    xt = c.B2[:, :].rearrange("p (k n) -> p k n", k=KD)
    with ExitStack() as ctx:
        sb = c.scratch(ctx)
        ring = sb("gl_ring", [P, 2 * D], FP32)
        w = sb("gl_w", [P, KD * width], FP32)
        row = sb("gl_row", [1, width], FP32)
        with nc.Block() as block:
            @block.sync
            def _(sp):
                sp.dma_start(w[:, :].rearrange("p (k f) -> p k f", k=KD), weight_view(w_gate)).then_inc(s["loaded"].sem, 16)
                sp.dma_start(row[:, :], bias_row).then_inc(s["loaded"].sem, 16)

            @block.vector
            def _(v):
                def stage(g, b):
                    v.wait_ge(s["product"].sem, s["product"].at(g - 1))
                    nc.vector.tensor_copy(ring[:, b * D:(b + 1) * D].rearrange("p (k n) -> p k n", k=KD),
                                          xt[:, :, bass.ds(g * P, P)]).then_inc(s["rows_ready"].sem, 1)

                def out(g, b):
                    v.wait_ge(s["product"].sem, s["product"].at(g + 1))
                    nc.vector.tensor_copy(logits[:, bass.ds(g * width, width)], c.bank[b][:, 0:width])\
                        .then_inc(s["product_out"].sem, 1)
                per_tile(v, stage, out)

            @block.tensor
            def _(pe):
                pe.wait_ge(s["loaded"].sem, s["loaded"].at(32))

                def multiply(g, b):
                    pe.wait_ge(s["rows_ready"].sem, s["rows_ready"].at(g + 1))
                    pe.wait_ge(s["product_out"].sem, s["product_out"].at(g - 1))
                    o = c.bank[b][:, 0:width]
                    for k in range(KD):
                        nc.tensor.matmul(o, ring[:, b * D + k * P:b * D + (k + 1) * P], w[:, k * width:(k + 1) * width],
                                         start=(k == 0), stop=False)
                    nc.tensor.matmul(o, c.ones[0:1, :], row[:, :], start=False, stop=True).then_inc(s["product"].sem, 1)
                per_tile(pe, multiply, lambda g, b: None)
    s["loaded"].passed(32)
    for n in ("rows_ready", "product", "product_out"):
        s[n].passed(G)


class Expert:

    def __init__(self, w1, w2, b2, mid=None):
        self.w1, self.w2, self.b2, self.mid = w1, w2, b2, mid


def experts(c, count, width, expert, act1, column1, gate, mid_act=None, column2=None):
    nc, s = c.nc, c.s
    nf = width // P
    units = 2 * (G // CH)
    xt = c.B2[:, 0:KD * NP].rearrange("p (k n) -> p k n", k=KD)
    mid = mid_act is not None
    n_loads = 4 if mid else 3
    with ExitStack() as ctx:
        sb = c.scratch(ctx)
        w1 = sb("ex_w1", [P, 2 * KD * width], FP32)
        w2 = sb("ex_w2", [P, 2 * nf * D], FP32)
        b2 = sb("ex_b2", [P, 2 * D], FP32)
        wm = sb("ex_wm", [P, 2 * nf * width], FP32) if mid else None
        hid = sb("ex_hid", [P, 2 * nf * TOK], FP32)
        hid2 = sb("ex_hid2", [P, 2 * nf * TOK], FP32) if mid else hid
        tmp = sb("ex_tmp", [P, 4 * D], FP32)
        stages = 2 if mid else 1
        tables = [x for col in (column1, column2) if col for x in col if not isinstance(x, float)]
        local = [sb(f"ex_column{n}", [P, 2 * nf], FP32) for n in range(len(tables))]
        per_unit = stages * nf * 2

        def h(buf, slot, f, n0, n):
            o = (slot * nf + f) * TOK + n0
            return buf[:, o:o + n]

        def outcome_bank(n):
            return c.bank[4 + n % 2][:, 0:D]

        def rounds(eng, body):
            if count > 2:
                with eng.Fori(0, count // 2 - 1) as i:
                    body(i, False)
            body(count // 2 - 1, True)

        with nc.Block() as block:
            @block.sync
            def _(sp):
                def load(e, slot, used):
                    if used is not None:
                        sp.wait_ge(s["weights_used"].sem, s["weights_used"].at(used))
                    sig = s["wa"] if slot == 0 else s["wb"]
                    pairs = [(w1[:, slot * KD * width:(slot + 1) * KD * width].rearrange("p (k f) -> p k f", k=KD), expert.w1(sp, e)),
                             (w2[:, slot * nf * D:(slot + 1) * nf * D].rearrange("p (k f) -> p k f", k=nf), expert.w2(sp, e)),
                             (b2[:, slot * D:(slot + 1) * D], expert.b2(sp, e))]
                    if mid:
                        pairs.append((wm[:, slot * nf * width:(slot + 1) * nf * width].rearrange("p (k f) -> p k f", k=nf),
                                      expert.mid(sp, e)))
                    for dst, src in pairs:
                        sp.dma_start(dst, src).then_inc(sig.sem, 16)
                load(0, 0, None)
                load(1, 1, None)
                if count > 2:
                    with sp.Fori(1, count // 2) as i:
                        load(i * 2, 0, i * 2 - 1)
                        load(i * 2 + 1, 1, i * 2)

            def weights_here(eng, i, slot, ahead=0):
                sig = s["wa"] if slot == 0 else s["wb"]
                eng.wait_ge(sig.sem, sig.at((i + ahead) * (16 * n_loads) + 16 * n_loads))

            @block.tensor
            def _(pe):
                def first_layer(i, u):
                    ahead, u = u // units, u % units
                    slot, ck, q = u // (units // 2), u % (units // 2), u % 2
                    if ck == 0:
                        weights_here(pe, i, slot, ahead)
                    n0 = (i + ahead) * (units * per_unit) + u * per_unit
                    for f in range(nf):
                        for half in range(2):
                            n = f * 2 + half
                            bank = n % 4
                            pe.wait_ge(s["hidden_out"].sem, s["hidden_out"].at(n0 + n - 3))
                            for k in range(KD):
                                last = nc.tensor.matmul(
                                    c.bank[bank][:, 0:HT], w1[:, (slot * KD + k) * width + f * P:(slot * KD + k) * width + (f + 1) * P],
                                    xt[:, k, ck * TOK + half * HT:ck * TOK + (half + 1) * HT], start=(k == 0), stop=(k == KD - 1))
                            last.then_inc(s["hidden"].sem, 1)

                def mid_layer(i, u):
                    slot, q = u // (units // 2), u % 2
                    n0 = i * (units * per_unit) + u * per_unit + nf * 2
                    pe.wait_ge(s["hidden_out"].sem, s["hidden_out"].at(n0))
                    for f in range(nf):
                        for half in range(2):
                            n = f * 2 + half
                            for k in range(nf):
                                last = nc.tensor.matmul(
                                    c.bank[n % 4][:, 0:HT], wm[:, (slot * nf + k) * width + f * P:(slot * nf + k) * width + (f + 1) * P],
                                    h(hid, q, k, half * HT, HT), start=(k == 0), stop=(k == nf - 1))
                            last.then_inc(s["hidden"].sem, 1)

                def last_layer(i, u, is_last):
                    slot, q = u // (units // 2), u % 2
                    pe.wait_ge(s["hidden_out"].sem, s["hidden_out"].at(i * (units * per_unit) + (u + 1) * per_unit))
                    for t in range(CH):
                        n = u * CH + t
                        pe.wait_ge(s["outcome_used"].sem, s["outcome_used"].at(i * (units * CH) + n - 1))
                        for k in range(nf):
                            last = nc.tensor.matmul(outcome_bank(n), h(hid2, q, k, t * P, P), w2[:, (slot * nf + k) * D:(slot * nf + k + 1) * D],
                                                    start=(k == 0), stop=(k == nf - 1))
                        last.then_inc(s["outcome"].sem, 1)

                if mid:
                    def body(i, is_last):
                        for u in range(units):
                            first_layer(i, u)
                            mid_layer(i, u)
                            last_layer(i, u, is_last)
                    rounds(pe, body)
                else:
                    first_layer(0, 0)

                    def body(i, is_last):
                        for u in range(units):
                            if not (is_last and u == units - 1):
                                first_layer(i, u + 1)
                            last_layer(i, u, is_last)
                    rounds(pe, body)

            @block.scalar
            def _(act):
                def body(i, is_last):
                    for u in range(units):
                        e_slot, q = u // (units // 2), u % 2
                        e = i * 2 + e_slot
                        act.wait_ge(s["outcome"].sem, s["outcome"].at(i * (units * CH) + (u - 1) * CH))
                        if u % (units // 2) == 0:
                            act.sem_inc(s["act_go"].sem, 1)
                            for n, table in enumerate(tables):
                                nc.scalar.activation(local[n][:, e_slot * nf:(e_slot + 1) * nf],
                                                     table[:, bass.ds(e * nf, nf)], ACT.Copy).then_inc(s["act"].sem, 1)
                            act.wait_ge(s["act"].sem, s["act"].at((i * 2 + e_slot + 1) * len(tables)))
                        for stage in range(stages):
                            fn, column = ((act1, column1), (mid_act, column2))[stage]
                            for f in range(nf):
                                scale, bias = [x if isinstance(x, float) else
                                               local[tables.index(x)][:, e_slot * nf + f:e_slot * nf + f + 1] for x in column]
                                for half in range(2):
                                    n = stage * nf * 2 + f * 2 + half
                                    act.wait_ge(s["hidden"].sem, s["hidden"].at(i * (units * per_unit) + u * per_unit + n + 1))
                                    nc.scalar.activation(h(hid if stage == 0 else hid2, q, f, half * HT, HT),
                                                         c.bank[(f * 2 + half) % 4][:, 0:HT], fn, bias=bias, scale=scale)\
                                        .then_inc(s["hidden_out"].sem, 1)
                rounds(act, body)

            @block.vector
            def _(v):
                nc.vector.memset(c.ACC[:, :], 0.0).then_inc(s["vec"].sem, 1)
                v.wait_ge(s["vec"].sem, s["vec"].at(1))

                def body(i, is_last):
                    for u in range(units):
                        slot, ck = u // (units // 2), u % (units // 2)
                        if ck == 0:
                            weights_here(v, i, slot)
                        for t in range(CH):
                            n = u * CH + t
                            tile = ck * CH + t
                            part = tmp[:, (n % 2) * D:(n % 2 + 1) * D]
                            v.wait_ge(s["outcome"].sem, s["outcome"].at(i * (units * CH) + n + 1))
                            nc.vector.tensor_tensor(part, outcome_bank(n), b2[:, slot * D:(slot + 1) * D], ALU.add)\
                                .then_inc(s["outcome_used"].sem, 1)
                            v.wait_ge(s["outcome_used"].sem, s["outcome_used"].at(i * (units * CH) + n + 1))
                            acc = c.ACC[:, tile * AW:tile * AW + D]
                            nc.vector.scalar_tensor_tensor(acc, part, gate(tile, i * 2 + slot), acc, ALU.mult, ALU.add)\
                                .then_inc(s["vec"].sem, 1)
                            v.wait_ge(s["vec"].sem, s["vec"].at(i * (units * CH) + n + 2))
                        if ck == units // 2 - 1:
                            v.sem_inc(s["weights_used"].sem, 1)
                rounds(v, body)
    pairs = count // 2
    for n in ("wa", "wb"):
        s[n].passed(pairs * 16 * n_loads)
    s["weights_used"].passed(count)
    s["act"].passed(count * len(tables))
    s["hidden"].passed(pairs * units * per_unit)
    s["hidden_out"].passed(pairs * units * per_unit)
    s["outcome"].passed(pairs * units * CH)
    s["outcome_used"].passed(pairs * units * CH)
    s["vec"].passed(pairs * units * CH + 1)


def top_two(c, logits, width, chosen, shares):
    nc, s = c.nc, c.s
    with ExitStack() as ctx:
        sb = c.scratch(ctx)
        best, where = sb("tt_best", [P, G * 8], FP32), sb("tt_where", [P, G * 8], U32)
        where_f = sb("tt_where_f", [P, G * 8], FP32)
        e2 = sb("tt_e2", [P, G], FP32)
        b3 = best[:, :].rearrange("p (g e) -> p g e", e=8)
        w3 = where_f[:, :].rearrange("p (g e) -> p g e", e=8)
        share1, share2 = shares[:, 0:G], shares[:, G:2 * G]
        with nc.Block() as block:
            @block.vector
            def _(v):
                ch = Chain(v, s["vec"])
                for g in range(G):
                    row = logits[:, g * width:(g + 1) * width]
                    ch.link(nc.vector.max(best[:, g * 8:(g + 1) * 8], row))
                    ch.link(nc.vector.max_index(where[:, g * 8:(g + 1) * 8], best[:, g * 8:(g + 1) * 8], row))
                ch.link(nc.vector.tensor_copy(where_f[:, :], where[:, :]))
                ch.link(nc.vector.tensor_tensor(e2[:, :], b3[:, :, 1], b3[:, :, 0], ALU.subtract))
                v.sem_inc(s["stats_ready"].sem, 1)
                for n in range(2):
                    ch.link(nc.vector.tensor_copy(chosen[:, n * G:(n + 1) * G], w3[:, :, n]))
                v.wait_ge(s["act"].sem, s["act"].at(1))
                ch.link(nc.vector.tensor_scalar(share1, e2[:, :], 1.0, None, ALU.add))
                ch.link(nc.vector.reciprocal(share1, share1))
                ch.link(nc.vector.tensor_tensor(share2, share1, e2[:, :], ALU.mult))
                c.vec_steps = ch.n

            @block.scalar
            def _(act):
                act.wait_ge(s["stats_ready"].sem, s["stats_ready"].at(1))
                nc.scalar.activation(e2[:, :], e2[:, :], ACT.Exp).then_inc(s["act"].sem, 1)
    s["vec"].passed(c.vec_steps)
    s["stats_ready"].passed(1)
    s["act"].passed(1)


def route(c, chosen, cols, count, tiles, slot, expert_of, table):
    nc, s = c.nc, c.s
    with ExitStack() as ctx:
        sb = c.scratch(ctx)
        member, prefix = sb("ro_member", [P, count * cols], FP32), sb("ro_prefix", [P, count * cols], FP32)
        rank, first, tmp = (sb(f"ro_{n}", [P, cols], FP32) for n in ("rank", "first", "tmp"))
        row_total, row_offset = sb("ro_row_total", [P, count], FP32), sb("ro_row_offset", [P, count], FP32)
        tiles_f, tiles_i = sb("ro_tiles_f", [P, count], FP32), sb("ro_tiles_i", [P, count], I32)
        end, start = sb("ro_end", [P, count], FP32), sb("ro_start", [P, count], FP32)
        expert_f = sb("ro_expert_f", [1, tiles], FP32)
        offs, totals = c.bank[0][:, 0:count], c.bank[1][:, 0:count]
        with nc.Block() as block:
            @block.sync
            def _(sp):
                sp.dma_start(table.rearrange("(p a) d -> p (a d)", p=P).rearrange("p (n m) -> p n m", m=2 * D),
                             c.zeros[:, 0:2 * D].unsqueeze(1).broadcast_to([P, tiles // 2, 2 * D])).then_inc(s["stored"].sem, 16)
                sp.wait_ge(s["stored"].sem, s["stored"].at(16))

            @block.gpsimd
            def _(pool):
                pool.wait_ge(s["stored"].sem, s["stored"].at(16))
                pool.wait_ge(s["slot_ready"].sem, s["slot_ready"].at(1))
                pool.sem_inc(s["pool_go"].sem, 1)
                for n in range(cols):
                    g = n % G
                    nc.gpsimd.indirect_dma_start(table[:, :], bass.IndirectOffsetOnAxis(ap=slot[:, n:n + 1], axis=0),
                                                 c.T[:, g * D:(g + 1) * D], None).then_inc(c.arrived[n % len(c.arrived)].sem, 16)
                wait_for_columns(c, pool, cols)

            @block.tensor
            def _(pe):
                pe.wait_ge(s["rows_ready"].sem, s["rows_ready"].at(1))
                nc.tensor.matmul(offs, c.earlier[:, :], row_total[:, :], start=True, stop=True)
                nc.tensor.matmul(totals, c.ones[:, :], row_total[:, :], start=True, stop=True).then_inc(s["product"].sem, 1)

            @block.vector
            def _(v):
                ch = Chain(v, s["vec"])
                ch.link(nc.vector.memset(rank[:, :], 0.0))
                ch.link(nc.vector.memset(first[:, :], 0.0))
                m3 = member[:, :].rearrange("p (e n) -> p e n", n=cols)
                p3 = prefix[:, :].rearrange("p (e n) -> p e n", n=cols)
                ch.link(nc.vector.tensor_tensor(m3, chosen.unsqueeze(1).broadcast_to([P, count, cols]),
                                                c.iota[:, 0:count].unsqueeze(2).broadcast_to([P, count, cols]), ALU.is_equal))
                n0 = ch.n
                with v.Fori(0, count) as e:
                    one = Chain(v, s["vec"], e + n0)
                    one.link(nc.vector.tensor_tensor_scan(c.rows(prefix, e, cols), c.rows(member, e, cols),
                                                          c.zeros[:, 0:cols], 0.0, ALU.add, ALU.add))
                ch.n = n0 + count
                ch.link(nc.vector.tensor_copy(row_total[:, :], p3[:, :, cols - 1]))
                v.sem_inc(s["rows_ready"].sem, 1)
                v.wait_ge(s["product"].sem, s["product"].at(1))
                ch.link(nc.vector.tensor_scalar(row_offset[:, :], offs, -1.0, None, ALU.add))
                ch.link(nc.vector.tensor_scalar(tiles_i[:, :], totals, float(P - 1), None, ALU.add))
                ch.link(nc.vector.tensor_scalar(tiles_i[:, :], tiles_i[:, :], 7, None, ALU.logical_shift_right))
                ch.link(nc.vector.tensor_copy(tiles_f[:, :], tiles_i[:, :]))
                ch.link(nc.vector.tensor_tensor_scan(end[:, :], tiles_f[:, :], c.zeros[:, 0:count], 0.0, ALU.add, ALU.add))
                ch.link(nc.vector.tensor_tensor(start[:, :], end[:, :], tiles_f[:, :], ALU.subtract))
                n1 = ch.n
                with v.Fori(0, count) as e:
                    one = Chain(v, s["vec"], e * 3 + n1)
                    me, pr, col = c.rows(member, e, cols), c.rows(prefix, e, cols), bass.ds(e, 1)
                    one.link(nc.vector.scalar_tensor_tensor(tmp[:, :], pr, row_offset[:, col], me, ALU.add, ALU.mult))
                    one.link(nc.vector.tensor_tensor(rank[:, :], rank[:, :], tmp[:, :], ALU.add))
                    one.link(nc.vector.scalar_tensor_tensor(first[:, :], me, start[:, col], first[:, :], ALU.mult, ALU.add))
                ch.n = n1 + 3 * count
                ch.link(nc.vector.scalar_tensor_tensor(first[:, :], first[:, :], float(P), rank[:, :], ALU.mult, ALU.add))
                ch.link(nc.vector.tensor_copy(slot[:, :], first[:, :]))
                v.sem_inc(s["slot_ready"].sem, 1)
                ch.link(nc.vector.memset(expert_f[:, :], 0.0))
                n2 = ch.n
                with v.Fori(0, count) as e:
                    one = Chain(v, s["vec"], e + n2)
                    one.link(nc.vector.scalar_tensor_tensor(expert_f[:, :], c.iota[0:1, 0:tiles], end[0:1, bass.ds(e, 1)],
                                                            expert_f[:, :], ALU.is_ge, ALU.add))
                ch.n = n2 + count
                ch.link(nc.vector.tensor_scalar(expert_of[:, :], expert_f[:, :], float(count - 1), None, ALU.min))
                c.vec_steps = ch.n
    s["stored"].passed(16)
    s["pool_go"].passed(1)
    s["vec"].passed(c.vec_steps)
    for n in ("product", "rows_ready", "slot_ready"):
        s[n].passed(1)
    columns_passed(c, cols)


def wait_for_column(c, eng, n):
    sig = c.arrived[n % len(c.arrived)]
    eng.wait_ge(sig.sem, sig.at(16 * (n // len(c.arrived) + 1)))


def wait_for_columns(c, eng, cols):
    for n in range(max(0, cols - len(c.arrived)), cols):
        wait_for_column(c, eng, n)


def columns_passed(c, cols):
    for n in range(cols):
        c.arrived[n % len(c.arrived)].passed(16)


def routed(c, tiles, expert_of, sent, returned, width, function, w2, b2, b1, w1=None, w1_here=None):
    nc, s = c.nc, c.s
    nf = width // P
    nb = nf // 4
    shared = w1_here is not None
    n_loads = 3 if shared else 4
    slots_of_weights = (s["wa"], s["wb"], s["wc"])
    per_round = ROUND // 3 * 16 * n_loads
    with ExitStack() as ctx:
        sb = c.scratch(ctx)
        w1_ring = w1_here if shared else sb("rt_w1", [P, 3 * KD * width], FP32)
        w2_ring = sb("rt_w2", [P, 3 * nf * D], FP32)
        b2_ring = sb("rt_b2", [1, 3 * D], FP32)
        x_ring, xt_ring = sb("rt_x", [P, 3 * D], FP32), sb("rt_xt", [P, 2 * D], FP32)
        hid = sb("rt_hid", [P, 2 * nf * P], FP32)
        out = sb("rt_out", [P, 2 * D], FP32)
        local = None if shared else sb("rt_b1", [P, 2 * nf], FP32)

        def experts_of_round(engine, i):
            _, values = nc.values_load_multi_w_load_instructions(expert_of[0:1, bass.ds(i * ROUND, ROUND)], engines=[engine],
                                                                 min_val=0, max_val=b2.shape[0] - 1)
            return values

        with nc.Block() as block:
            @block.sync
            def _(sp):
                def store(n, q):
                    sp.wait_ge(s["outcome_used"].sem, s["outcome_used"].at(n + 1))
                    sp.dma_start(returned[bass.ds(n * P, P), :], out[:, q * D:(q + 1) * D]).then_inc(c.written[q].sem, 16)

                def body(i, first):
                    for j, e in enumerate(experts_of_round(mybir.EngineType.SP, i)):
                        n, r, later = i * ROUND + j, j % 3, not (first and j < 3)
                        if later:
                            sp.wait_ge(s["outcome"].sem, s["outcome"].at(n - 2))
                        sig = slots_of_weights[r]
                        pairs = [(x_ring[:, r * D:(r + 1) * D], sent[bass.ds(n * P, P), :]),
                                 (w2_ring[:, r * nf * D:(r + 1) * nf * D].rearrange("p (k f) -> p k f", k=nf), at_expert(w2, e)),
                                 (b2_ring[:, r * D:(r + 1) * D], b2[bass.ds(e, 1), :])]
                        if not shared:
                            pairs.insert(1, (w1_ring[:, r * KD * width:(r + 1) * KD * width].rearrange("p (k f) -> p k f", k=KD),
                                             at_expert(w1, e)))
                        for dst, src in pairs:
                            sp.dma_start(dst, src).then_inc(sig.sem, 16)
                        if later:
                            store(n - 3, (j + 1) % 2)
                body(0, True)
                with sp.Fori(1, tiles // ROUND) as i:
                    body(i, False)
                for n in range(tiles - 3, tiles):
                    store(n, n % 2)
                for q in range(2):
                    sp.wait_ge(c.written[q].sem, c.written[q].at(16 * tiles // 2))

            def led(eng, lead, follow):
                lead(0, 0, 0)
                with eng.Fori(0, tiles // ROUND - 1) as i:
                    for j in range(ROUND):
                        lead(i, i * ROUND + j + 1, j + 1)
                        follow(i, i * ROUND + j, j)
                i = tiles // ROUND - 1
                for j in range(ROUND):
                    if j < ROUND - 1:
                        lead(i, i * ROUND + j + 1, j + 1)
                    follow(i, i * ROUND + j, j)

            @block.tensor
            def _(pe):
                def lead(i, n, j):
                    r, q = j % 3, j % 2
                    sig = slots_of_weights[r]
                    pe.wait_ge(sig.sem, sig.at(i * per_round + (j // 3 + 1) * (16 * n_loads)))
                    pe.wait_ge(s["turned_out"].sem, s["turned_out"].at(n - 1))
                    for k in range(KD):
                        turn = nc.tensor.transpose(c.bank[q][:, k * P:(k + 1) * P],
                                                   x_ring[:, r * D + k * P:r * D + (k + 1) * P], c.ident[:, :])
                    turn.then_inc(s["turned"].sem, 1)
                    pe.wait_ge(s["turned_out"].sem, s["turned_out"].at(n + 1))
                    base = 0 if shared else r * KD * width
                    for b in range(nb):
                        pe.wait_ge(s["hidden_out"].sem, s["hidden_out"].at(n * nf - 2 * nf + b * 4 + 4))
                        for f in range(b * 4, b * 4 + 4):
                            for k in range(KD):
                                last = nc.tensor.matmul(c.bank[2 + q * nb + b][:, (f % 4) * P:(f % 4 + 1) * P],
                                                        w1_ring[:, base + k * width + f * P:base + k * width + (f + 1) * P],
                                                        xt_ring[:, q * D + k * P:q * D + (k + 1) * P],
                                                        start=(k == 0), stop=(k == KD - 1))
                        last.then_inc(s["hidden"].sem, 1)

                def follow(i, n, j):
                    r, q = j % 3, j % 2
                    pe.wait_ge(s["hidden_out"].sem, s["hidden_out"].at((n + 1) * nf))
                    pe.wait_ge(s["outcome_used"].sem, s["outcome_used"].at(n - 1))
                    o = c.bank[6 + q][:, 0:D]
                    for k in range(nf):
                        nc.tensor.matmul(o, hid[:, (q * nf + k) * P:(q * nf + k + 1) * P],
                                         w2_ring[:, (r * nf + k) * D:(r * nf + k + 1) * D], start=(k == 0), stop=False)
                    nc.tensor.matmul(o, c.ones[0:1, :], b2_ring[:, r * D:(r + 1) * D], start=False, stop=True)\
                        .then_inc(s["outcome"].sem, 1)
                led(pe, lead, follow)

            @block.scalar
            def _(act):
                def lead(i, n, j):
                    q = j % 2
                    act.wait_ge(s["turned"].sem, s["turned"].at(n + 1))
                    act.wait_ge(s["hidden"].sem, s["hidden"].at(n * nb - nb))
                    nc.scalar.activation(xt_ring[:, q * D:(q + 1) * D], c.bank[q][:, 0:D], ACT.Copy)\
                        .then_inc(s["turned_out"].sem, 1)

                def follow(i, n, j):
                    q = j % 2
                    act.wait_ge(s["outcome"].sem, s["outcome"].at(n - 1))
                    if shared:
                        column = b1
                        act.sem_inc(s["act_go"].sem, 1)
                    else:
                        e = act.value_load(expert_of[0:1, bass.ds(n, 1)], min_val=0, max_val=b2.shape[0] - 1)
                        act.sem_inc(s["act_go"].sem, 1)
                        nc.scalar.activation(local[:, q * nf:(q + 1) * nf], b1[:, bass.ds(e * nf, nf)], ACT.Copy)\
                            .then_inc(s["act"].sem, 1)
                        act.wait_ge(s["act"].sem, s["act"].at(n + 1))
                        column = local[:, q * nf:(q + 1) * nf]
                    for f in range(nf):
                        if f % 4 == 0:
                            act.wait_ge(s["hidden"].sem, s["hidden"].at(n * nb + f // 4 + 1))
                        nc.scalar.activation(hid[:, (q * nf + f) * P:(q * nf + f + 1) * P],
                                             c.bank[2 + q * nb + f // 4][:, (f % 4) * P:(f % 4 + 1) * P], function,
                                             bias=column[:, f:f + 1]).then_inc(s["hidden_out"].sem, 1)
                led(act, lead, follow)

            @block.vector
            def _(v):
                with v.Fori(0, tiles // ROUND) as i:
                    for j in range(ROUND):
                        n, q = i * ROUND + j, j % 2
                        v.wait_ge(s["outcome"].sem, s["outcome"].at(n + 1))
                        v.wait_ge(c.written[q].sem, c.written[q].at(i * (16 * ROUND // 2) + 16 * (j // 2)))
                        nc.vector.tensor_copy(out[:, q * D:(q + 1) * D], c.bank[6 + q][:, 0:D])\
                            .then_inc(s["outcome_used"].sem, 1)
    for sig in slots_of_weights:
        sig.passed(tiles // 3 * 16 * n_loads)
    for sig in c.written:
        sig.passed(16 * tiles // 2)
    for n in ("turned", "turned_out", "outcome", "outcome_used", "act_go"):
        s[n].passed(tiles)
    s["hidden"].passed(tiles * nb)
    s["hidden_out"].passed(tiles * nf)
    if not shared:
        s["act"].passed(tiles)


def collect(c, slot, shares, choices, table):
    nc, s = c.nc, c.s
    ring = len(c.arrived)
    with nc.Block() as block:
        @block.gpsimd
        def _(pool):
            for g in range(G):
                for n, buf in enumerate((c.ACC[:, g * AW:g * AW + D], c.B2[:, g * D:(g + 1) * D])[0:choices]):
                    sent = g * choices + n
                    if sent >= ring and sent % HALF == 0:
                        pool.wait_ge(s["vec"].sem, s["vec"].at(sent - HALF))
                        pool.sem_inc(s["pool_go"].sem, 1)
                    nc.gpsimd.indirect_dma_start(buf, None, table[:, :],
                                                 bass.IndirectOffsetOnAxis(ap=slot[:, n * G + g:n * G + g + 1], axis=0))\
                        .then_inc(c.arrived[(g * choices + n) % len(c.arrived)].sem, 16)

        @block.vector
        def _(v):
            for g in range(G):
                acc = c.ACC[:, g * AW:g * AW + D]
                wait_for_column(c, v, g * choices)
                nc.vector.tensor_scalar(acc, acc, shares[:, g:g + 1], None, ALU.mult).then_inc(s["vec"].sem, 1)
                if choices == 2:
                    wait_for_column(c, v, g * choices + 1)
                    v.wait_ge(s["vec"].sem, s["vec"].at(g * choices + 1))
                    nc.vector.scalar_tensor_tensor(acc, c.B2[:, g * D:(g + 1) * D], shares[:, G + g:G + g + 1], acc,
                                                   ALU.mult, ALU.add).then_inc(s["vec"].sem, 1)
    s["vec"].passed(G * choices)
    s["pool_go"].passed(sum(sent % HALF == 0 for sent in range(ring, G * choices)))
    columns_passed(c, G * choices)


def routed_tiles(entries, count):
    return -(-((entries + count * (P - 1)) // P) // ROUND) * ROUND


def columns(v):
    return v.rearrange("e (f p) -> p (e f)", p=P)


def moe_relu(c, a):
    nc, s = c.nc, c.s
    layernorm(c, turn=True)
    ne, width = 16, 512
    nf = width // P
    with ExitStack() as ctx:
        sb = c.scratch(ctx)
        logits, chosen, shares = sb("logits", [P, G * ne], FP32), sb("chosen", [P, 2 * G], FP32), sb("shares", [P, 2 * G], FP32)
        tiles = routed_tiles(2 * NP, ne)
        slot, expert_of = sb("token_slot", [P, 2 * G], I32), sb("expert_of", [1, tiles], I32)
        sent, returned = (c.dram(f"L0_{n}", [tiles * P, D], FP32) for n in ("sent", "returned"))
        b1 = sb("b1", [P, ne * nf], FP32)
        gamma, beta = sb("gamma", [P, D], FP32), sb("beta", [P, D], FP32)
        load(c, [(b1[:, :], columns(a["L0_ffn_b1"])), (gamma[:, :], spread(a["L0_ffn_gamma"])),
                 (beta[:, :], spread(a["L0_ffn_beta"]))])
        gate_logits(c, a["L0_ffn_gate_w"], a["L0_ffn_gate_b"].unsqueeze(0), ne, logits)
        top_two(c, logits[:, :], ne, chosen[:, :], shares[:, :])
        route(c, chosen[:, :], 2 * G, ne, tiles, slot, expert_of, sent)
        routed(c, tiles, expert_of, sent, returned, width, ACT.Relu, a["L0_ffn_w2"], a["L0_ffn_b2"], b1, w1=a["L0_ffn_w1"])
        collect(c, slot, shares, 2, returned)
        add_normed(c, gamma, beta)


def load(c, pairs):
    s = c.s
    with c.nc.Block() as block:
        @block.sync
        def _(sp):
            for dst, src in pairs:
                sp.dma_start(dst, src, allow_slow_non_contiguous=True).then_inc(s["loaded"].sem, 16)
            sp.wait_ge(s["loaded"].sem, s["loaded"].at(16 * len(pairs)))
    s["loaded"].passed(16 * len(pairs))


def at_expert(w, e):
    return w[bass.ds(e, 1), :, :].rearrange("e (k p) f -> p (e k) f", p=P)


def row_spread(b, e):
    return b[bass.ds(e, 1), :].squeeze(0).partition_broadcast(P)


def add_normed(c, gamma, beta, eps=1e-5):
    nc, s = c.nc, c.s
    with ExitStack() as ctx:
        sb = c.scratch(ctx)
        stats, agg = sb("an_stats", [P, 6 * CH], FP32), sb("an_agg", [P, 2 * CH], FP32)
        before = 4 * (G // CH) + 3
        with nc.Block() as block:
            @block.vector
            def _(v):
                def add(g):
                    return nc.vector.tensor_tensor(c.rows(c.T, g), c.rows(c.T, g), c.rows(c.ACC, g, D, AW), ALU.add)
                ch = Chain(v, s["vec"], row_stats(c, v, stats, agg, lambda g: c.rows(c.T, g), 0, add))
                pair = c.stat_pair[:, :].rearrange("p (g n) -> p g n", n=2)
                ch.link(nc.vector.tensor_copy(c.mean[:, :], pair[:, :, 0]))
                ch.link(nc.vector.tensor_scalar(c.rstd[:, :], pair[:, :, 1], eps, None, ALU.add))
                v.sem_inc(s["stats_ready"].sem, 1)
                v.wait_ge(s["act"].sem, s["act"].at(1))
                ch.link(nc.vector.reciprocal(c.rstd[:, :], c.rstd[:, :]))
                with v.Fori(0, G) as g:
                    last = nc.vector.tensor_scalar(c.rows(c.T, g), c.rows(c.T, g), c.mean[:, bass.ds(g, 1)],
                                                   c.rstd[:, bass.ds(g, 1)], ALU.subtract, ALU.mult)
                    last.then_inc(s["vec"].sem, 1)
                v.wait_ge(s["vec"].sem, s["vec"].at(before + G))
                ch = Chain(v, s["vec"], before + G)
                t3 = c.T[:, :].rearrange("p (g d) -> p g d", d=D)

                def wide(x):
                    return x[:, :].unsqueeze(1).broadcast_to([P, G, D])
                ch.link(nc.vector.tensor_tensor(t3, t3, wide(gamma), ALU.mult))
                ch.link(nc.vector.tensor_tensor(t3, t3, wide(beta), ALU.add))
                ch.link(nc.vector.tensor_tensor(c.X[:, :], c.X[:, :], c.T[:, :], ALU.add))

            @block.scalar
            def _(act):
                act.wait_ge(s["stats_ready"].sem, s["stats_ready"].at(1))
                nc.scalar.activation(c.rstd[:, :], c.rstd[:, :], ACT.Sqrt).then_inc(s["act"].sem, 1)
    s["vec"].passed(before + G + 3)
    s["stats_ready"].passed(1)
    s["act"].passed(1)


def add_rows(c, buf, step, bias=None):
    nc, s = c.nc, c.s
    x3 = c.X[:, :].rearrange("p (g d) -> p g d", d=D)
    with nc.Block() as block:
        @block.vector
        def _(v):
            ch = Chain(v, s["vec"])
            ch.link(nc.vector.tensor_tensor(x3, x3, buf[:, :].rearrange("p (g d) -> p g d", d=step)[:, :, 0:D], ALU.add))
            if bias is not None:
                ch.link(nc.vector.tensor_tensor(x3, x3, bias[:, :].unsqueeze(1).broadcast_to([P, G, D]), ALU.add))
    s["vec"].passed(2 if bias is not None else 1)


def pairs_of_halves(eng, body):
    n = TILES // (2 * HALF)
    with eng.Fori(0, n - 1) as i:
        for h in range(2):
            body(i * 2 + h, h, False)
    body(2 * n - 2, 0, False)
    body(2 * n - 1, 1, True)


def edge_scores(c, k_table, scores):
    nc, s = c.nc, c.s
    _, low, _ = record(c, "dst")
    with ExitStack() as ctx:
        sb = c.scratch(ctx)
        idx_ring = sb("es_idx", [P, 2 * HALF], I32)
        rows = sb("es_rows", [P, 2 * HALF * D], FP32)
        hot = sb("es_hot", [P, 2 * HALF * P], FP32)
        hot_t = sb("es_hot_t", [P, 4 * P], FP32)
        prod = sb("es_prod", [P, HALF * D], FP32)
        with nc.Block() as block:
            @block.gpsimd
            def _(pool):
                gather_rows(c, pool, k_table, idx_ring, rows)

            @block.tensor
            def _(pe):
                def turn(t, q, j):
                    pe.wait_ge(s["onehot_ready"].sem, s["onehot_ready"].at(t + 1))
                    pe.wait_ge(s["turned_out"].sem, s["turned_out"].at(t - 3))
                    nc.tensor.transpose(c.bank[j % 4][:, 0:P], hot[:, q * P:(q + 1) * P], c.ident[:, :])\
                        .then_inc(s["turned"].sem, 1)

                def body(k, h, last):
                    for j, g in enumerate(groups_of_half(c, mybir.EngineType.PE, "dst", k)):
                        t = k * HALF + j
                        if not (last and j == HALF - 1):
                            turn(t + 1, (h * HALF + j + 1) % (2 * HALF), j + 1)
                        pe.wait_ge(s["turned_out"].sem, s["turned_out"].at(t + 1))
                        pe.wait_ge(s["summed"].sem, s["summed"].at(t - 3))
                        nc.tensor.matmul(c.bank[4 + j % 4][:, 0:D], hot_t[:, (j % 4) * P:(j % 4 + 1) * P], c.rows(c.B2, g),
                                         start=True, stop=True).then_inc(s["product"].sem, 1)
                turn(0, 0, 0)
                pairs_of_halves(pe, body)

            @block.scalar
            def _(act):
                def body(k, h, last):
                    for j in range(HALF):
                        t = k * HALF + j
                        act.wait_ge(s["turned"].sem, s["turned"].at(t + 1))
                        act.wait_ge(s["product"].sem, s["product"].at(t - 3))
                        nc.scalar.activation(hot_t[:, (j % 4) * P:(j % 4 + 1) * P], c.bank[j % 4][:, 0:P], ACT.Copy)\
                            .then_inc(s["turned_out"].sem, 1)
                        if j == HALF // 2 and not last:
                            stage_index(c, act, "dst", idx_ring, k + 1, 1 - h, s["summed"])
                stage_index(c, act, "dst", idx_ring, 0, 0, None)
                pairs_of_halves(act, body)

            @block.vector
            def _(v):
                def hots(k, h):
                    v.wait_ge(s["turned"].sem, s["turned"].at((k - 1) * HALF))
                    for j in range(HALF):
                        q = h * HALF + j
                        nc.vector.tensor_scalar(hot[:, q * P:(q + 1) * P], c.iota[:, 0:P], low[:, bass.ds(k * HALF + j, 1)],
                                                None, ALU.is_equal).then_inc(s["onehot_ready"].sem, 1)

                def body(k, h, last):
                    if not last:
                        hots(k + 1, 1 - h)
                    for j in range(HALF):
                        q = h * HALF + j
                        v.wait_ge(s["product"].sem, s["product"].at(k * HALF + j + 1))
                        v.wait_ge(c.arrived[q].sem, c.arrived[q].at((k - h) * 8 + 16))
                        v.wait_ge(s["vec"].sem, s["vec"].at(k))
                        nc.vector.tensor_tensor(prod[:, j * D:(j + 1) * D], c.bank[4 + j % 4][:, 0:D],
                                                rows[:, q * D:(q + 1) * D], ALU.mult).then_inc(s["summed"].sem, 1)
                    v.wait_ge(s["summed"].sem, s["summed"].at((k + 1) * HALF))
                    nc.vector.tensor_reduce(scores[:, bass.ds(k * (HALF * HEADS), HALF * HEADS)],
                                            prod[:, :].rearrange("p (h e) -> p h e", e=DK), AX.X, ALU.add)\
                        .then_inc(s["vec"].sem, 1)
                hots(0, 0)
                pairs_of_halves(v, body)
    gather_passed(c, TILES // HALF - 1)
    for n in ("product", "summed", "onehot_ready", "turned", "turned_out"):
        s[n].passed(TILES)
    s["vec"].passed(TILES // HALF)


def score_maxima(c, scores, maxima, move):
    nc, s = c.nc, c.s
    PICKS = 4 * 3
    _, low, _ = record(c, "dst")
    W = 3 * HEADS
    TW = P // 4
    with ExitStack() as ctx:
        sb = c.scratch(ctx)
        parts = sb("sm_parts", [P, TILES * W], BF16)
        rest = sb("sm_rest", [P, TILES * HEADS], FP32)
        ring = sb("sm_ring", [P, 2 * HALF * TW], BF16)
        turned = sb("sm_turned", [P, 2 * P], BF16)
        miss = sb("sm_miss", [P, 2 * HALF * P], BF16)
        pick = sb("sm_pick", [P, HEADS * P], BF16)
        big = sb("sm_big", [P, 4 * P], BF16)
        ident_b = sb("sm_ident", [P, P], BF16)
        tile_max = sb("sm_tile_max", [P, 2 * HEADS], FP32)
        part = parts[:, :].rearrange("p (t k e) -> p t k e", k=3, e=HEADS)
        s3 = scores.rearrange("p (t e) -> p t e", e=HEADS)
        r3 = rest[:, :].rearrange("p (t e) -> p t e", e=HEADS)
        ring3 = ring[:, :].rearrange("p (t w) -> p t w", w=TW)
        with nc.Block() as block:
            @block.sync
            def _(sp):
                move.fetch(c, sp)

            @block.gpsimd
            def _(pool):
                nc.gpsimd.memset(pick[:, :], 0.0).then_inc(s["pool"].sem, 1)
                v3 = pick[:, :].rearrange("r (h n) -> r h n", n=P)
                for n in range(PICKS):
                    pool.wait_ge(s["pool"].sem, s["pool"].at(n + 1))
                    nc.gpsimd.affine_select(out=v3, in_=v3, compare_op=ALU.not_equal, fill=1.0,
                                            base=-(n // 3 * TW + n % 3 * HEADS), pattern=[[-1, HEADS], [0, P]],
                                            channel_multiplier=1).then_inc(s["pool"].sem, 1)
                move.run(c, pool)

            @block.tensor
            def _(pe):
                pe.wait_ge(s["pool"].sem, s["pool"].at(PICKS + 1))
                pe.wait_ge(s["mask_ready"].sem, s["mask_ready"].at(1))

                def turn(k, h, m):
                    q = (h * HALF + 4 * m) * TW
                    pe.wait_ge(s["ring_staged"].sem, s["ring_staged"].at(k + 1))
                    pe.wait_ge(s["turned_out"].sem, s["turned_out"].at(k * 2 + m - 1))
                    nc.tensor.transpose(c.bank[6 + m][:, 0:P // 2].bitcast(BF16), ring[:, q:q + P], ident_b[:, :])\
                        .then_inc(s["turned"].sem, 1)

                def body(k, h, last):
                    for j in range(HALF):
                        t, q, m = k * HALF + j, h * HALF + j, j // 4
                        if j == 0:
                            turn(k, h, 1)
                        elif j == 4 and not last:
                            turn(k + 1, 1 - h, 0)
                        pe.wait_ge(s["onehot_ready"].sem, s["onehot_ready"].at(t + 1))
                        if j % 4 == 0:
                            pe.wait_ge(s["turned_out"].sem, s["turned_out"].at(k * 2 + m + 1))
                        r = (j % 4) * TW
                        for n in range(2):
                            o = c.bank[2 * (j % 2) + n]
                            pe.wait_ge(s["summed"].sem, s["summed"].at(2 * t + n - 3))
                            nc.tensor.matmul(o[:, :], miss[:, q * P:(q + 1) * P], big[:, :], start=True, stop=False)
                            for e in range(4):
                                head = 4 * n + e
                                last_mm = nc.tensor.matmul(o[:, e * P:(e + 1) * P], pick[r:r + W, head * P:(head + 1) * P],
                                                           turned[r:r + W, m * P:(m + 1) * P], start=False, stop=(e == 3))
                            last_mm.then_inc(s["product"].sem, 1)
                turn(0, 0, 0)
                pairs_of_halves(pe, body)

            @block.scalar
            def _(act):
                def stage(k, h, first=False):
                    if not first:
                        act.wait_ge(s["turned"].sem, s["turned"].at((k - 1) * 2))
                        act.sem_inc(s["act_go"].sem, 1)
                    nc.scalar.activation(ring3[:, h * HALF:(h + 1) * HALF, 0:W],
                                         parts[:, bass.ds(k * (HALF * W), HALF * W)].rearrange("p (t w) -> p t w", w=W),
                                         ACT.Copy).then_inc(s["ring_staged"].sem, 1)

                def body(k, h, last):
                    if not last:
                        stage(k + 1, 1 - h)
                    for m in range(2):
                        act.wait_ge(s["turned"].sem, s["turned"].at(k * 2 + m + 1))
                        act.wait_ge(s["product"].sem, s["product"].at((k * 2 + m - 1) * 8))
                        nc.scalar.activation(turned[:, m * P:(m + 1) * P], c.bank[6 + m][:, 0:P // 2].bitcast(BF16), ACT.Copy)\
                            .then_inc(s["turned_out"].sem, 1)
                act.wait_ge(s["mask_ready"].sem, s["mask_ready"].at(1))
                act.sem_inc(s["act_go"].sem, 1)
                stage(0, 0, True)
                pairs_of_halves(act, body)

            @block.vector
            def _(v):
                ch = Chain(v, s["vec"])
                ch.link(nc.vector.tensor_copy(part[:, :, 0, :], s3))
                ch.link(nc.vector.tensor_tensor(r3, s3, part[:, :, 0, :], ALU.subtract))
                ch.link(nc.vector.tensor_copy(part[:, :, 1, :], r3))
                ch.link(nc.vector.tensor_tensor(r3, r3, part[:, :, 1, :], ALU.subtract))
                ch.link(nc.vector.tensor_copy(part[:, :, 2, :], r3))
                ch.link(nc.vector.memset(ring[:, :], 0.0))
                ch.link(nc.vector.tensor_copy(ident_b[:, :], c.ident[:, :]))
                for n in range(4):
                    ch.link(nc.vector.tensor_scalar(big[:, n * P:(n + 1) * P], c.ident[:, :], BIG, None, ALU.mult))
                ch.link(nc.vector.memset(maxima[:, :], -BIG))
                v.sem_inc(s["mask_ready"].sem, 1)
                before = ch.n

                def misses(k, h):
                    v.wait_ge(s["product"].sem, s["product"].at((k - 1) * 2 * HALF))
                    for j in range(HALF):
                        q = h * HALF + j
                        nc.vector.tensor_scalar(miss[:, q * P:(q + 1) * P], c.iota[:, 0:P], low[:, bass.ds(k * HALF + j, 1)],
                                                -1.0, ALU.is_equal, ALU.add).then_inc(s["onehot_ready"].sem, 1)

                def body(k, h, last):
                    if not last:
                        misses(k + 1, 1 - h)
                    for j, g in enumerate(groups_of_half(c, mybir.EngineType.DVE, "dst", k)):
                        t = k * HALF + j
                        o = (j % 2) * HEADS
                        for n in range(2):
                            v.wait_ge(s["product"].sem, s["product"].at(2 * t + n + 1))
                            nc.vector.tensor_reduce(tile_max[:, o + 4 * n:o + 4 * n + 4],
                                                    c.bank[2 * (j % 2) + n][:, :].rearrange("p (h e) -> p h e", e=P),
                                                    AX.X, ALU.max).then_inc(s["summed"].sem, 1)
                        v.wait_ge(s["summed"].sem, s["summed"].at(2 * t + 2))
                        v.wait_ge(s["vec"].sem, s["vec"].at(t + before))
                        m = c.rows(maxima, g, HEADS)
                        nc.vector.tensor_tensor(m, m, tile_max[:, o:o + HEADS], ALU.max).then_inc(s["vec"].sem, 1)
                misses(0, 0)
                pairs_of_halves(v, body)
                c.vec_steps = before
    s["vec"].passed(c.vec_steps + TILES)
    s["pool"].passed(PICKS + 1)
    move.passed(c)
    s["act_go"].passed(TILES // HALF)
    s["ring_staged"].passed(TILES // HALF)
    s["mask_ready"].passed(1)
    s["onehot_ready"].passed(TILES)
    for n in ("product", "summed"):
        s[n].passed(2 * TILES)
    for n in ("turned", "turned_out"):
        s[n].passed(TILES // 4)


def attend(c, v_table, scores, maxima):
    nc, s = c.nc, c.s
    _, low, _ = record(c, "dst")
    with ExitStack() as ctx:
        sb = c.scratch(ctx)
        idx_ring = sb("at_idx", [P, 2 * HALF], I32)
        rows = sb("at_rows", [P, 2 * HALF * AW], FP32)
        hot = sb("at_hot", [P, 2 * HALF * P], FP32)
        hot_t = sb("at_hot_t", [P, HALF * P], FP32)
        diff = sb("at_diff", [P, 2 * HALF * HEADS], FP32)
        w3 = rows[:, :].rearrange("p (t a) -> p t a", a=AW)
        with nc.Block() as block:
            @block.gpsimd
            def _(pool):
                gather_rows(c, pool, v_table, idx_ring, rows, AW)

            @block.tensor
            def _(pe):
                def peaks(k, h):
                    for m in range(2):
                        pe.wait_ge(s["onehot_ready"].sem, s["onehot_ready"].at(k * HALF + 4 * m + 4))
                        pe.wait_ge(s["turned_out"].sem, s["turned_out"].at(k * 2 + m - 1))
                        for j in range(4 * m, 4 * m + 4):
                            q = h * HALF + j
                            turn = nc.tensor.transpose(c.bank[m][:, (j % 4) * P:(j % 4 + 1) * P], hot[:, q * P:(q + 1) * P],
                                                       c.ident[:, :])
                        turn.then_inc(s["turned"].sem, 1)
                    pe.wait_ge(s["vec"].sem, s["vec"].at(k))
                    for j, g in enumerate(groups_of_half(c, mybir.EngineType.PE, "dst", k)):
                        if j % 4 == 0:
                            pe.wait_ge(s["turned_out"].sem, s["turned_out"].at(k * 2 + j // 4 + 1))
                        peak = nc.tensor.matmul(c.bank[2 + h][:, j * HEADS:(j + 1) * HEADS], hot_t[:, j * P:(j + 1) * P],
                                                c.rows(maxima, g, HEADS), start=True, stop=True)
                    peak.then_inc(s["hot_used"].sem, 1)

                def body(k, h, last):
                    if not last:
                        peaks(k + 1, 1 - h)
                    for j in range(HALF):
                        q = h * HALF + j
                        pe.wait_ge(s["score_ready"].sem, s["score_ready"].at(k * HALF + j + 1))
                        pe.wait_ge(s["summed"].sem, s["summed"].at(k * HALF + j - 3))
                        nc.tensor.matmul(c.bank[4 + j % 4][:, 0:AW], hot[:, q * P:(q + 1) * P], rows[:, q * AW:(q + 1) * AW],
                                         start=True, stop=True).then_inc(s["product"].sem, 1)
                peaks(0, 0)
                pairs_of_halves(pe, body)

            @block.scalar
            def _(act):
                def turns(k, h):
                    for m in range(2):
                        act.wait_ge(s["turned"].sem, s["turned"].at(k * 2 + m + 1))
                        act.wait_ge(s["hot_used"].sem, s["hot_used"].at(k))
                        nc.scalar.activation(hot_t[:, 4 * m * P:4 * (m + 1) * P], c.bank[m][:, :], ACT.Copy)\
                            .then_inc(s["turned_out"].sem, 1)

                def exps(k, h):
                    act.wait_ge(s["vec"].sem, s["vec"].at(k + 1 + 1))
                    act.wait_ge(s["product"].sem, s["product"].at((k - 1) * HALF))
                    nc.scalar.activation(w3[:, h * HALF:(h + 1) * HALF, D:AW],
                                         diff[:, h * HALF * HEADS:(h + 1) * HALF * HEADS].rearrange("p (t e) -> p t e", e=HEADS),
                                         ACT.Exp).then_inc(s["exps_ready"].sem, 1)

                def body(k, h, last):
                    if not last:
                        stage_index(c, act, "dst", idx_ring, k + 1, 1 - h, s["product"])
                        turns(k + 1, 1 - h)
                        exps(k + 1, 1 - h)
                stage_index(c, act, "dst", idx_ring, 0, 0, None)
                turns(0, 0)
                exps(0, 0)
                pairs_of_halves(act, body)

            @block.vector
            def _(v):
                nc.vector.memset(c.ACC[:, :], 0.0).then_inc(s["vec"].sem, 1)
                v.wait_ge(s["vec"].sem, s["vec"].at(1))

                def hots(k, h):
                    v.wait_ge(s["product"].sem, s["product"].at((k - 1) * HALF))
                    for j in range(HALF):
                        q = h * HALF + j
                        nc.vector.tensor_scalar(hot[:, q * P:(q + 1) * P], c.iota[:, 0:P], low[:, bass.ds(k * HALF + j, 1)],
                                                None, ALU.is_equal).then_inc(s["onehot_ready"].sem, 1)

                def below_peak(k, h):
                    v.wait_ge(s["hot_used"].sem, s["hot_used"].at(k + 1))
                    v.wait_ge(s["exps_ready"].sem, s["exps_ready"].at(k - 1))
                    nc.vector.tensor_tensor(diff[:, h * HALF * HEADS:(h + 1) * HALF * HEADS],
                                            scores[:, bass.ds(k * (HALF * HEADS), HALF * HEADS)],
                                            c.bank[2 + h][:, 0:HALF * HEADS], ALU.subtract).then_inc(s["vec"].sem, 1)

                def body(k, h, last):
                    if not last:
                        hots(k + 1, 1 - h)
                    v.wait_ge(s["exps_ready"].sem, s["exps_ready"].at(k + 1))
                    for j in range(HALF):
                        q = h * HALF + j
                        v.wait_ge(c.arrived[q].sem, c.arrived[q].at((k - h) * 8 + 16))
                        nc.vector.tensor_tensor(
                            w3[:, q, 0:D].rearrange("p (h e) -> p h e", e=DK),
                            w3[:, q, 0:D].rearrange("p (h e) -> p h e", e=DK),
                            w3[:, q, D:AW].unsqueeze(2).broadcast_to([P, HEADS, DK]), ALU.mult).then_inc(s["score_ready"].sem, 1)
                    if not last:
                        below_peak(k + 1, 1 - h)
                    for j, g in enumerate(groups_of_half(c, mybir.EngineType.DVE, "dst", k)):
                        t = k * HALF + j
                        v.wait_ge(s["product"].sem, s["product"].at(t + 1))
                        v.wait_ge(s["summed"].sem, s["summed"].at(t))
                        acc = c.rows(c.ACC, g, AW)
                        nc.vector.tensor_tensor(acc, acc, c.bank[4 + j % 4][:, 0:AW], ALU.add).then_inc(s["summed"].sem, 1)
                hots(0, 0)
                below_peak(0, 0)
                pairs_of_halves(v, body)
    gather_passed(c, TILES // HALF - 1)
    for n in ("product", "summed", "onehot_ready", "score_ready"):
        s[n].passed(TILES)
    for n in ("turned", "turned_out"):
        s[n].passed(TILES // 4)
    s["hot_used"].passed(TILES // HALF)
    s["exps_ready"].passed(TILES // HALF)
    s["vec"].passed(TILES // HALF + 1)


def fold(c, w, bias, rel, out_w, out_row, pri=None):
    nc, s = c.nc, c.s
    with ExitStack() as ctx:
        sb = c.scratch(ctx)
        wt, r, b = sb("fo_w", [P, KD * D], FP32), sb("fo_r", [P, KD * D], FP32), sb("fo_b", [P, KD], FP32)
        n_loads = 2 + HEADS
        with nc.Block() as block:
            @block.sync
            def _(sp):
                sp.dma_start(as_k(wt[:, :]), weight_view(w)).then_inc(s["loaded"].sem, 16)
                sp.dma_start(b[:, :], bias.rearrange("(k p) -> p k", p=P), allow_slow_non_contiguous=True)\
                    .then_inc(s["loaded"].sem, 16)
                sp.wait_ge(s["vec"].sem, s["vec"].at(1))
                for h in range(HEADS):
                    p0, k = DK * (h % 4), h // 4
                    sp.dma_start(r[p0:p0 + DK, k * D + h * DK:k * D + (h + 1) * DK], rel[h, :, :]).then_inc(s["loaded"].sem, 16)
                sp.wait_ge(s["loaded"].sem, s["loaded"].at(16 * n_loads))

            @block.tensor
            def _(pe):
                pe.wait_ge(s["loaded"].sem, s["loaded"].at(16 * n_loads))
                for m in range(KD):
                    for k in range(KD):
                        nc.tensor.matmul(c.bank[m][:, 0:D], wt[:, k * D + m * P:k * D + (m + 1) * P], r[:, k * D:(k + 1) * D],
                                         start=(k == 0), stop=(k == KD - 1))
                for k in range(KD):
                    last = nc.tensor.matmul(c.bank[2][0:1, 0:D], b[:, k:k + 1], r[:, k * D:(k + 1) * D],
                                            start=(k == 0), stop=(k == KD - 1))
                last.then_inc(s["product"].sem, 1)

            @block.vector
            def _(v):
                nc.vector.memset(r[:, :], 0.0).then_inc(s["vec"].sem, 1)
                v.wait_ge(s["product"].sem, s["product"].at(1))
                for m, (dst, src) in enumerate([(out_w[:, 0:D], c.bank[0][:, 0:D]), (out_w[:, D:2 * D], c.bank[1][:, 0:D]),
                                                (out_row[:, :], c.bank[2][0:1, 0:D])]):
                    if pri is None:
                        nc.vector.tensor_copy(dst, src).then_inc(s["vec"].sem, 1)
                    else:
                        n = P if m < 2 else 1
                        nc.vector.tensor_tensor(dst.rearrange("p (h e) -> p h e", e=DK), src.rearrange("p (h e) -> p h e", e=DK),
                                                pri[0:n, :].unsqueeze(2).broadcast_to([n, HEADS, DK]), ALU.mult)\
                            .then_inc(s["vec"].sem, 1)
    s["loaded"].passed(16 * n_loads)
    s["product"].passed(1)
    s["vec"].passed(4)


def attention(c, a, move):
    nc, s = c.nc, c.s
    layernorm(c)
    k_table, v_table = c.dram("k_table", [NP, D], FP32), c.dram("v_table", [NP, D], FP32)
    with ExitStack() as ctx:
        sb = c.scratch(ctx)
        wk, wv = sb("wk", [P, KD * D], FP32), sb("wv", [P, KD * D], FP32)
        wq, wa = sb("wq", [P, KD * D], FP32), sb("wa", [P, KD * D], FP32)
        rk, rv, rq, ra = (sb(f"row_{n}", [1, D], FP32) for n in "kvqa")
        pri, alpha = sb("pri", [P, HEADS], FP32), sb("alpha", [P, 2], FP32)
        maxima = sb("maxima", [P, G * HEADS], FP32)
        zr = sb("zr", [P, G * HEADS], FP32)
        scores = sb("scores", [P, TILES * HEADS], FP32)
        load(c, [(as_k(wq[:, :]), weight_view(a["L1_gnn_Wq"])), (as_k(wa[:, :]), weight_view(a["L1_gnn_Wa"])),
                 (rq[:, :], a["L1_gnn_bq"].unsqueeze(0)), (ra[:, :], a["L1_gnn_ba"].unsqueeze(0)),
                 (pri[:, :], spread(a["L1_gnn_rel_pri"])), (alpha[:, 0:1], a["L1_gnn_skip"].squeeze(0).partition_broadcast(P))])
        with nc.Block() as block:
            @block.scalar
            def _(act):
                nc.scalar.activation(alpha[:, 0:1], alpha[:, 0:1], ACT.Sigmoid).then_inc(s["act"].sem, 1)

            @block.vector
            def _(v):
                nc.vector.tensor_scalar(pri[:, :], pri[:, :], DK ** -0.5, None, ALU.mult).then_inc(s["vec"].sem, 1)
                v.wait_ge(s["act"].sem, s["act"].at(1))
                nc.vector.tensor_scalar(alpha[:, 1:2], alpha[:, 0:1], -1.0, 1.0, ALU.mult, ALU.add).then_inc(s["vec"].sem, 1)
        s["act"].passed(1)
        s["vec"].passed(2)
        fold(c, a["L1_gnn_Wk"], a["L1_gnn_bk"], a["L1_gnn_rel_att"], wk, rk, pri)
        fold(c, a["L1_gnn_Wv"], a["L1_gnn_bv"], a["L1_gnn_rel_msg"], wv, rv)

        def plain(g, out):
            return nc.vector.tensor_copy(out, c.rows(c.T, g))
        project(c, [plain], [([wk], rk[:, :], ("dram", k_table)), ([wv], rv[:, :], ("dram", v_table)),
                             ([wq], rq[:, :], ("sbuf", lambda g: c.rows(c.B2, g)))])
        edge_scores(c, k_table, scores[:, :])
        score_maxima(c, scores[:, :], maxima, move)
        attend(c, v_table, scores[:, :], maxima)
        acc3 = c.ACC[:, :].rearrange("p (g a) -> p g a", a=AW)
        with nc.Block() as block:
            @block.vector
            def _(v):
                ch = Chain(v, s["vec"])
                z = zr[:, :].rearrange("p (g h) -> p g h", h=HEADS)
                ch.link(nc.vector.tensor_scalar(z, acc3[:, :, D:AW], 1e-30, None, ALU.max))
                ch.link(nc.vector.reciprocal(zr[:, :], zr[:, :]))
        s["vec"].passed(2)

        def shares(g, out):
            return nc.vector.tensor_tensor(out.rearrange("p (h e) -> p h e", e=DK),
                                           c.rows(c.ACC, g, D, AW).rearrange("p (h e) -> p h e", e=DK),
                                           c.rows(zr, g, HEADS).unsqueeze(2).broadcast_to([P, HEADS, DK]), ALU.mult)

        def mix(ch, g, product):
            x = c.rows(c.X, g)
            ch.link(nc.vector.scalar_tensor_tensor(x, product, alpha[:, 0:1], x, ALU.mult, ALU.add))
            ch.link(nc.vector.scalar_tensor_tensor(x, c.rows(c.T, g), alpha[:, 1:2], x, ALU.mult, ALU.add))
        project(c, [shares], [([wa], ra[:, :], ("vec", mix))], post_steps=2)


def softmax_rows(v, nc, ch, s, act_count, x, rows, width, small):
    top = small[:, 0:rows]
    x3 = x.rearrange("p (g e) -> p g e", e=width)

    def wide(col):
        return col.unsqueeze(2).broadcast_to([P, rows, width])
    ch.link(nc.vector.tensor_reduce(top, x3, AX.X, ALU.max))
    ch.link(nc.vector.tensor_tensor(x3, x3, wide(top), ALU.subtract))
    v.sem_inc(s["stats_ready"].sem, 1)
    v.wait_ge(s["exps_ready"].sem, s["exps_ready"].at(act_count))
    ch.link(nc.vector.tensor_reduce(top, x3, AX.X, ALU.add))
    ch.link(nc.vector.reciprocal(top, top))
    ch.link(nc.vector.tensor_tensor(x3, x3, wide(top), ALU.mult))


def moe_top_one(c, a):
    nc, s = c.nc, c.s
    layernorm(c, turn=True)
    width, ne = 1024, 8
    nf = width // P
    chunks = G // CH
    xt = c.B2[:, 0:KD * NP].rearrange("p (k n) -> p k n", k=KD)
    with ExitStack() as ctx:
        sb = c.scratch(ctx)
        w1, b1 = sb("w1", [P, KD * width], FP32), sb("b1", [P, nf], FP32)
        wg, bg = sb("wg", [P, nf * ne], FP32), sb("bg", [1, ne], FP32)
        tiles = routed_tiles(NP, ne)
        slot, expert_of = sb("token_slot", [P, G], I32), sb("expert_of", [1, tiles], I32)
        sent, returned = (c.dram(f"L1_{n}", [tiles * P, D], FP32) for n in ("sent", "returned"))
        chosen, shares = sb("chosen", [P, G], FP32), sb("shares", [P, G], FP32)
        hid = sb("hid", [P, nf * TOK], FP32)
        probs, small = sb("probs", [P, CH * ne], FP32), sb("small", [P, 8], FP32)
        best, where = sb("best", [P, CH * 8], FP32), sb("where", [P, CH * 8], U32)
        load(c, [(w1[:, :].rearrange("p (k f) -> p k f", k=KD), weight_view(a["L1_ffn_W1"])),
                 (b1[:, :], a["L1_ffn_b1"].rearrange("(f p) -> p f", p=P)),
                 (wg[:, :].rearrange("p (k f) -> p k f", k=nf), weight_view(a["L1_ffn_Wg"])),
                 (bg[:, :], a["L1_ffn_bg"].unsqueeze(0))])

        with nc.Block() as block:
            @block.tensor
            def _(pe):
                with pe.Fori(0, chunks) as i:
                    for f in range(nf):
                        for half in range(2):
                            n = f * 2 + half
                            pe.wait_ge(s["hidden_out"].sem, s["hidden_out"].at(i * (2 * nf) + n - 3))
                            for k in range(KD):
                                last = nc.tensor.matmul(
                                    c.bank[n % 4][:, 0:HT], w1[:, k * width + f * P:k * width + (f + 1) * P],
                                    xt[:, k, bass.ds(i * TOK + half * HT, HT)], start=(k == 0), stop=(k == KD - 1))
                            last.then_inc(s["hidden"].sem, 1)
                    pe.wait_ge(s["hidden_out"].sem, s["hidden_out"].at((i + 1) * (2 * nf)))
                    for t in range(CH):
                        o = c.bank[6][:, t * ne:(t + 1) * ne]
                        for k in range(nf):
                            nc.tensor.matmul(o, hid[:, k * TOK + t * P:k * TOK + (t + 1) * P], wg[:, k * ne:(k + 1) * ne],
                                             start=(k == 0), stop=False)
                        last = nc.tensor.matmul(o, c.ones[0:1, :], bg[:, :], start=False, stop=True)
                    last.then_inc(s["product"].sem, 1)

            @block.scalar
            def _(act):
                with act.Fori(0, chunks) as i:
                    act.wait_ge(s["product"].sem, s["product"].at(i))
                    for f in range(nf):
                        for half in range(2):
                            n = f * 2 + half
                            act.wait_ge(s["hidden"].sem, s["hidden"].at(i * (2 * nf) + n + 1))
                            nc.scalar.activation(hid[:, f * TOK + half * HT:f * TOK + (half + 1) * HT],
                                                 c.bank[n % 4][:, 0:HT], ACT.Gelu, bias=b1[:, f:f + 1])\
                                .then_inc(s["hidden_out"].sem, 1)
                    act.wait_ge(s["stats_ready"].sem, s["stats_ready"].at(i + 1))
                    nc.scalar.activation(probs[:, :], probs[:, :], ACT.Exp).then_inc(s["exps_ready"].sem, 1)

            @block.vector
            def _(v):
                PER = 6 + 2 * CH + 2
                b3 = best[:, :].rearrange("p (g e) -> p g e", e=8)
                w3 = where[:, :].rearrange("p (g e) -> p g e", e=8)
                with v.Fori(0, chunks) as i:
                    ch = Chain(v, s["vec"], i * PER)
                    v.wait_ge(s["product"].sem, s["product"].at(i + 1))
                    ch.link(nc.vector.tensor_copy(probs[:, :], c.bank[6][:, 0:CH * ne]))
                    softmax_rows(v, nc, ch, s, i + 1, probs[:, :], CH, ne, small)
                    for t in range(CH):
                        row = probs[:, t * ne:(t + 1) * ne]
                        v.sem_inc(s["vec_go"].sem, 1)
                        ch.link(nc.vector.max(best[:, t * 8:(t + 1) * 8], row))
                        v.sem_inc(s["vec_go"].sem, 1)
                        ch.link(nc.vector.max_index(where[:, t * 8:(t + 1) * 8], best[:, t * 8:(t + 1) * 8], row))
                    ch.link(nc.vector.tensor_copy(chosen[:, bass.ds(i * CH, CH)], w3[:, :, 0]))
                    ch.link(nc.vector.tensor_copy(shares[:, bass.ds(i * CH, CH)], b3[:, :, 0]))
                c.vec_steps = PER * chunks
        s["vec"].passed(c.vec_steps)
        s["hidden"].passed(chunks * 2 * nf)
        s["hidden_out"].passed(chunks * 2 * nf)
        for n in ("product", "stats_ready", "exps_ready"):
            s[n].passed(chunks)
        route(c, chosen[:, :], G, ne, tiles, slot, expert_of, sent)
        routed(c, tiles, expert_of, sent, returned, width, ACT.Gelu, a["L1_ffn_Wd"], a["L1_ffn_bd"], b1, w1_here=w1)
        collect(c, slot, shares, 1, returned)
    add_rows(c, c.ACC, AW)


def weighted_graph(c, a):
    layernorm(c)
    table = c.dram("w_table", [NP, D], FP32)
    with ExitStack() as ctx:
        sb = c.scratch(ctx)
        w, bias = sb("w", [P, KD * D], FP32), sb("bias", [P, D], FP32)

        def plain(g, out):
            return c.nc.vector.tensor_copy(out, c.rows(c.T, g))
        project(c, [plain], [([w], None, ("dram", table))],
                loads=[(as_k(w[:, :]), weight_view(a["L2_gnn_W"])), (bias[:, :], spread(a["L2_gnn_b"]))])
        aggregate(c, table, "src", weighted=True)
        add_rows(c, c.ACC, AW, bias)


def token_sums(c, pe, buf, step, out, ready=None):
    nc = c.nc
    nc.tensor.matmul(out, c.zeros[:, 0:P], c.zeros[:, 0:D], start=True, stop=False)
    with pe.Fori(0, G - 1) as g:
        if ready is not None:
            ready(g)
        nc.tensor.matmul(out, c.ones[:, :], c.rows(buf, g, D, step), start=False, stop=False)
    if ready is not None:
        ready(G - 1)
    return nc.tensor.matmul(out, c.ones_last[:, :], buf[:, (G - 1) * step:(G - 1) * step + D], start=False, stop=True)


def moe_graph_gate(c, a):
    nc, s = c.nc, c.s
    layernorm(c, turn=True)
    ne, width = 8, 512
    nf = width // P
    capacity = float(-(-int(N * 1.25 * 1000) // (ne * 1000)))
    with ExitStack() as ctx:
        sb = c.scratch(ctx)
        mean, mean_t = sb("mean_row", [P, D], FP32), sb("mean_t", [P, D], FP32)
        wr, br = sb("wr", [P, KD * ne], FP32), sb("br", [1, ne], FP32)
        r, t8, small = sb("r", [P, ne], FP32), sb("t8", [P, ne], FP32), sb("small", [P, 8], FP32)
        best, where, share = sb("best", [P, 8], FP32), sb("where", [P, 8], U32), sb("share", [P, 2], FP32)
        number = sb("number", [1, 8], I32)
        b1 = sb("b1", [P, 2 * nf], FP32)
        gamma, beta = sb("gamma", [P, D], FP32), sb("beta", [P, D], FP32)
        load(c, [(wr[:, :].rearrange("p (k f) -> p k f", k=KD), weight_view(a["L2_ffn_Wr"])),
                 (br[:, :], a["L2_ffn_br"].unsqueeze(0)),
                 (gamma[:, :], spread(a["L2_ffn_gamma"])), (beta[:, :], spread(a["L2_ffn_beta"]))])
        with nc.Block() as block:
            @block.tensor
            def _(pe):
                token_sums(c, pe, c.T, D, c.bank[0][:, 0:D]).then_inc(s["product"].sem, 1)
                pe.wait_ge(s["rows_ready"].sem, s["rows_ready"].at(1))
                for k in range(KD):
                    last = nc.tensor.transpose(c.bank[1][:, k * P:(k + 1) * P], mean[:, k * P:(k + 1) * P], c.ident[:, :])
                last.then_inc(s["product"].sem, 1)
                pe.wait_ge(s["rows_ready"].sem, s["rows_ready"].at(2))
                for k in range(KD):
                    nc.tensor.matmul(c.bank[2][:, 0:ne], mean_t[:, k * P:(k + 1) * P], wr[:, k * ne:(k + 1) * ne],
                                     start=(k == 0), stop=False)
                nc.tensor.matmul(c.bank[2][:, 0:ne], c.ones[0:1, :], br[:, :], start=False, stop=True)\
                    .then_inc(s["product"].sem, 1)

            @block.scalar
            def _(act):
                for n, x in enumerate((r, r, share[:, 0:1])):
                    act.wait_ge(s["stats_ready"].sem, s["stats_ready"].at(n + 1))
                    nc.scalar.activation(x[:, :], x[:, :], ACT.Exp).then_inc(s["exps_ready"].sem, 1)

            @block.vector
            def _(v):
                ch = Chain(v, s["vec"])
                v.wait_ge(s["product"].sem, s["product"].at(1))
                nc.vector.tensor_scalar(mean[:, :], c.bank[0][:, 0:D], 1.0 / N, None, ALU.mult).then_inc(s["rows_ready"].sem, 1)
                v.wait_ge(s["product"].sem, s["product"].at(2))
                nc.vector.tensor_copy(mean_t[:, :], c.bank[1][:, 0:D]).then_inc(s["rows_ready"].sem, 1)
                v.wait_ge(s["product"].sem, s["product"].at(3))
                ch.link(nc.vector.tensor_copy(r[:, :], c.bank[2][:, 0:ne]))
                softmax_rows(v, nc, ch, s, 1, r[:, :], 1, ne, small)
                ch.link(nc.vector.tensor_scalar(t8[:, :], r[:, :], float(N), None, ALU.mult))
                ch.link(nc.vector.tensor_scalar(best[:, :], t8[:, :], capacity, None, ALU.is_gt))
                ch.link(nc.vector.tensor_scalar(t8[:, :], t8[:, :], capacity, None, ALU.max))
                ch.link(nc.vector.reciprocal(t8[:, :], t8[:, :]))
                ch.link(nc.vector.tensor_scalar(t8[:, :], t8[:, :], capacity, None, ALU.mult))
                ch.link(nc.vector.tensor_tensor(t8[:, :], t8[:, :], best[:, :], ALU.mult))
                ch.link(nc.vector.tensor_scalar(best[:, :], best[:, :], -1.0, 1.0, ALU.mult, ALU.add))
                ch.link(nc.vector.tensor_tensor(t8[:, :], t8[:, :], best[:, :], ALU.add))
                ch.link(nc.vector.tensor_tensor(r[:, :], r[:, :], t8[:, :], ALU.mult))
                softmax_rows(v, nc, ch, s, 2, r[:, :], 1, ne, small)
                ch.link(nc.vector.max(best[:, :], r[:, :]))
                ch.link(nc.vector.max_index(where[:, :], best[:, :], r[:, :]))
                ch.link(nc.vector.tensor_copy(number[:, :], where[0:1, :]))
                ch.link(nc.vector.tensor_tensor(share[:, 0:1], best[:, 1:2], best[:, 0:1], ALU.subtract))
                v.sem_inc(s["stats_ready"].sem, 1)
                v.wait_ge(s["exps_ready"].sem, s["exps_ready"].at(3))
                ch.link(nc.vector.tensor_scalar(t8[:, 0:1], share[:, 0:1], 1.0, None, ALU.add))
                ch.link(nc.vector.reciprocal(t8[:, 0:1], t8[:, 0:1]))
                ch.link(nc.vector.tensor_tensor(share[:, 1:2], share[:, 0:1], t8[:, 0:1], ALU.mult))
                ch.link(nc.vector.tensor_copy(share[:, 0:1], t8[:, 0:1]))
                c.vec_steps = ch.n
        s["vec"].passed(c.vec_steps)
        s["product"].passed(3)
        s["rows_ready"].passed(2)
        s["stats_ready"].passed(3)
        s["exps_ready"].passed(3)

        w1, w2, b2, b1_d = (a[f"L2_ffn_{n}"] for n in ("W1", "W2", "b2", "b1"))
        with nc.Block() as block:
            @block.sync
            def _(sp):
                for n in range(2):
                    e = sp.value_load(number[0:1, n:n + 1], min_val=0, max_val=ne - 1)
                    src = b1_d[bass.ds(e, 1), :].rearrange("e (f p) -> p (e f)", p=P)
                    sp.dma_start(b1[:, n * nf:(n + 1) * nf], src, allow_slow_non_contiguous=True).then_inc(s["loaded"].sem, 16)
                sp.wait_ge(s["loaded"].sem, s["loaded"].at(32))
        s["loaded"].passed(32)

        def chosen(sp, n):
            return sp.value_load(number[0:1, n:n + 1], min_val=0, max_val=ne - 1)
        experts(c, 2, width,
                Expert(lambda sp, n: at_expert(w1, chosen(sp, n)), lambda sp, n: at_expert(w2, chosen(sp, n)),
                       lambda sp, n: row_spread(b2, chosen(sp, n))),
                ACT.Gelu, (1.0, b1), lambda tile, n: share[:, n:n + 1])
        add_normed(c, gamma, beta)


def batchnorm_relu(c, gamma, beta, eps=1e-5):
    nc, s = c.nc, c.s
    with ExitStack() as ctx:
        sb = c.scratch(ctx)
        mean, scale = sb("bn_mean", [P, D], FP32), sb("bn_scale", [P, D], FP32)
        squares = sb("bn_squares", [P, 2 * D], FP32)
        with nc.Block() as block:
            @block.tensor
            def _(pe):
                token_sums(c, pe, c.ACC, AW, c.bank[0][:, 0:D]).then_inc(s["product"].sem, 1)
                o = c.bank[1][:, 0:D]

                def add(g, b):
                    pe.wait_ge(s["turned_out"].sem, s["turned_out"].at(g + 1))
                    nc.tensor.matmul(o, c.ones[:, :], squares[:, b * D:(b + 1) * D], start=False, stop=False)\
                        .then_inc(s["turned"].sem, 1)
                nc.tensor.matmul(o, c.zeros[:, 0:P], c.zeros[:, 0:D], start=True, stop=False)
                with pe.Fori(0, (G - 1) // 2) as i:
                    for b in range(2):
                        add(i * 2 + b, b)
                pe.wait_ge(s["turned_out"].sem, s["turned_out"].at(G))
                nc.tensor.matmul(o, c.ones_last[:, :], squares[:, 0:D], start=False, stop=True).then_inc(s["product"].sem, 1)

            @block.scalar
            def _(act):
                def square(g, b):
                    act.wait_ge(s["rows_ready"].sem, s["rows_ready"].at(g + 1))
                    act.wait_ge(s["turned"].sem, s["turned"].at(g - 1))
                    act.sem_inc(s["act_go"].sem, 1)
                    nc.scalar.activation(squares[:, b * D:(b + 1) * D], c.rows(c.ACC, g, D, AW), ACT.Square)\
                        .then_inc(s["turned_out"].sem, 1)
                per_tile(act, square, lambda g, b: None)
                act.wait_ge(s["stats_ready"].sem, s["stats_ready"].at(1))
                nc.scalar.activation(scale[:, :], scale[:, :], ACT.Sqrt).then_inc(s["act"].sem, 1)

            @block.vector
            def _(v):
                ch = Chain(v, s["vec"])
                v.wait_ge(s["product"].sem, s["product"].at(1))
                ch.link(nc.vector.tensor_scalar(mean[:, :], c.bank[0][:, 0:D], 1.0 / N, None, ALU.mult))
                with v.Fori(0, G) as g:
                    h = c.rows(c.ACC, g, D, AW)
                    nc.vector.tensor_tensor(h, h, mean[:, :], ALU.subtract).then_inc(s["rows_ready"].sem, 1)
                v.wait_ge(s["product"].sem, s["product"].at(2))
                ch.link(nc.vector.tensor_scalar(scale[:, :], c.bank[1][:, 0:D], 1.0 / N, eps, ALU.mult, ALU.add))
                v.sem_inc(s["stats_ready"].sem, 1)
                v.wait_ge(s["act"].sem, s["act"].at(1))
                ch.link(nc.vector.reciprocal(scale[:, :], scale[:, :]))
                ch.link(nc.vector.tensor_tensor(scale[:, :], scale[:, :], gamma, ALU.mult))
                with v.Fori(0, G) as g:
                    ch = Chain(v, s["vec"], g * 3 + 4)
                    h, t = c.rows(c.ACC, g, D, AW), c.rows(c.T, g)
                    ch.link(nc.vector.tensor_tensor(t, h, scale[:, :], ALU.mult))
                    ch.link(nc.vector.tensor_tensor(t, t, beta, ALU.add))
                    ch.link(nc.vector.tensor_scalar(t, t, 0.0, None, ALU.max))
    s["product"].passed(2)
    s["act_go"].passed(G)
    s["act"].passed(1)
    s["stats_ready"].passed(1)
    s["rows_ready"].passed(G)
    s["turned_out"].passed(G)
    s["turned"].passed(G - 1)
    s["vec"].passed(3 * G + 4)


def sage(c, a):
    nc, s = c.nc, c.s
    layernorm(c)
    table = c.dram("sage_table", [NP, D], FP32)
    with ExitStack() as ctx:
        sb = c.scratch(ctx)
        wl, wr, bl = sb("wl", [P, KD * D], FP32), sb("wr", [P, KD * D], FP32), sb("bl", [1, D], FP32)
        gamma, beta = sb("gamma", [P, D], FP32), sb("beta", [P, D], FP32)
        for layer in range(3):
            load(c, [(table.rearrange("(g p) d -> p g d", p=P), c.T[:, :].rearrange("p (g d) -> p g d", d=D)),
                     (as_k(wl[:, :]), weight_view(a["L3_gnn_Wl"][layer, :, :])),
                     (as_k(wr[:, :]), weight_view(a["L3_gnn_Wr"][layer, :, :])),
                     (bl[:, :], a["L3_gnn_bl"][layer:layer + 1, :]),
                     (gamma[:, :], a["L3_gnn_gamma"][layer, :].partition_broadcast(P)),
                     (beta[:, :], a["L3_gnn_beta"][layer, :].partition_broadcast(P))])
            aggregate(c, table, "dst")

            def mean_rows(g, out):
                return nc.vector.tensor_scalar(out, c.rows(c.ACC, g, D, AW), c.rdeg[:, bass.ds(g, 1)], None, ALU.mult)

            def own_rows(g, out):
                return nc.vector.tensor_copy(out, c.rows(c.T, g))
            project(c, [mean_rows, own_rows], [([wl, wr], bl[:, :], ("sbuf", lambda g: c.rows(c.ACC, g, D, AW)))])
            batchnorm_relu(c, gamma[:, :], beta[:, :])
    add_rows(c, c.T, D)


def deep_experts(c, a):
    nc, s = c.nc, c.s
    layernorm(c, turn=True)
    ne, width, eps = 8, 256, 1e-3
    nf = width // P
    with ExitStack() as ctx:
        sb = c.scratch(ctx)
        gates, small = sb("gates", [P, G * ne], FP32), sb("small", [P, G], FP32)
        names = [f"{n}{m}" for m in (1, 2) for n in ("g", "be", "m", "v", "b")]
        t = {n: sb(f"bn_{n}", [P, ne * nf], FP32) for n in names}
        load(c, [(t[n][:, :], columns(a[f"L3_ffn_{n}"])) for n in names])
        gate_logits(c, a["L3_ffn_Wr"], a["L3_ffn_br"].unsqueeze(0), ne, gates)
        with nc.Block() as block:
            @block.scalar
            def _(act):
                for m in (1, 2):
                    act.wait_ge(s["rows_ready"].sem, s["rows_ready"].at(m))
                    nc.scalar.activation(t[f"v{m}"][:, :], t[f"v{m}"][:, :], ACT.Sqrt).then_inc(s["act"].sem, 1)
                act.wait_ge(s["stats_ready"].sem, s["stats_ready"].at(1))
                nc.scalar.activation(gates[:, :], gates[:, :], ACT.Exp).then_inc(s["exps_ready"].sem, 1)

            @block.vector
            def _(v):
                ch = Chain(v, s["vec"])
                for m in (1, 2):
                    g, be, mu, var, b = (t[f"{n}{m}"][:, :] for n in ("g", "be", "m", "v", "b"))
                    ch.link(nc.vector.tensor_scalar(var, var, eps, None, ALU.add))
                    v.sem_inc(s["rows_ready"].sem, 1)
                    v.wait_ge(s["act"].sem, s["act"].at(m))
                    ch.link(nc.vector.reciprocal(var, var))
                    ch.link(nc.vector.tensor_tensor(var, var, g, ALU.mult))
                    ch.link(nc.vector.tensor_tensor(b, b, mu, ALU.subtract))
                    ch.link(nc.vector.tensor_tensor(b, b, var, ALU.mult))
                    ch.link(nc.vector.tensor_tensor(b, b, be, ALU.add))
                softmax_rows(v, nc, ch, s, 1, gates[:, :], G, ne, small)
                c.vec_steps = ch.n
        s["vec"].passed(c.vec_steps)
        s["rows_ready"].passed(2)
        s["act"].passed(2)
        s["stats_ready"].passed(1)
        s["exps_ready"].passed(1)
        w1, w2, wo, bo = (a[f"L3_ffn_{n}"] for n in ("W1", "W2", "Wo", "bo"))
        experts(c, ne, width,
                Expert(lambda sp, e: at_expert(w1, e), lambda sp, e: at_expert(wo, e), lambda sp, e: row_spread(bo, e),
                       lambda sp, e: at_expert(w2, e)),
                ACT.Relu, (t["v1"], t["b1"]), lambda tile, e: gates[:, bass.ds(e + tile * ne, 1)],
                ACT.Relu, (t["v2"], t["b2"]))
    add_rows(c, c.ACC, AW)


def finish(c, out):
    nc, s = c.nc, c.s
    with nc.Block() as block:
        @block.sync
        def _(sp):
            full = out[0:(G - 1) * P, :].rearrange("(g p) d -> p g d", p=P)
            sp.dma_start(full, c.X[:, 0:(G - 1) * D].rearrange("p (g d) -> p g d", d=D)).then_inc(s["stored"].sem, 16)
            sp.dma_start(out[(G - 1) * P:N, :], c.X[0:LAST, (G - 1) * D:G * D]).then_inc(s["stored"].sem, 16)
            sp.wait_ge(s["stored"].sem, s["stored"].at(32))


def build(nc, a, out):
    with ExitStack() as ctx:
        def dram(name, shape, dt):
            return nc.dram_tensor(name, shape, dt, kind="Internal").ap()
        c = Core(ctx, nc, dram)
        setup(c, a["x"])
        with ExitStack() as early:
            bucket(c, "dst", a["dst"], a["src"], a["edge_weight"], True, Scatter(c, "dst", c.scratch(early)), True)
        with ExitStack() as early:
            move = Scatter(c, "src", c.scratch(early))
            bucket(c, "src", a["src"], a["dst"], a["edge_weight"], False, move, False)
            gcn(c, a)
            moe_relu(c, a)
            attention(c, a, move)
        moe_top_one(c, a)
        weighted_graph(c, a)
        moe_graph_gate(c, a)
        sage(c, a)
        deep_experts(c, a)
        finish(c, out)


def kernel(**inputs):
    import numpy as _np
    import concourse.bacc as _bacc
    from concourse import mybir as _mybir
    from concourse.bass_utils import run_bass_kernel_spmd as _run

    nc = _bacc.Bacc("TRN2", target_bir_lowering=False, num_devices=1)
    arrays, args = {}, {}
    for name in inputs:
        a = _np.ascontiguousarray(inputs[name])
        if name == "L1_gnn_skip":
            a = a.reshape(1, 1)
        if name in ("L1_gnn_Wq", "L1_gnn_Wa"):
            a = _np.ascontiguousarray(a.T)
        arrays[f"in_{name}"] = a
        args[name] = nc.dram_tensor(f"in_{name}", a.shape, _mybir.dt.from_np(a.dtype), kind="ExternalInput").ap()
    out = nc.dram_tensor("out_0", (3125, 256), _mybir.dt.float32, kind="ExternalOutput").ap()
    build(nc, args, out)
    r = _run(nc, [arrays], core_ids=[0])
    return r.results[0]["out_0"]
```
